# Optimizing a Trainium2 kernel written in Bass

```python
import numpy as np
import jax
import jax.numpy as jnp

def _softmax(x, axis=-1):
    return jax.nn.softmax(x, axis=axis)

def _gelu(x):
    return jax.nn.gelu(x, approximate=True)

def _silu(x):
    return jax.nn.silu(x)

def _sigmoid(x):
    return jax.nn.sigmoid(x)

def _layernorm(x, axis=-1, eps=1e-05):
    m = jnp.mean(x, axis=axis, keepdims=True)
    v = jnp.var(x, axis=axis, keepdims=True)
    return (x - m) / jnp.sqrt(v + eps)

def _scatter_add(tgt, idx, src, axis=0):
    return tgt.at[idx].add(src)

def _segment_sum(src, seg, n):
    return jax.ops.segment_sum(src, seg, n)
kernel_name = 'mk_decoder_preln_d2_seqx_r8_b430f9'

def setup_inputs(seed: int=0):
    np.random.seed(seed)
    _w = jnp.asarray

    def _rec_inputs():
        import jax
        import jax.numpy as jnp
        _rk = jax.random.key(seed)
        x = -0.0003929 + 0.9999 * jax.random.normal(jax.random.fold_in(_rk, 1), (4, 256, 128), jnp.float32)
        _lenS = 256 - jax.random.randint(jax.random.fold_in(_rk, 7), (4,), 0, max(1, 256 // 4) + 1, jnp.int32)
        _lenS2 = 64 - jax.random.randint(jax.random.fold_in(_rk, 8), (4,), 0, max(1, 64 // 4) + 1, jnp.int32)
        _ctx_512P = jax.random.normal(jax.random.fold_in(_rk, 11), (4, 16, 64), jnp.float32)
        _ctx_512c = jax.random.dirichlet(jax.random.fold_in(_rk, 511), 0.3 * jnp.ones((16,), jnp.float32), (4, 64))
        _ctx_512t = jnp.einsum('bsk,bkd->bsd', _ctx_512c, _ctx_512P)
        _ctx_512t = _ctx_512t * jax.lax.rsqrt(jnp.mean(jnp.square(_ctx_512t)) + 1e-12) * 0.953939
        ctx_512 = -1.39393e-06 + 0.999914 * (_ctx_512t + 0.3 * jax.random.normal(jax.random.fold_in(_rk, 611), (4, 64, 64), jnp.float32))
        return (x, ctx_512)
    x, ctx_512 = _rec_inputs()

    def _L0_attn_setup():
        import jax, jax.numpy as jnp
        import numpy as np
        D = 128
        H = 16
        G = 4
        HD = D // H
        HPG = H // G
        THETA = 10000.0
        EPS = 1e-10

        def _l2_qk_norm(t):
            return t / (jnp.sqrt(jnp.sum(t * t, axis=-1, keepdims=True)) + EPS)

        def _rope(t):
            T = t.shape[1]
            half = HD // 2
            inv_freq = 1.0 / THETA ** (jnp.arange(half, dtype=jnp.float32) / half)
            ang = jnp.arange(T, dtype=jnp.float32)[:, None] * inv_freq[None, :]
            cos = jnp.cos(ang)[None, :, None, :]
            sin = jnp.sin(ang)[None, :, None, :]
            x1, x2 = (t[..., :half], t[..., half:])
            return jnp.concatenate([x1 * cos - x2 * sin, x2 * cos + x1 * sin], axis=-1)
        key = jax.random.key(seed)
        k1, k2, k3 = jax.random.split(key, 3)
        x = jax.random.normal(k1, (1, 512, D), jnp.float32)
        w_qkv = jax.random.normal(k2, (D, H * HD + 2 * G * HD), jnp.float32) * 0.02
        w_o = jax.random.normal(k3, (D, D), jnp.float32) * 0.02
        return {'x': x, 'w_qkv': w_qkv, 'w_o': w_o}
    _L0_attn_all = _L0_attn_setup()
    _L0_attn_in = {k: v for k, v in _L0_attn_all.items() if k in ('w_qkv', 'w_o')}
    del _L0_attn_all

    def _L0_xattn_setup():
        import jax, jax.numpy as jnp
        import numpy as np
        HEADS = 16
        D_MODEL = 128
        IMG_MODEL = 64
        D_K = D_MODEL // HEADS
        key = jax.random.key(seed)
        ks = jax.random.split(key, 12)
        B, LQ, LKV = (8, 256, 128)
        s_dm = 1.0 / np.sqrt(D_MODEL)
        s_im = 1.0 / np.sqrt(IMG_MODEL)
        return {'q': jax.random.normal(ks[0], (B, LQ, D_MODEL), jnp.float32), 'k': jax.random.normal(ks[1], (B, LKV, IMG_MODEL), jnp.float32), 'v': jax.random.normal(ks[2], (B, LKV, IMG_MODEL), jnp.float32), 'Wq': jax.random.normal(ks[3], (D_MODEL, D_MODEL), jnp.float32) * s_dm, 'bq': jnp.zeros((D_MODEL,), jnp.float32), 'Wk': jax.random.normal(ks[4], (IMG_MODEL, D_MODEL), jnp.float32) * s_im, 'bk': jnp.zeros((D_MODEL,), jnp.float32), 'Wv': jax.random.normal(ks[5], (IMG_MODEL, D_MODEL), jnp.float32) * s_im, 'bv': jnp.zeros((D_MODEL,), jnp.float32), 'Wo': jax.random.normal(ks[6], (D_MODEL, D_MODEL), jnp.float32) * s_dm, 'bo': jnp.zeros((D_MODEL,), jnp.float32)}
    _L0_xattn_all = _L0_xattn_setup()
    _L0_xattn_in = {k: v for k, v in _L0_xattn_all.items() if k in ('Wq', 'bq', 'Wk', 'bk', 'Wv', 'bv', 'Wo', 'bo')}
    del _L0_xattn_all

    def _L0_ffn_setup():
        import jax, jax.numpy as jnp
        import numpy as np
        MICRO_BATCHES = 2
        TOP_K = 2
        NUM_EXPERTS = 8
        B, S, D = (4, 512, 128)
        H = 4 * D
        key = jax.random.key(seed)
        ks = jax.random.split(key, 8)
        s = 0.02
        return {'x': jax.random.normal(ks[0], (B, S, D), jnp.float32), 'ln_scale': jnp.ones((D,), jnp.float32), 'ln_bias': jnp.zeros((D,), jnp.float32), 'attn_w': jax.random.normal(ks[1], (D, D), jnp.float32) * s, 'attn_b': jnp.zeros((D,), jnp.float32), 'gate_w': jax.random.normal(ks[2], (NUM_EXPERTS, D), jnp.float32) * s, 'w1': jax.random.normal(ks[3], (NUM_EXPERTS, D, H), jnp.float32) * s, 'b1': jnp.zeros((NUM_EXPERTS, H), jnp.float32), 'w2': jax.random.normal(ks[4], (NUM_EXPERTS, H, D), jnp.float32) * s, 'b2': jnp.zeros((NUM_EXPERTS, D), jnp.float32), 'next_w': jax.random.normal(ks[5], (D, D), jnp.float32) * s, 'next_b': jnp.zeros((D,), jnp.float32)}
    _L0_ffn_all = _L0_ffn_setup()
    _L0_ffn_in = {k: v for k, v in _L0_ffn_all.items() if k in ('ln_scale', 'ln_bias', 'attn_w', 'attn_b', 'gate_w', 'w1', 'b1', 'w2', 'b2', 'next_w', 'next_b')}
    del _L0_ffn_all

    def _L1_attn_setup():
        import jax, jax.numpy as jnp
        import numpy as np
        D_MODEL = 128
        D_HEAD = 64
        EPS = 1e-06

        def _forward(x, norm_w, Wq, Wk, Wv, wi_w, wi_b, wf_w, wf_b, Wo, bo, Wout):
            B, T, d_model = x.shape
            d = Wq.shape[0]
            scale = 1.0 / jnp.sqrt(jnp.asarray(d, x.dtype))
            normed = x * jax.lax.rsqrt(jnp.mean(x * x, axis=-1, keepdims=True) + EPS) * norm_w
            q = jnp.einsum('btm,dm->btd', normed, Wq) * scale
            k = jnp.einsum('btm,dm->btd', normed, Wk) * scale
            v = jnp.einsum('btm,dm->btd', normed, Wv)
            zi = jnp.einsum('btm,m->bt', normed, wi_w[0]) + wi_b[0]
            zf = jnp.einsum('btm,m->bt', normed, wf_w[0]) + wf_b[0]
            o = jax.nn.sigmoid(jnp.einsum('btm,dm->btd', normed, Wo) + bo)
            qT = jnp.moveaxis(q, 1, 0)
            kT = jnp.moveaxis(k, 1, 0)
            vT = jnp.moveaxis(v, 1, 0)
            ziT = jnp.moveaxis(zi, 1, 0)
            zfT = jnp.moveaxis(zf, 1, 0)
            oT = jnp.moveaxis(o, 1, 0)
            C0 = jnp.zeros((B, d, d), x.dtype)
            n0 = jnp.zeros((B, d), x.dtype)
            m0 = jnp.full((B,), -jnp.inf, x.dtype)

            def step(carry, inp):
                C, n, m = carry
                q_t, k_t, v_t, zi_t, zf_t, o_t = inp
                m_t = jnp.maximum(zf_t + m, zi_t)
                i_p = jnp.exp(zi_t - m_t)
                f_p = jnp.exp(zf_t + m - m_t)
                C_t = f_p[:, None, None] * C + i_p[:, None, None] * (v_t[:, :, None] * k_t[:, None, :])
                n_t = f_p[:, None] * n + i_p[:, None] * k_t
                Cq = jnp.einsum('bij,bj->bi', C_t, q_t)
                denom = jnp.maximum(jnp.abs(jnp.sum(n_t * q_t, axis=-1, keepdims=True)), 1.0)
                h = o_t * Cq / denom
                return ((C_t, n_t, m_t), h)
            (C_f, n_f, m_f), hT = jax.lax.scan(step, (C0, n0, m0), (qT, kT, vT, ziT, zfT, oT))
            h = jnp.moveaxis(hT, 0, 1)
            out = x + jnp.einsum('btd,md->btm', h, Wout)
            return out
        key = jax.random.key(seed)
        ks = jax.random.split(key, 12)
        s = 0.02
        B, T = (8, 256)
        return {'x': jax.random.normal(ks[0], (B, T, D_MODEL), dtype=jnp.float32), 'norm_w': jnp.ones((D_MODEL,), dtype=jnp.float32), 'Wq': jax.random.normal(ks[1], (D_HEAD, D_MODEL), dtype=jnp.float32) * s, 'Wk': jax.random.normal(ks[2], (D_HEAD, D_MODEL), dtype=jnp.float32) * s, 'Wv': jax.random.normal(ks[3], (D_HEAD, D_MODEL), dtype=jnp.float32) * s, 'wi_w': jax.random.normal(ks[4], (1, D_MODEL), dtype=jnp.float32) * s, 'wi_b': jnp.zeros((1,), dtype=jnp.float32), 'wf_w': jax.random.normal(ks[5], (1, D_MODEL), dtype=jnp.float32) * s, 'wf_b': jnp.zeros((1,), dtype=jnp.float32), 'Wo': jax.random.normal(ks[6], (D_HEAD, D_MODEL), dtype=jnp.float32) * s, 'bo': jnp.zeros((D_HEAD,), dtype=jnp.float32), 'Wout': jax.random.normal(ks[7], (D_MODEL, D_HEAD), dtype=jnp.float32) * s}
    _L1_attn_all = _L1_attn_setup()
    _L1_attn_in = {k: v for k, v in _L1_attn_all.items() if k in ('norm_w', 'Wq', 'Wk', 'Wv', 'wi_w', 'wi_b', 'wf_w', 'wf_b', 'Wo', 'bo', 'Wout')}
    del _L1_attn_all

    def _L1_xattn_setup():
        import jax, jax.numpy as jnp
        import numpy as np
        B, T, TC, C, CC, H = (2, 256, 64, 128, 64, 16)
        D = C // H

        def _heads(t):
            b, l, _ = t.shape
            return t.reshape(b, l, H, D).transpose(0, 2, 1, 3)
        key = jax.random.key(seed)
        ks = jax.random.split(key, 18)
        w = lambda k, i, o: jax.random.normal(k, (i, o), jnp.float32) / np.sqrt(i).astype(np.float32)
        return {'x': jax.random.normal(ks[0], (B, T, C), jnp.float32), 'cross_input': jax.random.normal(ks[1], (B, TC, CC), jnp.float32), 'Wk': w(ks[2], C, C), 'bk': jnp.zeros((C,), jnp.float32), 'Wq': w(ks[3], C, C), 'bq': jnp.zeros((C,), jnp.float32), 'Wv': w(ks[4], C, C), 'bv': jnp.zeros((C,), jnp.float32), 'Wck': w(ks[5], CC, C), 'bck': jnp.zeros((C,), jnp.float32), 'Wcq': w(ks[6], C, C), 'bcq': jnp.zeros((C,), jnp.float32), 'Wcv': w(ks[7], CC, C), 'bcv': jnp.zeros((C,), jnp.float32), 'Wp': w(ks[8], C, C), 'bp': jnp.zeros((C,), jnp.float32)}
    _L1_xattn_all = _L1_xattn_setup()
    _L1_xattn_in = {k: v for k, v in _L1_xattn_all.items() if k in ('Wk', 'bk', 'Wq', 'bq', 'Wv', 'bv', 'Wck', 'bck', 'Wcq', 'bcq', 'Wcv', 'bcv', 'Wp', 'bp')}
    del _L1_xattn_all

    def _L1_ffn_setup():
        import jax, jax.numpy as jnp
        import numpy as np
        D_MODEL = 128
        NUM_EXPERTS = 8
        HIDDEN = 512
        TOP_K = 2
        key = jax.random.key(seed)
        ks = jax.random.split(key, 6)
        x = jax.random.normal(ks[0], (2, 128, D_MODEL), dtype=jnp.float32)
        gate_w = jax.random.normal(ks[1], (NUM_EXPERTS, D_MODEL), dtype=jnp.float32) * (1.0 / np.sqrt(D_MODEL))
        w1 = jax.random.normal(ks[2], (NUM_EXPERTS, HIDDEN, D_MODEL), dtype=jnp.float32) * (1.0 / np.sqrt(D_MODEL))
        b1 = jax.random.normal(ks[3], (NUM_EXPERTS, HIDDEN), dtype=jnp.float32) * 0.01
        w2 = jax.random.normal(ks[4], (NUM_EXPERTS, D_MODEL, HIDDEN), dtype=jnp.float32) * (1.0 / np.sqrt(HIDDEN))
        b2 = jax.random.normal(ks[5], (NUM_EXPERTS, D_MODEL), dtype=jnp.float32) * 0.01
        return {'x': x, 'gate_w': gate_w, 'w1': w1, 'b1': b1, 'w2': w2, 'b2': b2}
    _L1_ffn_all = _L1_ffn_setup()
    _L1_ffn_in = {k: v for k, v in _L1_ffn_all.items() if k in ('gate_w', 'w1', 'b1', 'w2', 'b2')}
    del _L1_ffn_all
    return {'x': x, 'ctx_512': ctx_512, 'L0_attn_w_qkv': _L0_attn_in['w_qkv'], 'L0_attn_w_o': _L0_attn_in['w_o'], 'L0_xattn_Wq': _L0_xattn_in['Wq'], 'L0_xattn_bq': _L0_xattn_in['bq'], 'L0_xattn_Wk': _L0_xattn_in['Wk'], 'L0_xattn_bk': _L0_xattn_in['bk'], 'L0_xattn_Wv': _L0_xattn_in['Wv'], 'L0_xattn_bv': _L0_xattn_in['bv'], 'L0_xattn_Wo': _L0_xattn_in['Wo'], 'L0_xattn_bo': _L0_xattn_in['bo'], 'L0_ffn_ln_scale': _L0_ffn_in['ln_scale'], 'L0_ffn_ln_bias': _L0_ffn_in['ln_bias'], 'L0_ffn_attn_w': _L0_ffn_in['attn_w'], 'L0_ffn_attn_b': _L0_ffn_in['attn_b'], 'L0_ffn_gate_w': _L0_ffn_in['gate_w'], 'L0_ffn_w1': _L0_ffn_in['w1'], 'L0_ffn_b1': _L0_ffn_in['b1'], 'L0_ffn_w2': _L0_ffn_in['w2'], 'L0_ffn_b2': _L0_ffn_in['b2'], 'L0_ffn_next_w': _L0_ffn_in['next_w'], 'L0_ffn_next_b': _L0_ffn_in['next_b'], 'L1_attn_norm_w': _L1_attn_in['norm_w'], 'L1_attn_Wq': _L1_attn_in['Wq'], 'L1_attn_Wk': _L1_attn_in['Wk'], 'L1_attn_Wv': _L1_attn_in['Wv'], 'L1_attn_wi_w': _L1_attn_in['wi_w'], 'L1_attn_wi_b': _L1_attn_in['wi_b'], 'L1_attn_wf_w': _L1_attn_in['wf_w'], 'L1_attn_wf_b': _L1_attn_in['wf_b'], 'L1_attn_Wo': _L1_attn_in['Wo'], 'L1_attn_bo': _L1_attn_in['bo'], 'L1_attn_Wout': _L1_attn_in['Wout'], 'L1_xattn_Wk': _L1_xattn_in['Wk'], 'L1_xattn_bk': _L1_xattn_in['bk'], 'L1_xattn_Wq': _L1_xattn_in['Wq'], 'L1_xattn_bq': _L1_xattn_in['bq'], 'L1_xattn_Wv': _L1_xattn_in['Wv'], 'L1_xattn_bv': _L1_xattn_in['bv'], 'L1_xattn_Wck': _L1_xattn_in['Wck'], 'L1_xattn_bck': _L1_xattn_in['bck'], 'L1_xattn_Wcq': _L1_xattn_in['Wcq'], 'L1_xattn_bcq': _L1_xattn_in['bcq'], 'L1_xattn_Wcv': _L1_xattn_in['Wcv'], 'L1_xattn_bcv': _L1_xattn_in['bcv'], 'L1_xattn_Wp': _L1_xattn_in['Wp'], 'L1_xattn_bp': _L1_xattn_in['bp'], 'L1_ffn_gate_w': _L1_ffn_in['gate_w'], 'L1_ffn_w1': _L1_ffn_in['w1'], 'L1_ffn_b1': _L1_ffn_in['b1'], 'L1_ffn_w2': _L1_ffn_in['w2'], 'L1_ffn_b2': _L1_ffn_in['b2']}

def reference(x, ctx_512, L0_attn_w_qkv, L0_attn_w_o, L0_xattn_Wq, L0_xattn_bq, L0_xattn_Wk, L0_xattn_bk, L0_xattn_Wv, L0_xattn_bv, L0_xattn_Wo, L0_xattn_bo, L0_ffn_ln_scale, L0_ffn_ln_bias, L0_ffn_attn_w, L0_ffn_attn_b, L0_ffn_gate_w, L0_ffn_w1, L0_ffn_b1, L0_ffn_w2, L0_ffn_b2, L0_ffn_next_w, L0_ffn_next_b, L1_attn_norm_w, L1_attn_Wq, L1_attn_Wk, L1_attn_Wv, L1_attn_wi_w, L1_attn_wi_b, L1_attn_wf_w, L1_attn_wf_b, L1_attn_Wo, L1_attn_bo, L1_attn_Wout, L1_xattn_Wk, L1_xattn_bk, L1_xattn_Wq, L1_xattn_bq, L1_xattn_Wv, L1_xattn_bv, L1_xattn_Wck, L1_xattn_bck, L1_xattn_Wcq, L1_xattn_bcq, L1_xattn_Wcv, L1_xattn_bcv, L1_xattn_Wp, L1_xattn_bp, L1_ffn_gate_w, L1_ffn_w1, L1_ffn_b1, L1_ffn_w2, L1_ffn_b2):
    import jax
    import jax.numpy as jnp

    def _L0_attn_ref(x, w_qkv, w_o):
        import jax, jax.numpy as jnp
        import numpy as np
        D = 128
        H = 16
        G = 4
        HD = D // H
        HPG = H // G
        THETA = 10000.0
        EPS = 1e-10

        def _l2_qk_norm(t):
            return t / (jnp.sqrt(jnp.sum(t * t, axis=-1, keepdims=True)) + EPS)

        def _rope(t):
            T = t.shape[1]
            half = HD // 2
            inv_freq = 1.0 / THETA ** (jnp.arange(half, dtype=jnp.float32) / half)
            ang = jnp.arange(T, dtype=jnp.float32)[:, None] * inv_freq[None, :]
            cos = jnp.cos(ang)[None, :, None, :]
            sin = jnp.sin(ang)[None, :, None, :]
            x1, x2 = (t[..., :half], t[..., half:])
            return jnp.concatenate([x1 * cos - x2 * sin, x2 * cos + x1 * sin], axis=-1)
        B, T, _ = x.shape
        qkv = x @ w_qkv
        q, k, v = jnp.split(qkv, [H * HD, H * HD + G * HD], axis=-1)
        q = q.reshape(B, T, H, HD)
        k = k.reshape(B, T, G, HD)
        v = v.reshape(B, T, G, HD)
        q = _l2_qk_norm(q)
        k = _l2_qk_norm(k)
        q = _rope(q)
        k = _rope(k)
        k = jnp.repeat(k, HPG, axis=2)
        v = jnp.repeat(v, HPG, axis=2)
        q = jnp.transpose(q, (0, 2, 1, 3))
        k = jnp.transpose(k, (0, 2, 1, 3))
        v = jnp.transpose(v, (0, 2, 1, 3))
        scale = 1.0 / np.sqrt(HD).astype(np.float32)
        scores = jnp.einsum('bhqd,bhkd->bhqk', q, k) * scale
        causal = jnp.tril(jnp.ones((T, T), dtype=bool))
        scores = jnp.where(causal[None, None], scores, jnp.float32(-1e+30))
        attn = jax.nn.softmax(scores, axis=-1)
        out = jnp.einsum('bhqk,bhkd->bhqd', attn, v)
        out = jnp.transpose(out, (0, 2, 1, 3)).reshape(B, T, H * HD)
        return out @ w_o

    def _L0_xattn_ref(q, k, v, Wq, bq, Wk, bk, Wv, bv, Wo, bo):
        import jax, jax.numpy as jnp
        import numpy as np
        HEADS = 16
        D_MODEL = 128
        IMG_MODEL = 64
        D_K = D_MODEL // HEADS
        B, LQ, _ = q.shape
        LKV = k.shape[1]
        qh = (q @ Wq + bq).reshape(B, LQ, HEADS, D_K).transpose(0, 2, 1, 3)
        kh = (k @ Wk + bk).reshape(B, LKV, HEADS, D_K).transpose(0, 2, 1, 3)
        vh = (v @ Wv + bv).reshape(B, LKV, HEADS, D_K).transpose(0, 2, 1, 3)
        scale = 1.0 / np.sqrt(D_K)
        scores = jnp.einsum('bhqd,bhkd->bhqk', qh, kh) * scale
        attn = jax.nn.softmax(scores, axis=-1)
        out = jnp.einsum('bhqk,bhkd->bhqd', attn, vh)
        concat = out.transpose(0, 2, 1, 3).reshape(B, LQ, D_MODEL)
        return concat @ Wo + bo

    def _L0_ffn_ref(x, ln_scale, ln_bias, attn_w, attn_b, gate_w, w1, b1, w2, b2, next_w, next_b):
        import jax, jax.numpy as jnp
        import numpy as np
        MICRO_BATCHES = 2
        TOP_K = 2
        NUM_EXPERTS = 8
        B, S, D = (4, 512, 128)
        H = 4 * D
        b, s, d = x.shape
        flat = x.reshape(b * s, d)
        mu = jnp.mean(flat, axis=-1, keepdims=True)
        var = jnp.mean((flat - mu) ** 2, axis=-1, keepdims=True)
        xn = (flat - mu) * jax.lax.rsqrt(var + 1e-05) * ln_scale + ln_bias
        x_attn = xn @ attn_w.T + attn_b + flat
        logits = x_attn @ gate_w.T
        _vals, _idx = jax.lax.top_k(logits, TOP_K)
        e = w1.shape[0]
        n = b * s // (MICRO_BATCHES * e)
        xe = x_attn.reshape(MICRO_BATCHES, e, n, d)
        h = jax.nn.gelu(jnp.einsum('mend,edh->menh', xe, w1) + b1[None, :, None, :], approximate=False)
        eo = jnp.einsum('menh,ehd->mend', h, w2) + b2[None, :, None, :]
        eo = eo.reshape(b * s, d)
        out = jax.nn.gelu(eo @ next_w.T + next_b, approximate=False)
        return out.reshape(b, s, d)

    def _L1_attn_ref(x, norm_w, Wq, Wk, Wv, wi_w, wi_b, wf_w, wf_b, Wo, bo, Wout):
        import jax, jax.numpy as jnp
        import numpy as np
        D_MODEL = 128
        D_HEAD = 64
        EPS = 1e-06

        def _forward(x, norm_w, Wq, Wk, Wv, wi_w, wi_b, wf_w, wf_b, Wo, bo, Wout):
            B, T, d_model = x.shape
            d = Wq.shape[0]
            scale = 1.0 / jnp.sqrt(jnp.asarray(d, x.dtype))
            normed = x * jax.lax.rsqrt(jnp.mean(x * x, axis=-1, keepdims=True) + EPS) * norm_w
            q = jnp.einsum('btm,dm->btd', normed, Wq) * scale
            k = jnp.einsum('btm,dm->btd', normed, Wk) * scale
            v = jnp.einsum('btm,dm->btd', normed, Wv)
            zi = jnp.einsum('btm,m->bt', normed, wi_w[0]) + wi_b[0]
            zf = jnp.einsum('btm,m->bt', normed, wf_w[0]) + wf_b[0]
            o = jax.nn.sigmoid(jnp.einsum('btm,dm->btd', normed, Wo) + bo)
            qT = jnp.moveaxis(q, 1, 0)
            kT = jnp.moveaxis(k, 1, 0)
            vT = jnp.moveaxis(v, 1, 0)
            ziT = jnp.moveaxis(zi, 1, 0)
            zfT = jnp.moveaxis(zf, 1, 0)
            oT = jnp.moveaxis(o, 1, 0)
            C0 = jnp.zeros((B, d, d), x.dtype)
            n0 = jnp.zeros((B, d), x.dtype)
            m0 = jnp.full((B,), -jnp.inf, x.dtype)

            def step(carry, inp):
                C, n, m = carry
                q_t, k_t, v_t, zi_t, zf_t, o_t = inp
                m_t = jnp.maximum(zf_t + m, zi_t)
                i_p = jnp.exp(zi_t - m_t)
                f_p = jnp.exp(zf_t + m - m_t)
                C_t = f_p[:, None, None] * C + i_p[:, None, None] * (v_t[:, :, None] * k_t[:, None, :])
                n_t = f_p[:, None] * n + i_p[:, None] * k_t
                Cq = jnp.einsum('bij,bj->bi', C_t, q_t)
                denom = jnp.maximum(jnp.abs(jnp.sum(n_t * q_t, axis=-1, keepdims=True)), 1.0)
                h = o_t * Cq / denom
                return ((C_t, n_t, m_t), h)
            (C_f, n_f, m_f), hT = jax.lax.scan(step, (C0, n0, m0), (qT, kT, vT, ziT, zfT, oT))
            h = jnp.moveaxis(hT, 0, 1)
            out = x + jnp.einsum('btd,md->btm', h, Wout)
            return out
        return _forward(x, norm_w, Wq, Wk, Wv, wi_w, wi_b, wf_w, wf_b, Wo, bo, Wout)

    def _L1_xattn_ref(x, cross_input, Wk, bk, Wq, bq, Wv, bv, Wck, bck, Wcq, bcq, Wcv, bcv, Wp, bp):
        import jax, jax.numpy as jnp
        import numpy as np
        B, T, TC, C, CC, H = (2, 256, 64, 128, 64, 16)
        D = C // H

        def _heads(t):
            b, l, _ = t.shape
            return t.reshape(b, l, H, D).transpose(0, 2, 1, 3)
        scale = np.float32(1.0 / np.sqrt(D))
        q = _heads(x @ Wq + bq)
        k = _heads(x @ Wk + bk)
        v = _heads(x @ Wv + bv)
        att = jnp.einsum('bhqd,bhkd->bhqk', q, k) * scale
        causal = jnp.tril(jnp.ones((T, T), bool))
        att = jnp.where(causal[None, None], att, -jnp.inf)
        y = jnp.einsum('bhqk,bhkd->bhqd', jax.nn.softmax(att, axis=-1), v)
        qc = _heads(x @ Wcq + bcq)
        kc = _heads(cross_input @ Wck + bck)
        vc = _heads(cross_input @ Wcv + bcv)
        attc = jnp.einsum('bhqd,bhkd->bhqk', qc, kc) * scale
        y = y + jnp.einsum('bhqk,bhkd->bhqd', jax.nn.softmax(attc, axis=-1), vc)
        y = y.transpose(0, 2, 1, 3).reshape(x.shape[0], T, C)
        return y @ Wp + bp

    def _L1_ffn_ref(x, gate_w, w1, b1, w2, b2):
        import jax, jax.numpy as jnp
        import numpy as np
        D_MODEL = 128
        NUM_EXPERTS = 8
        HIDDEN = 512
        TOP_K = 2
        B, S, D = x.shape
        xf = x.reshape(-1, D)
        T = xf.shape[0]
        gate_logits = xf @ gate_w.T
        gate_probs = jax.nn.softmax(gate_logits, axis=-1)
        topk_scores, topk_idx = jax.lax.top_k(gate_probs, TOP_K)
        topk_scores = topk_scores / jnp.sum(topk_scores, axis=-1, keepdims=True)
        combine = jnp.zeros((T, NUM_EXPERTS), dtype=x.dtype)
        combine = combine.at[jnp.arange(T)[:, None], topk_idx].set(topk_scores)
        h = jax.nn.relu(jnp.einsum('td,ehd->teh', xf, w1) + b1)
        expert_out = jnp.einsum('teh,edh->ted', h, w2) + b2
        out = jnp.einsum('ted,te->td', expert_out, combine)
        return out.reshape(B, S, D)
    x = x + _L0_attn_ref(_layernorm(x, axis=-1), L0_attn_w_qkv, L0_attn_w_o)
    x = x + _L0_xattn_ref(_layernorm(x, axis=-1), ctx_512, ctx_512, L0_xattn_Wq, L0_xattn_bq, L0_xattn_Wk, L0_xattn_bk, L0_xattn_Wv, L0_xattn_bv, L0_xattn_Wo, L0_xattn_bo)
    x = x + _L0_ffn_ref(_layernorm(x, axis=-1), L0_ffn_ln_scale, L0_ffn_ln_bias, L0_ffn_attn_w, L0_ffn_attn_b, L0_ffn_gate_w, L0_ffn_w1, L0_ffn_b1, L0_ffn_w2, L0_ffn_b2, L0_ffn_next_w, L0_ffn_next_b)
    x = x + _L1_attn_ref(_layernorm(x, axis=-1), L1_attn_norm_w, L1_attn_Wq, L1_attn_Wk, L1_attn_Wv, L1_attn_wi_w, L1_attn_wi_b, L1_attn_wf_w, L1_attn_wf_b, L1_attn_Wo, L1_attn_bo, L1_attn_Wout)
    x = x + _L1_xattn_ref(_layernorm(x, axis=-1), ctx_512, L1_xattn_Wk, L1_xattn_bk, L1_xattn_Wq, L1_xattn_bq, L1_xattn_Wv, L1_xattn_bv, L1_xattn_Wck, L1_xattn_bck, L1_xattn_Wcq, L1_xattn_bcq, L1_xattn_Wcv, L1_xattn_bcv, L1_xattn_Wp, L1_xattn_bp)
    x = x + _L1_ffn_ref(_layernorm(x, axis=-1), L1_ffn_gate_w, L1_ffn_w1, L1_ffn_b1, L1_ffn_w2, L1_ffn_b2)
    return x

_drawn_inputs = setup_inputs


def setup_inputs(seed=0):
    import zlib

    import numpy as np

    out = dict(_drawn_inputs(seed))
    spreads = {'L0_xattn_bq': (0.0, 0.1),
     'L0_xattn_bk': (0.0, 2.0),
     'L0_xattn_bv': (0.0, 0.1),
     'L0_xattn_bo': (0.0, 0.1),
     'L0_ffn_ln_scale': (1.0, 0.6),
     'L0_ffn_ln_bias': (0.0, 0.8),
     'L0_ffn_attn_b': (0.0, 0.8),
     'L0_ffn_b1': (0.0, 0.512),
     'L0_ffn_b2': (0.0, 0.379),
     'L0_ffn_next_b': (0.0, 0.1),
     'L1_attn_norm_w': (1.0, 0.6),
     'L1_attn_bo': (0.0, 0.8),
     'L1_xattn_bk': (0.0, 2.0),
     'L1_xattn_bq': (0.0, 0.562),
     'L1_xattn_bv': (0.0, 0.1),
     'L1_xattn_bck': (0.0, 2.0),
     'L1_xattn_bcq': (0.0, 0.95),
     'L1_xattn_bcv': (0.0, 0.1),
     'L1_xattn_bp': (0.0, 0.1)}
    factors = {'L0_attn_w_qkv': 3.548,
     'L0_attn_w_o': 3.778,
     'L0_ffn_attn_w': 6.651,
     'L0_ffn_w1': 4.192,
     'L0_ffn_w2': 4.971,
     'L0_ffn_next_w': 2.787,
     'L1_attn_Wq': 8.0,
     'L1_attn_Wk': 8.0,
     'L1_attn_Wv': 8.0,
     'L1_attn_wi_w': 8.0,
     'L1_attn_wf_w': 8.0,
     'L1_attn_Wo': 8.0,
     'L1_attn_Wout': 8.0,
     'L1_ffn_b1': 40.233,
     'L1_ffn_b2': 27.311}
    for name, (base, spread) in spreads.items():
        noise = np.random.default_rng([zlib.crc32(name.encode()), seed]).standard_normal(out[name].shape)
        drawn = base * np.exp(spread * noise) if base else spread * noise
        out[name] = jnp.asarray(drawn.astype(out[name].dtype))
    for name, factor in factors.items():
        out[name] = (out[name] * factor).astype(out[name].dtype)
    return out
```

```python
from contextlib import ExitStack

import concourse.bass as bass
from concourse import mybir

F32 = mybir.dt.float32
F16 = mybir.dt.float16
BF16 = mybir.dt.bfloat16
U32 = mybir.dt.uint32
ALU = mybir.AluOpType
ACT = mybir.ActivationFunctionType
X = mybir.AxisListType.X

P = 128
NB = 4
T = 256
NT = NB * T // P
NTOK = NB * T
H = 16
HD = 8
KV = 64
DH = 64
NE = 8
HC = 4
SCALE = float(1.0 / (HD ** 0.5))
MAXDIV = 64.0



def columns(*sizes):
    at, out = 0, {}
    for name, n in sizes:
        out[name] = (at, n)
        at += n
    out["all"] = (0, at)
    return out


CST = columns(("ident", P), ("perm", P), ("causal_nat", P), ("causal_tr", P), ("rowmask", 4),
              ("iota", NE), ("cos", 2 * HD), ("sin", 2 * HD))
WA = columns(("qkv", 192), ("wo0", 2 * P))
WB = columns(("wq1", P), ("wo1", 2 * P), ("attn_w", P), ("next_w", P), ("wq3", DH), ("wk3", DH),
             ("wvo3", 2 * DH), ("wi3", 1), ("wf3", 1), ("wk4", P), ("wq4", P), ("wv4", P),
             ("wcq4", P), ("wp4", 2 * P), ("gate", NE))
W64 = columns(("wk1", P), ("wv1", P), ("wck4", P), ("wcv4", P), ("wout3", P), ("ctx", NB * KV),
              ("ctx2", NB * 2 * KV))
COL = columns(("ln_scale", 1), ("ln_bias", 1), ("attn_b", 1), ("b2", NE), ("b1", NE * HC),
              ("norm_w", 1), ("b1m", NE * HC))
ROW = columns(("bq1", P), ("bk1", P), ("bv1", P), ("bo1", P), ("next_b", P), ("bo3", DH),
              ("bk4", P), ("bq4", P), ("bv4", P), ("bck4", P), ("bcq4", P), ("bcv4", P), ("bp4", P))


class Ring:

    def __init__(self, slots, uses):
        self.at, given = {}, [0] * slots
        for n, (key, gives) in enumerate(uses):
            s = n % slots
            self.at[key] = (s, n + 1, given[s], given[s] + gives)
            given[s] += gives

    def slot(self, key):
        return self.at[key][0]

    def full(self, key):
        return self.at[key][1]

    def before(self, key):
        return self.at[key][2]

    def done(self, key):
        return self.at[key][3]


def weave(main, side):
    out, k = [], 0
    for n, step in enumerate(main):
        out.append(step)
        upto = len(side) * (n + 1) // len(main)
        out += side[k:upto]
        k = upto
    return out


def staggered(chains, lag):
    out = []
    for t in range(max(len(c) + lag * i for i, c in enumerate(chains))):
        for i, c in enumerate(chains):
            if 0 <= t - lag * i < len(c):
                out.append(c[t - lag * i])
    return out


SELF_CHUNKS = [("k0", 0), ("k0", 1), ("k1", 0), ("k0", 2), ("k0", 3), ("k1", 1)]
LAST_SELF, LAST_CROSS = len(SELF_CHUNKS) - 1, 1


def the_order():
    at0 = lambda b: [("at0", b, c) for c in range(6)]
    at1 = lambda b: [("at1", b, J) for J in range(2)]
    end = lambda s, b: [("out_copy", s, b), ("out_norm", s, b), ("out_proj", s, b)]
    to1 = lambda b: end(0, b) + [("ln", 1, b), ("tr", 1, b), ("q1", b), ("tq", 1, b),
                                 ("mxc", 1, b), ("tqm", 1, b)]
    to2 = lambda b: end(1, b) + [("ln", 2, b), ("tr2", b), ("xa", b)]
    o = [("ln", 0, b) for b in range(NB)]
    for b in range(NB):
        o += [("tr", 0, b), ("qkv", b)]
    for b in range(NB):
        o += [("rope", b), ("tq0", b, 0), ("tq0", b, 1)]
    o += [("kc", 1)]
    o += at0(0)
    o += weave(at0(1), to1(0))
    o += weave(at0(2) + at1(0), to1(1))
    o += weave(at0(3) + at1(1), to1(2) + to2(0))
    o += to1(3) + at1(2) + to2(1)
    o += at1(3) + to2(2) + to2(3)
    o += [("kc", 4), ("presets4",)]
    o += [("ffn_up", 0)]
    for j in range(1, NE // 2):
        o += [("ffn_up", j), ("ffn_down", j - 1)]
    o += [("ffn_down", NE // 2 - 1)]
    l1 = lambda b: [("nxt", b), ("ln3", b), ("tr3", b), ("prj3", b), ("rows3", b)] + [
        ("ml", b, n) for n in range(4)]
    pre4 = lambda b: [("ln", 4, b), ("tr", 4, b), ("q4", b), ("k4", b), ("tq", 4, b), ("tk4", b),
                      ("qc4", b), ("tq", 5, b), ("v4", b)]
    max4 = lambda b: [("mxs", b, c) for c in range(6)] + [("mxs_end", b), ("tqm", 4, b),
                                                          ("mxc", 5, b), ("tqm", 5, b)]
    at4 = lambda b: [("at4", b, c) for c in range(6)] + [("out_copy", 4, b)] + [
        ("at5", b, J) for J in range(2)]
    end4 = lambda b: [("out_norm", 4, b), ("out_copy", 5, b), ("out_norm", 5, b),
                      ("out_proj", 5, b), ("ln", 6, b), ("tr", 6, b), ("gate", b), ("gate_b", b)]
    o += staggered([l1(b) for b in range(NB)], 2)
    o += pre4(0) + max4(0)
    o += weave(at4(0), pre4(1) + max4(1))
    o += weave(at4(1), end4(0) + pre4(2) + max4(2))
    o += weave(at4(2), end4(1) + pre4(3) + max4(3))
    moe = []
    for n in range(2 * NE):
        moe.append(("moe_up", n // NE, n % NE))
        if n:
            moe.append(("moe_down", (n - 1) // NE, (n - 1) % NE))
    moe.append(("moe_down", 1, NE - 1))
    cut = 2 * NE - 6
    o += weave(at4(3), end4(2) + moe[:8])
    o += weave(moe[8:cut], end4(3))
    o += moe[cut:]
    return o


ORDER = the_order()
INDEX = {step: n for n, step in enumerate(ORDER)}


def count(kinds, step):
    return sum(1 for s in ORDER[:INDEX[step] + 1] if s[0] in kinds)


def misc_uses():
    one = ("tr", "qkv", "q1", "tq", "tqm", "out_norm", "out_proj", "xa", "ffn_down", "nxt", "tr3",
           "rows3", "q4", "k4", "tk4", "qc4", "v4", "gate", "moe_down")
    out = []
    for step in ORDER:
        kind = step[0]
        if kind in one:
            out.append((step, 1))
        elif kind in ("tq0", "tr2"):
            out.append((step, 2))
        elif kind == "kc":
            out += [(step + (n,), 1) for n in ("k", "v", "t")]
        elif kind == "prj3":
            out += [(step + (n,), 2) for n in ("qk", "vo")]
        elif kind == "ml" and step[2] > 0:
            out.append((step, 1))
        elif kind == "gate_b":
            out += [(step + (n,), 1) for n in ("t", "b")]
    return out


def score_uses():
    out = []
    for step in ORDER:
        kind = step[0]
        if kind in ("at0", "at1", "at4", "at5", "mxs", "ffn_up") or step[0] == "ml" and step[2] == 0:
            out.append((step, 1))
        elif kind == "mxc":
            out += [(step + (i,), 1) for i in range(2)]
        elif kind == "moe_up":
            out += [(step + (n,), 2) for n in range(2)]
    return out


ATTENTION = ("at0", "at1", "at4", "at5")
NPROB = 4
MISC = Ring(2, misc_uses())
SC = Ring(2, score_uses())
PR = Ring(NPROB, [(s, 1) for s in ORDER if s[0] in ATTENTION])
OS = Ring(2, [((int(s[0][2]), s[1]), 1) for s in ORDER if s[0] in ATTENTION and s[2] == 0])
NORMS = [s for s in ORDER if s[0] == "out_norm"]
PROJS = [s for s in ORDER if s[0] == "out_proj"]


def decoder(nc, d, out):
    with ExitStack() as ctx:
        sb = lambda name, shape, dt=F32: ctx.enter_context(nc.sbuf_tensor(name, shape, dt))
        psum = lambda name, shape, dt=F32: ctx.enter_context(nc.psum_tensor(name, shape, dt))
        sems = {}

        def sem(name):
            if name not in sems:
                sems[name] = ctx.enter_context(nc.semaphore(name))
            return sems[name]

        scores = psum("scores", [P, 2, 1024])
        outs = psum("outs", [P, 2, 512])
        misc = psum("misc", [P, 2, 512])
        misc16 = [misc[:, s, :].bitcast(F16) for s in range(2)]

        x = sb("x", [P, NT, P])
        cst = sb("cst", [P, CST["all"][1]])
        wa = sb("wa", [P, WA["all"][1]])
        wb = sb("wb", [P, WB["all"][1]])
        w64 = sb("w64", [64, W64["all"][1]])
        col = sb("col", [P, COL["all"][1]])
        row = sb("row", [P, ROW["all"][1]])
        gate_bias = sb("gate_bias", [1, 2])
        b2m = sb("b2m", [NE, P])
        w1 = sb("w1", [P, NE, HC * P])
        w2 = sb("w2", [P, NE, HC, P])
        xn = sb("xn", [P, 2, NT, P])
        xnT = sb("xnT", [P, 2, NTOK])
        n2 = sb("n2", [P, NT, P])
        stat = sb("stat", [P, 2, NT, 6])
        mv = sb("mv", [P, 2, NT, 2])
        rstd = sb("rstd", [P, 2, NT])
        neg_half = sb("neg_half", [P, 2])
        ident16 = sb("ident16", [P, P], F16)
        identb = sb("identb", [P, P], BF16)
        causal_nat = sb("causal_nat", [P, 4, P], BF16)
        causal_tr = sb("causal_tr", [P, 4, P], BF16)
        qn = sb("qn", [P, 2, 2, H, 32], F16)
        kn = sb("kn", [P, 2, 2, H, 32], F16)
        qcn = sb("qcn", [P, 2, 2, H, 32], F16)
        qT = sb("qT", [P, 4, NTOK], F16)
        qcT = sb("qcT", [P, 2, 4, T], F16)
        kT = sb("kT", [P, 4, T], F16)
        kcm = sb("kcm", [P, 4, 4, NB * KV], F16)
        split = sb("split", [P, 2, P])
        vst = sb("vst", [P, NT, H, 32])
        vc = sb("vc", [P, 2, NB, 2, 4, 32])
        mx = sb("mx", [P, 2, 2, H])
        mxc = sb("mxc", [P, 2, 2, H])
        copied = sb("copied", [P, 2, 512])
        normed = sb("normed", [P, 2, 512])
        region_k = sb("region_k", [P, 4096])
        km0 = region_k[:, 0:2048].bitcast(F16).rearrange("p (r t) -> p r t", r=4)
        km4 = region_k[:, :].bitcast(F16).rearrange("p (s r g t) -> p s r g t", s=2, r=4, g=4)
        eoT = region_k[:, 0:1024]
        flatT, n2T = region_k[:, 2048:3072], region_k[:, 3072:4096]
        xaT = xnT[:, 0, :]
        region_p = sb("region_p", [P, NPROB * 1024])
        probs = region_p[:, :].rearrange("p (s n) -> p s n", s=NPROB)
        hid0 = region_p[:, 0:4096].rearrange("p (e n) -> p e n", e=NE)
        tmp = sb("tmp", [P, 4480])
        raw = tmp[:, 0:1536].rearrange("p (b i n) -> p b i n", b=4, i=2)
        sq = tmp[:, 1536:1856].rearrange("p (i h e) -> p i h e", i=2, h=20)
        rot = tmp[:, 1856:2176].rearrange("p (i h e) -> p i h e", i=2, h=20)
        swp = tmp[:, 2176:2496].rearrange("p (i h e) -> p i h e", i=2, h=20)
        nrm = tmp[:, 2496:2656].rearrange("p (b i h) -> p b i h", b=4, i=2)
        qT3 = tmp[0:DH, 0:512].rearrange("p (s t) -> p s t", s=2)
        kT3 = tmp[0:DH, 512:1024].rearrange("p (s t) -> p s t", s=2)
        v3 = tmp[:, 1024:1284].rearrange("p (s i n) -> p s i n", s=2, i=2)
        og3 = tmp[:, 1290:1546].rearrange("p (s i n) -> p s i n", s=2, i=2)
        decay = tmp[:, 1546:2314].rearrange("p (s n) -> p s n", s=2)
        weight = tmp[:, 2314:3082].rearrange("p (s n) -> p s n", s=2)
        zif = tmp[0:1, 3082:3594]
        cumf = tmp[0:1, 3594:3850]
        h3 = tmp[:, 3850:4106].rearrange("p (s i n) -> p s i n", s=2, i=2)
        den3 = tmp[:, 4106:4108]
        h3T = tmp[0:DH, 4110:4366]
        hid1 = tmp[:, 0:4096].rearrange("p (s c n) -> p s c n", s=2, c=HC)
        rowa = sb("rowa", [1, 2, T])
        rowg = sb("rowg", [1, 2, T])
        zero_row = sb("zero_row", [1, T])
        one_row = sb("one_row", [1, T])
        zn = split
        gl = sb("gl", [P, NT, NE])
        top = sb("top", [P, NT, NE])
        topi = sb("topi", [P, NT, NE], U32)
        topf = sb("topf", [P, NT, 2])
        gex = sb("gex", [P, NT, 2])
        gtmp = sb("gtmp", [P, NE])
        comb = sb("comb", [P, NT, NE])
        combT = sb("combT", [NE, T])

        def part(t, table, name):
            a, n = table[name]
            return t[:, a:a + n]

        ident = part(cst, CST, "ident")
        perm = part(cst, CST, "perm")
        rowmask = part(cst, CST, "rowmask")
        bias = lambda name: part(row, ROW, name)
        both = lambda name: bias(name).unsqueeze(1).to_broadcast([P, 2, P])
        W = lambda name: part(wb, WB, name)
        W6 = lambda name: part(w64, W64, name)
        colv = lambda name, n=0: part(col, COL, name)[:, n:n + 1]
        tiles = lambda b: slice(2 * b, 2 * b + 2)
        toks = lambda b: slice(T * b, T * (b + 1))
        half = {0: 0, 1: 1, 2: 0, 3: 1, 4: 0, 6: 1}
        experts = lambda ap, e: ap.rearrange("p (m t) -> p m t", m=2)[:, :, e * 64:(e + 1) * 64]
        v0 = vst[:, :, 0:8, :].rearrange("p t (r j) n -> p t r j n", r=4)
        v4 = vst[:, :, :, :].rearrange("p t (j q r) n -> p t j q r n", j=2, q=2)

        misc_done = [sem(f"misc_done{s}") for s in range(2)]
        score_done = [sem(f"score_done{s}") for s in range(2)]
        prob_done = [sem(f"prob_done{s}") for s in range(NPROB)]
        out_done = [sem(f"out_done{s}") for s in range(2)]
        misc_full, score_full = sem("misc_full"), sem("score_full")

        def misc_written(eng, key):
            eng.wait_ge(misc_done[MISC.slot(key)], MISC.done(key))

        def score_written(eng, key):
            eng.wait_ge(score_done[SC.slot(key)], SC.done(key))

        def after_scalar(eng, key):
            eng.wait_ge(misc_done[MISC.slot(key)], MISC.before(key) + 1)

        def psum_misc(key):
            return misc[:, MISC.slot(key), :]

        def psum_scores(key):
            return scores[:, SC.slot(key), :]

        last_chunk = lambda s, b: (f"at{s}", b, LAST_SELF if s in (0, 4) else LAST_CROSS)
        norm_slot = lambda s, b: NORMS.index(("out_norm", s, b)) % 2

        def relu(eng, step, n, cc):
            _, h, e = step
            key, c = step + (n,), 2 * n + cc
            k = h * NE + e
            if k >= 2 and n == 0:
                eng.wait_ge(misc_full, MISC.full(("moe_down", (k - 2) // NE, (k - 2) % NE)))
            eng.wait_ge(score_full, SC.full(key))
            src = psum_scores(key)[:, cc * 512:(cc + 1) * 512]
            dst, b1 = hid1[:, k % 2, c, :], colv("b1m", e * HC + c)
            if cc == 0:
                ins = nc.scalar.activation(dst, src, ACT.Relu, bias=b1)
            else:
                ins = nc.vector.tensor_scalar(dst, src, b1, 0.0, ALU.add, ALU.max)
            ins.then_inc(score_done[SC.slot(key)], 1)

        block = ctx.enter_context(nc.Block())

        @block.sync
        def _(sp):
            xin = d["x"].rearrange("b (i p) n -> p (b i) n", p=P)
            sp.dma_start(x[:, tiles(0), :], xin[:, tiles(0), :]).then_inc(sem("x_loaded0"), 16)
            sp.dma_start(cst[:, :], d["cst"]).then_inc(sem("cst_loaded"), 16)
            sp.dma_start(wa[:, :], d["wa"]).then_inc(sem("wa_loaded"), 16)
            for b in range(1, NB):
                sp.dma_start(x[:, tiles(b), :], xin[:, tiles(b), :]).then_inc(sem(f"x_loaded{b}"), 16)
            sp.dma_start(w64[:, :], d["w64"]).then_inc(sem("w64_loaded"), 16)
            sp.dma_start(row[:, :], d["row"].to_broadcast([P, ROW["all"][1]])).then_inc(
                sem("row_loaded"), 16)
            sp.dma_start(wb[:, :], d["wb"]).then_inc(sem("wb_loaded"), 16)
            sp.dma_start(col[:, :], d["col"]).then_inc(sem("col_loaded"), 16)
            sp.dma_start(gate_bias[:, :], d["gate_bias"]).then_inc(sem("gate_bias_loaded"), 16)
            sp.dma_start(b2m[:, :], d["b2m"]).then_inc(sem("b2m_loaded"), 16)
            for h in range(2):
                es = slice(4 * h, 4 * h + 4)
                sp.dma_start(w1[:, es, :], d["w1a"][:, es, :]).then_inc(sem(f"w1a_loaded{h}"), 16)
                sp.dma_start(w2[:, es, :, :], d["w2a"][:, es, :, :]).then_inc(sem(f"w2a_loaded{h}"), 16)
            sp.wait_ge(misc_full, MISC.full(("ffn_down", NE // 2 - 1)))
            for h in range(2):
                es = slice(4 * h, 4 * h + 4)
                sp.dma_start(w1[:, es, :], d["w1b"][:, es, :]).then_inc(sem(f"w1b_loaded{h}"), 16)
                sp.dma_start(w2[:, es, :, :], d["w2b"][:, es, :, :]).then_inc(sem(f"w2b_loaded{h}"), 16)
            outv = out.rearrange("b (i p) n -> p (b i) n", p=P)
            for h in range(2):
                misc_written(sp, ("moe_down", h, NE - 1))
                sp.dma_start(outv[:, 4 * h:4 * h + 4, :], x[:, 4 * h:4 * h + 4, :]).then_inc(
                    sem("stored"), 16)
            sp.wait_ge(sem("stored"), 32)

        @block.gpsimd
        def _(pool):
            g = nc.gpsimd
            counts = {}

            def then(ins, name="pool_step"):
                counts[name] = counts.get(name, 0) + 1
                ins.then_inc(sem(name), 1)
                pool.wait_ge(sem(name), counts[name])

            then(g.memset(neg_half[:, :], -0.5))
            then(g.memset(vst[:, :, :, :], 0.0))
            for jj in range(2):
                a = 16 * jj + 8
                then(g.memset(v0[:, :, :, jj, a:a + 8], 1.0))
            then(g.memset(vc[:, :, :, :, :, :], 0.0))
            for rows, a in ((slice(0, 64), 8), (slice(64, 128), 24)):
                for l in range(2):
                    then(g.memset(vc[rows, l, :, :, :, a:a + 8].rearrange(
                        "p b j r n -> p (b j r) n"), 1.0))
            then(g.memset(zero_row[:, :], 0.0))
            then(g.memset(one_row[:, :], 1.0), "presets")

            variances = [0]

            def root(b, h):
                variances[0] += 1
                pool.wait_ge(sem("var_ready"), variances[0])
                then(g.tensor_scalar(rstd[:, h, tiles(b)], mv[:, h, tiles(b), 1], 1e-5, None, ALU.add))
                then(g.tensor_tensor(rstd[:, h, tiles(b)], rstd[:, h, tiles(b)], neg_half[:, :],
                                     ALU.pow), "rstd_ready")

            for step in ORDER:
                kind, b = step[0], step[-1]
                if kind == "ln":
                    s = step[1]
                    root(b, half[s])
                    if s == 2:
                        root(b, half[s])
                    if s in (1, 4):
                        pool.wait_ge(sem("xn_ready"), count(("ln", "ln3"), step))
                        pool.wait_ge(sem("row_loaded"), 16)
                        then(g.tensor_tensor(x[:, tiles(b), :], x[:, tiles(b), :],
                                             both({1: "bo1", 4: "bp4"}[s]), ALU.add), "x_biased")
                elif kind == "ln3":
                    root(b, half[3])
                    variances[0] += 1
                    pool.wait_ge(sem("var_ready"), variances[0])
                    m, v = mv[:, half[3], tiles(b), 0], mv[:, half[3], tiles(b), 1]
                    then(g.tensor_tensor(m, m, m, ALU.mult))
                    then(g.tensor_tensor(v, v, m, ALU.add))
                    then(g.tensor_scalar(v, v, 1e-6, None, ALU.add))
                    then(g.tensor_tensor(rstd[:, half[3], tiles(b)], v, neg_half[:, :], ALU.pow),
                         "rstd_ready")
                    then(g.tensor_tensor(x[:, tiles(b), :], x[:, tiles(b), :],
                                         xn[:, half[3], tiles(b), :], ALU.add), "x_biased")
                elif kind == "rope":
                    misc_written(pool, ("qkv", b))
                    for i in range(2):
                        for jj in range(2):
                            v = raw[:, b, i, 160:192].rearrange("p (r e) -> p r e", e=HD)
                            then(g.tensor_copy(v0[:, 2 * b + i, :, jj, 16 * jj:16 * jj + HD], v),
                                 "v0_ready")
                elif kind == "at0":
                    score_written(pool, step)
                    k1 = SELF_CHUNKS[step[2]][0] == "k1"
                    n = 8 if k1 else 4
                    v = probs[:, PR.slot(step), :].rearrange("p (h t) -> p h t", h=n)[:, :, 0:P]
                    then(g.affine_select(out=v, in_=v, compare_op=ALU.is_ge, fill=0.0, base=0,
                                         pattern=[[0, n], [1, P]], channel_multiplier=-1),
                         "prob_masked")
                elif kind == "presets4":
                    pool.wait_ge(prob_done[PR.slot(last_chunk(0, NB - 1))], PR.done(last_chunk(0, NB - 1)))
                    then(g.memset(vst[:, :, :, :], 0.0))
                    for jj in range(2):
                        for t in range(NT):
                            a = 16 * jj + 8
                            then(g.memset(v4[:, t, :, jj, :, a:a + 8], 1.0), "presets4")

        @block.scalar
        def _(act):
            a = nc.scalar
            counts = {}

            def then(ins, name):
                counts[name] = counts.get(name, 0) + 1
                ins.then_inc(sem(name), 1)
                act.wait_ge(sem(name), counts[name])

            def evac(key, out_ap, in_ap, scale=1.0):
                act.wait_ge(misc_full, MISC.full(key))
                a.activation(out_ap, in_ap, ACT.Identity if not isinstance(scale, float) else ACT.Copy,
                             scale=scale).then_inc(misc_done[MISC.slot(key)], 1)

            def stack_evac(step, dst):
                act.wait_ge(misc_full, MISC.full(step))
                for i in range(2):
                    ins = a.activation(dst[:, :, i * P:(i + 1) * P],
                                       misc16[MISC.slot(step)].rearrange(
                                           "p (i g t) -> p i g t", i=2, g=4)[:, i], ACT.Copy)
                    if i == 0:
                        then(ins, "act_step")
                    else:
                        ins.then_inc(misc_done[MISC.slot(step)], 1)

            for step in ORDER:
                kind, b = step[0], step[-1]
                if kind == "tr":
                    evac(step, xnT[:, half[step[1]], toks(b)], psum_misc(step)[:, 0:T])
                elif kind == "qkv":
                    evac(step, raw[:, b, :, :], psum_misc(step)[:, 0:384].rearrange(
                        "p (i n) -> p i n", i=2))
                elif kind == "rope":
                    misc_written(act, ("qkv", b))
                    if b:
                        act.wait_ge(sem("rope_done"), b)
                    then(a.activation(sq[:, :, :, :].rearrange("p i h e -> p i (h e)"),
                                      raw[:, b, :, 0:160], ACT.Square), "squares_ready")
                    act.wait_ge(sem("sums_ready"), b + 1)
                    then(a.activation(nrm[:, b, :, :], nrm[:, b, :, :], ACT.Sqrt), "norms_ready")
                elif kind == "tq0":
                    _, b, i = step
                    evac(step, qT[:, :, (2 * b + i) * P:(2 * b + i + 1) * P],
                         misc16[MISC.slot(step)][:, 0:512].rearrange("p (g t) -> p g t", g=4))
                elif kind in ("tq", "tqm"):
                    dst = qcT[:, b % 2, :, :] if step[1] == 5 else qT[:, :, toks(b)]
                    stack_evac(step, dst)
                elif kind == "tk4":
                    if b:
                        act.wait_ge(sem("km4_ready"), 4 * b)
                    stack_evac(step, kT[:, :, :])
                elif kind in ATTENTION:
                    act.wait_ge(score_full, SC.full(step))
                    if PR.before(step):
                        act.wait_ge(prob_done[PR.slot(step)], PR.before(step))
                    a.activation(probs[:, PR.slot(step), :], psum_scores(step), ACT.Exp,
                                 scale=SCALE).then_inc(score_done[SC.slot(step)], 1)
                elif kind == "out_copy":
                    _, s, b = step
                    n = NORMS.index(("out_norm", s, b))
                    if n >= 2:
                        act.wait_ge(sem("normed_ready"), n - 1)
                    k = last_chunk(s, b)
                    act.wait_ge(prob_done[PR.slot(k)], PR.done(k))
                    a.activation(copied[:, n % 2, :], outs[:, OS.slot((s, b)), :], ACT.Copy)\
                        .then_inc(out_done[OS.slot((s, b))], 1)
                elif kind == "tr2":
                    evac(step, flatT[:, toks(b)], psum_misc(step)[:, 0:T])
                elif kind == "ffn_up":
                    act.wait_ge(score_full, SC.full(step))
                    act.wait_ge(sem("col_loaded"), 16)
                    for n in range(2 * HC):
                        e, c = 2 * step[1] + n // HC, n % HC
                        ins = a.activation(hid0[:, e, c * P:(c + 1) * P],
                                           psum_scores(step)[:, n * P:(n + 1) * P], ACT.Gelu,
                                           bias=colv("b1", e * HC + c))
                        if n < 2 * HC - 1:
                            then(ins, "act_step")
                    ins.then_inc(score_done[SC.slot(step)], 1)
                elif kind == "nxt":
                    misc_written(act, step)
                    then(a.activation(zn[:, :, :], zn[:, :, :], ACT.Gelu), "gelu_ready")
                elif kind == "tr3":
                    evac(step, xnT[:, 1, toks(b)], psum_misc(step)[:, 0:T], colv("norm_w"))
                elif kind == "prj3":
                    if b >= 2:
                        act.wait_ge(misc_full, MISC.full(("ml", b - 2, 1)))
                        misc_written(act, ("ml", b - 2, 1))
                    evac(step + ("qk",), qT3[:, b % 2, :], psum_misc(step + ("qk",))[0:DH, 0:T],
                         1.0 / DH)
                    evac(step + ("vo",), v3[:, b % 2, :, 0:DH], psum_misc(step + ("vo",))[:, 0:T]
                         .rearrange("p (i n) -> p i n", i=2)[:, :, 0:DH])
                    misc_written(act, step + ("vo",))
                    then(a.activation(og3[:, b % 2, :, :], og3[:, b % 2, :, :], ACT.Exp, scale=-1.0),
                         "og_exp")
                elif kind == "ml" and step[2] == 0:
                    b = step[1]
                    act.wait_ge(score_full, SC.full(step))
                    if b >= 2:
                        score_written(act, ("ml", b - 2, 0))
                    then(a.activation(decay[:, b % 2, :], psum_scores(step)[:, 0:384], ACT.Exp),
                         "decay_ready")
                elif kind == "ml" and step[2] == 2:
                    if step[1]:
                        act.wait_ge(misc_full, MISC.full(("ml", step[1] - 1, 3)))
                    evac(step, h3T, psum_misc(step)[0:DH, 0:T])
                elif kind == "gate":
                    act.wait_ge(sem("gate_diff"), b + 1)
                    then(a.activation(gex[:, tiles(b), 0], gex[:, tiles(b), 0], ACT.Exp), "gate_exp")
                elif kind == "moe_up":
                    act.wait_ge(sem("col_loaded"), 16)
                    for n in range(2):
                        relu(act, step, n, 0)

        @block.vector
        def _(dve):
            v = nc.vector
            counts = {}

            def then(ins, name="dve_step"):
                counts[name] = counts.get(name, 0) + 1
                ins.then_inc(sem(name), 1)
                dve.wait_ge(sem(name), counts[name])

            def gives(key, ins):
                ins.then_inc(misc_done[MISC.slot(key)], 1)
                misc_written(dve, key)

            def gives_scores(key, ins):
                ins.then_inc(score_done[SC.slot(key)], 1)
                score_written(dve, key)

            roots = [0]

            def stats(src, b, h):
                for t in (2 * b, 2 * b + 1):
                    then(v.bn_stats(stat[:, h, t, :], src[:, t, :]))
                for t in (2 * b, 2 * b + 1):
                    then(v.bn_aggr(mv[:, h, t, :], stat[:, h, t, :]),
                         "var_ready" if t % 2 else "dve_step")
                roots[0] += 1
                dve.wait_ge(sem("rstd_ready"), roots[0])

            def normalise(dst, src, b, h, last):
                for t in (2 * b, 2 * b + 1):
                    then(v.tensor_scalar(dst[:, t, :], src[:, t, :], mv[:, h, t, 0:1],
                                         rstd[:, h, t:t + 1], ALU.subtract, ALU.mult),
                         last if t % 2 else "dve_step")

            def query_stack(dst, key, name):
                dve.wait_ge(misc_full, MISC.full(key))
                dve.wait_ge(sem("row_loaded"), 16)
                gives(key, v.tensor_tensor(split[:, :, :], psum_misc(key)[:, 0:T].rearrange(
                    "p (i n) -> p i n", i=2), both(name), ALU.add))
                s = split[:, :, :].rearrange("p i (h e) -> p (i h) e", e=HD)
                q = dst.rearrange("p i h n -> p (i h) n")
                then(v.tensor_copy(q[:, :, 0:8], s))
                then(v.tensor_tensor(q[:, :, 8:16], s, q[:, :, 0:8], ALU.subtract))
                then(v.tensor_copy(q[:, :, 16:24], q[:, :, 0:8]))
                then(v.memset(q[:, :, 24:32], 0.0), "stack_ready")

            def key_stack(dst, key, name):
                dve.wait_ge(misc_full, MISC.full(key))
                dve.wait_ge(sem("row_loaded"), 16)
                gives(key, v.tensor_tensor(split[:, :, :], psum_misc(key)[:, 0:T].rearrange(
                    "p (i n) -> p i n", i=2), both(name), ALU.add))
                s = split[:, :, :].rearrange("p i (h e) -> p (i h) e", e=HD)
                q = dst.rearrange("p i h n -> p (i h) n")
                then(v.tensor_copy(q[:, :, 0:8], s))
                then(v.tensor_tensor(q[:, :, 16:24], s, q[:, :, 0:8], ALU.subtract))
                then(v.tensor_copy(q[:, :, 8:16], q[:, :, 0:8]))
                then(v.memset(q[:, :, 24:26], MAXDIV))
                then(v.memset(q[:, :, 26:32], 0.0), "stack_ready")

            def insert_max(maxes, dst):
                m = maxes.rearrange("p i h -> p (i h)")
                q = dst.rearrange("p i h n -> p (i h) n")
                then(v.tensor_scalar(m, m, -1.0 / MAXDIV, None, ALU.mult))
                then(v.tensor_copy(q[:, :, 24], m))
                then(v.tensor_tensor(q[:, :, 25], m, q[:, :, 24], ALU.subtract), "max_ready")

            dve.wait_ge(sem("cst_loaded"), 16)
            then(v.tensor_copy(ident16[:, :], ident))
            then(v.tensor_copy(identb[:, :], ident))
            for name, dst in (("causal_nat", causal_nat), ("causal_tr", causal_tr)):
                m = part(cst, CST, name).unsqueeze(1).to_broadcast([P, 4, P])
                then(v.tensor_copy(dst[:, :, :], m), "masks_ready")

            for step in ORDER:
                kind, b = step[0], step[-1]
                if kind == "ln":
                    s = step[1]
                    h = half[s]
                    if s == 0:
                        dve.wait_ge(sem(f"x_loaded{b}"), 16)
                    stats(x, b, h)
                    normalise(xn[:, h], x, b, h, "flat_ready" if s == 2 else "xn_ready")
                    if s == 2:
                        stats(xn[:, h], b, h)
                        normalise(n2, xn[:, h], b, h, "xn_ready")
                elif kind == "rope":
                    dve.wait_ge(sem("squares_ready"), b + 1)
                    then(v.tensor_reduce(nrm[:, b, :, :], sq[:, :, :, :], X, ALU.add), "sums_ready")
                    dve.wait_ge(sem("norms_ready"), b + 1)
                    then(v.tensor_scalar(nrm[:, b, :, :], nrm[:, b, :, :], 1e-10, None, ALU.add))
                    then(v.reciprocal(nrm[:, b, :, :], nrm[:, b, :, :]))
                    r = raw[:, b, :, 0:160].rearrange("p i (h e) -> p i h e", e=HD)
                    for i in range(2):
                        then(v.tensor_tensor(sq[:, i], r[:, i],
                                             nrm[:, b, i, :].unsqueeze(2).to_broadcast([P, 20, HD]),
                                             ALU.mult))
                    for i in range(2):
                        cs = part(cst, CST, "cos")[:, i * HD:(i + 1) * HD].unsqueeze(1)
                        sn = part(cst, CST, "sin")[:, i * HD:(i + 1) * HD].unsqueeze(1)
                        then(v.tensor_tensor(rot[:, i], sq[:, i], cs.to_broadcast([P, 20, HD]), ALU.mult))
                        for lo, hi in ((0, 4), (4, 0)):
                            then(v.tensor_tensor(swp[:, i, :, lo:lo + 4], sq[:, i, :, hi:hi + 4],
                                                 sn[:, :, lo:lo + 4].to_broadcast([P, 20, 4]), ALU.mult))
                    f = lambda ap: ap.rearrange("p i h e -> p (i h e)")
                    then(v.tensor_tensor(f(rot[:, :, :, :]), f(rot[:, :, :, :]), f(swp[:, :, :, :]),
                                         ALU.add), "rope_done")
                    if b >= 2:
                        dve.wait_ge(misc_full, MISC.full(("tq0", b - 2, 1)))
                    q, k = qn[:, b % 2], kn[:, b % 2, :, 0:4, :]
                    rq, rk = rot[:, :, 0:16, :], rot[:, :, 16:20, :]
                    then(v.tensor_copy(q[:, :, :, 0:8], rq))
                    then(v.tensor_tensor(q[:, :, :, 8:16], rq, q[:, :, :, 0:8], ALU.subtract))
                    then(v.tensor_copy(q[:, :, :, 16:32], q[:, :, :, 0:16]))
                    then(v.tensor_copy(k[:, :, :, 0:8], rk))
                    then(v.tensor_tensor(k[:, :, :, 16:24], rk, k[:, :, :, 0:8], ALU.subtract))
                    then(v.tensor_copy(k[:, :, :, 8:16], k[:, :, :, 0:8]))
                    then(v.tensor_copy(k[:, :, :, 24:32], k[:, :, :, 16:24]), "stack_ready")
                elif kind == "tq0":
                    _, b, i = step
                    t = 2 * b + i
                    after_scalar(dve, step)
                    m = misc16[MISC.slot(step)][:, 512:640].unsqueeze(1).to_broadcast([P, 4, P])
                    v.tensor_tensor(km0[:, :, t * P:(t + 1) * P], m,
                                    rowmask.unsqueeze(2).to_broadcast([P, 4, P]), ALU.mult)\
                        .then_inc(misc_done[MISC.slot(step)], 1)
                    misc_written(dve, step)
                elif kind == "kc":
                    l = step[1]
                    if l == 1:
                        dve.wait_ge(misc_full, MISC.full(("tq0", NB - 1, 1)))
                    key_stack(kn[:, 0], step + ("k",), {1: "bk1", 4: "bck4"}[l])
                    key = step + ("v",)
                    dve.wait_ge(misc_full, MISC.full(key))
                    dve.wait_ge(sem("presets"), 1)
                    bv = bias({1: "bv1", 4: "bcv4"}[l])
                    for n, rows in enumerate((slice(0, 64), slice(64, 128))):
                        for b in range(NB):
                            sel = lambda ap: ap.rearrange("p (j q r e) -> p j q r e", j=2, q=2, r=4)[:, :, n]
                            ins = v.tensor_tensor(vc[rows, l // 4, b, :, :, 16 * n:16 * n + HD],
                                                  sel(psum_misc(key)[rows, b * P:(b + 1) * P]),
                                                  sel(bv[rows, :]), ALU.add)
                            if (n, b) == (1, NB - 1):
                                gives(key, ins)
                            else:
                                then(ins)
                    key = step + ("t",)
                    dve.wait_ge(misc_full, MISC.full(key))
                    m = misc16[MISC.slot(key)].rearrange("p (i g t) -> p i g t", i=2, g=4)
                    for i in range(2):
                        for r in range(4):
                            ins = v.tensor_scalar(kcm[:, r, :, i * P:(i + 1) * P], m[:, i],
                                                  rowmask[:, r:r + 1], None, ALU.mult)
                            if (i, r) == (1, 3):
                                gives(key, ins)
                            else:
                                then(ins)
                elif kind == "out_norm":
                    _, s, b = step
                    n = NORMS.index(step)
                    if n >= 2:
                        before = [p for p in PROJS if INDEX[p] < INDEX[step]]
                        dve.wait_ge(misc_full, MISC.full(before[-1]))
                    dve.wait_ge(misc_full, MISC.full(step))
                    gives(step, v.reciprocal(normed[:, n % 2, :], psum_misc(step)))
                    dve.wait_ge(out_done[OS.slot((s, b))], OS.done((s, b)))
                    if s == 5:
                        then(v.tensor_tensor(normed[:, n % 2, :], copied[:, n % 2, :],
                                             normed[:, n % 2, :], ALU.mult))
                        then(v.tensor_tensor(normed[:, n % 2, :], normed[:, n % 2, :],
                                             normed[:, (n - 1) % 2, :], ALU.add), "normed_ready")
                    else:
                        then(v.tensor_tensor(normed[:, n % 2, :], copied[:, n % 2, :],
                                             normed[:, n % 2, :], ALU.mult), "normed_ready")
                elif kind == "out_proj" or kind == "ml" and step[2] == 3:
                    b = step[2] if kind == "out_proj" else step[1]
                    dve.wait_ge(misc_full, MISC.full(step))
                    if kind == "ml":
                        dve.wait_ge(sem("x_biased"), count(("ln3",), ("ln3", b)) + NB)
                    elif step[1] == 1:
                        dve.wait_ge(sem("x_biased"), b + 1)
                    elif step[1] == 5:
                        dve.wait_ge(sem("x_biased"), 2 * NB + b + 1)
                    gives(step, v.tensor_tensor(x[:, tiles(b), :], x[:, tiles(b), :],
                                                psum_misc(step)[:, 0:T].rearrange("p (i n) -> p i n", i=2),
                                                ALU.add))
                elif kind == "q1":
                    query_stack(qn[:, b % 2], step, "bq1")
                elif kind == "q4":
                    query_stack(qn[:, b % 2], step, "bq4")
                elif kind == "qc4":
                    query_stack(qcn[:, b % 2], step, "bcq4")
                elif kind == "k4":
                    key_stack(kn[:, b % 2], step, "bk4")
                elif kind == "tk4":
                    misc_written(dve, step)
                    for r in range(4):
                        then(v.tensor_scalar(km4[:, b % 2, r, :, :], kT[:, :, :], rowmask[:, r:r + 1],
                                             None, ALU.mult), "km4_ready")
                elif kind == "v4":
                    dve.wait_ge(misc_full, MISC.full(step))
                    dve.wait_ge(sem("presets4"), 2 * NT)
                    for i in range(2):
                        for jj in range(2):
                            sel = lambda ap: ap.rearrange("p (j q r e) -> p j q r e", j=2, q=2, r=4)[:, :, jj]
                            ins = v.tensor_tensor(v4[:, 2 * b + i, :, jj, :, 16 * jj:16 * jj + HD],
                                                  sel(psum_misc(step)[:, i * P:(i + 1) * P]),
                                                  sel(bias("bv4")), ALU.add)
                            if i == jj == 1:
                                gives(step, ins)
                            else:
                                then(ins)
                elif kind == "mxc":
                    for i in range(2):
                        key = step + (i,)
                        dve.wait_ge(score_full, SC.full(key))
                        gives_scores(key, v.tensor_reduce(
                            mxc[:, b % 2, i, :], psum_scores(key).rearrange("p (h k) -> p h k", k=KV),
                            X, ALU.max))
                    insert_max(mxc[:, b % 2], (qn if step[1] == 1 else qcn)[:, b % 2])
                elif kind == "mxs":
                    _, b, c = step
                    dve.wait_ge(score_full, SC.full(step))
                    if c < 2:
                        dst, k = mx[:, b % 2, 0, 8 * c:8 * c + 8], P
                    else:
                        dst, k = mx[:, b % 2, 1, 4 * (c - 2):4 * (c - 2) + 4], T
                    gives_scores(step, v.tensor_reduce(
                        dst, psum_scores(step).rearrange("p (h k) -> p h k", k=k), X, ALU.max))
                elif kind == "mxs_end":
                    insert_max(mx[:, b % 2], qn[:, b % 2])
                elif kind == "tr2":
                    after_scalar(dve, step)
                    dve.wait_ge(sem("col_loaded"), 16)
                    gives(step, v.tensor_scalar(n2T[:, toks(b)], psum_misc(step)[:, T:2 * T],
                                                colv("ln_scale"), colv("ln_bias"), ALU.mult, ALU.add))
                elif kind == "xa":
                    dve.wait_ge(misc_full, MISC.full(step))
                    gives(step, v.scalar_tensor_tensor(xaT[:, toks(b)], psum_misc(step)[:, 0:T],
                                                       colv("attn_b"), flatT[:, toks(b)],
                                                       ALU.add, ALU.add))
                elif kind == "ffn_down":
                    dve.wait_ge(misc_full, MISC.full(step))
                    for n in range(2):
                        e = 2 * step[1] + n
                        ins = v.tensor_scalar(experts(eoT, e), psum_misc(step)[:, n * P:(n + 1) * P]
                                              .rearrange("p (m t) -> p m t", m=2),
                                              colv("b2", e), None, ALU.add)
                        then(ins) if n == 0 else gives(step, ins)
                elif kind == "nxt":
                    dve.wait_ge(misc_full, MISC.full(step))
                    gives(step, v.tensor_tensor(zn[:, :, :], psum_misc(step)[:, 0:T].rearrange(
                        "p (i n) -> p i n", i=2), both("next_b"), ALU.add))
                    dve.wait_ge(sem("gelu_ready"), b + 1)
                    then(v.tensor_tensor(x[:, tiles(b), :], x[:, tiles(b), :], zn[:, :, :], ALU.add))
                elif kind == "ln3":
                    h = half[3]
                    stats(x, b, h)
                    normalise(xn[:, h], x, b, h, "n1_ready")
                    stats(xn[:, h], b, h)
                    for t in (2 * b, 2 * b + 1):
                        then(v.tensor_scalar(n2[:, t, :], xn[:, h, t, :], rstd[:, h, t:t + 1], None,
                                             ALU.mult), "xn_ready" if t % 2 else "dve_step")
                elif kind == "prj3":
                    if b >= 2:
                        dve.wait_ge(misc_full, MISC.full(("ml", b - 2, 1)))
                    after_scalar(dve, step + ("qk",))
                    gives(step + ("qk",), v.tensor_copy(kT3[:, b % 2, :],
                                                        psum_misc(step + ("qk",))[0:DH, T:2 * T]))
                    then(v.memset(v3[:, b % 2, :, DH:DH + 1], 1.0), "v3_ones")
                    after_scalar(dve, step + ("vo",))
                    gives(step + ("vo",), v.tensor_tensor(
                        og3[:, b % 2, :, :], psum_misc(step + ("vo",))[:, 0:T].rearrange(
                            "p (i n) -> p i n", i=2)[:, :, DH:2 * DH],
                        bias("bo3").unsqueeze(1).to_broadcast([P, 2, DH]), ALU.add))
                elif kind == "rows3":
                    if b >= 2:
                        dve.wait_ge(score_full, SC.full(("ml", b - 2, 0)))
                    dve.wait_ge(misc_full, MISC.full(step))
                    dve.wait_ge(sem("gate_bias_loaded"), 16)
                    dve.wait_ge(sem("presets"), 1)
                    then(v.tensor_scalar(zif[:, 0:T], psum_misc(step)[0:1, 0:T], gate_bias[:, 0:1],
                                         None, ALU.add))
                    gives(step, v.tensor_scalar(zif[:, T:2 * T], psum_misc(step)[0:1, T:2 * T],
                                                gate_bias[:, 1:2], None, ALU.add))
                    then(v.tensor_tensor_scan(cumf, zif[:, T:2 * T], zero_row[:, :], 0.0,
                                              ALU.add, ALU.add))
                    then(v.tensor_tensor(rowa[:, b % 2, :], zif[:, 0:T], cumf, ALU.subtract))
                    then(v.tensor_tensor_scan(cumf, rowa[:, b % 2, :], rowa[:, b % 2, :], -3.0e38,
                                              ALU.max, ALU.max))
                    then(v.tensor_scalar(rowg[:, b % 2, :], cumf, -1.0, None, ALU.mult), "rows_ready")
                elif kind == "ml" and step[2] == 0:
                    b = step[1]
                    dve.wait_ge(sem("decay_ready"), b + 1)
                    if b >= 2:
                        dve.wait_ge(misc_full, MISC.full(("ml", b - 2, 1)))
                    gives_scores(step, v.tensor_tensor(weight[:, b % 2, :], decay[:, b % 2, :],
                                                       psum_scores(step)[:, 512:896], ALU.mult))
                elif kind == "ml" and step[2] == 1:
                    b = step[1]
                    dve.wait_ge(sem("og_exp"), b + 1)
                    o = og3[:, b % 2, :, :]
                    then(v.tensor_scalar(o, o, 1.0, None, ALU.add))
                    then(v.reciprocal(o, o))
                    dve.wait_ge(misc_full, MISC.full(step))
                    ps = psum_misc(step)[:, 0:2 * (DH + 1)].rearrange("p (i n) -> p i n", i=2)
                    then(v.tensor_scalar(den3, ps[:, :, DH], -1.0, None, ALU.mult))
                    then(v.tensor_tensor(den3, den3, ps[:, :, DH], ALU.max))
                    then(v.tensor_scalar(den3, den3, 1.0, None, ALU.max))
                    then(v.reciprocal(den3, den3))
                    if b >= 2:
                        dve.wait_ge(misc_full, MISC.full(("ml", b - 2, 2)))
                    for i in range(2):
                        ins = v.scalar_tensor_tensor(h3[:, b % 2, i, :], ps[:, i, 0:DH],
                                                     den3[:, i:i + 1], og3[:, b % 2, i, :],
                                                     ALU.mult, ALU.mult)
                        then(ins) if i == 0 else gives(step, ins)
                elif kind == "gate":
                    dve.wait_ge(misc_full, MISC.full(step))
                    gives(step, v.tensor_copy(gl[:, tiles(b), :], psum_misc(step)[:, 0:2 * NE]
                                              .rearrange("p (i n) -> p i n", i=2)))
                    for t in (2 * b, 2 * b + 1):
                        then(v.max(top[:, t, :], gl[:, t, :]))
                        then(v.max_index(topi[:, t, :], top[:, t, :], gl[:, t, :]))
                    then(v.tensor_copy(topf[:, tiles(b), :], topi[:, tiles(b), 0:2]))
                    then(v.tensor_tensor(gex[:, tiles(b), 0], top[:, tiles(b), 1], top[:, tiles(b), 0],
                                         ALU.subtract), "gate_diff")
                elif kind == "gate_b":
                    dve.wait_ge(sem("gate_exp"), b + 1)
                    e, w = gex[:, tiles(b), 0], gex[:, tiles(b), 1]
                    then(v.tensor_scalar(w, e, 1.0, None, ALU.add))
                    then(v.reciprocal(w, w))
                    then(v.tensor_tensor(e, e, w, ALU.mult))
                    iota = part(cst, CST, "iota")
                    for t in (2 * b, 2 * b + 1):
                        then(v.tensor_scalar(comb[:, t, :], iota, topf[:, t, 0:1], gex[:, t, 1:2],
                                             ALU.is_equal, ALU.mult))
                        then(v.tensor_scalar(gtmp[:, :], iota, topf[:, t, 1:2], gex[:, t, 0:1],
                                             ALU.is_equal, ALU.mult))
                        then(v.tensor_tensor(comb[:, t, :], comb[:, t, :], gtmp[:, :], ALU.add),
                             "comb_ready")
                    key = step + ("t",)
                    dve.wait_ge(misc_full, MISC.full(key))
                    gives(key, v.tensor_copy(combT[:, :], psum_misc(key)[0:NE, 0:T]))
                    key = step + ("b",)
                    dve.wait_ge(misc_full, MISC.full(key))
                    gives(key, v.tensor_tensor(x[:, tiles(b), :], x[:, tiles(b), :],
                                               psum_misc(key)[:, 0:T].rearrange("p (i n) -> p i n", i=2),
                                               ALU.add))
                elif kind == "moe_up":
                    dve.wait_ge(sem("col_loaded"), 16)
                    for n in range(2):
                        relu(dve, step, n, 1)
                elif kind == "moe_down":
                    _, h, e = step
                    dve.wait_ge(misc_full, MISC.full(step))
                    for i in range(4):
                        t = 4 * h + i
                        ins = v.scalar_tensor_tensor(x[:, t, :], psum_misc(step)[:, i * P:(i + 1) * P],
                                                     comb[:, t, e:e + 1], x[:, t, :], ALU.mult, ALU.add)
                        then(ins) if i < 3 else gives(step, ins)

        @block.tensor
        def _(pe):
            mm = nc.tensor.matmul

            def take_misc(key):
                if MISC.before(key):
                    pe.wait_ge(misc_done[MISC.slot(key)], MISC.before(key))
                return psum_misc(key)

            def take_scores(key):
                if SC.before(key):
                    pe.wait_ge(score_done[SC.slot(key)], SC.before(key))
                return psum_scores(key)

            def transposes(key, dst, blocks, identity):
                for n, blk in enumerate(blocks):
                    ins = nc.tensor.transpose(dst[:, n * P:(n + 1) * P], blk, identity)
                ins.then_inc(misc_full, 1)

            def natural(key, lhsTs, rhs):
                dst = take_misc(key)
                n = rhs.shape[-1]
                for i, l in enumerate(lhsTs):
                    ins = mm(dst[:, i * n:(i + 1) * n], l, rhs, start=True, stop=True)
                ins.then_inc(misc_full, 1)

            tile_cols = lambda ap, b: [ap[:, (2 * b + i) * P:(2 * b + i + 1) * P] for i in range(2)]

            def stacked(step, buf):
                take_misc(step)
                transposes(step, misc16[MISC.slot(step)],
                           [buf[:, i, 4 * B:4 * B + 4, :].rearrange("p h n -> p (h n)")
                            for i in range(2) for B in range(4)], ident16[:, :])

            def self_scores(step, s):
                _, b, c = step
                kind, n = SELF_CHUNKS[c]
                dst = take_scores(step)
                if s == 0:
                    for i in range(2):
                        misc_written(pe, ("tq0", b, i))
                    keys = lambda r, B, kt: km0[:, r, (2 * b + kt) * P:(2 * b + kt + 1) * P]
                else:
                    pe.wait_ge(sem("masks_ready"), 2)
                    pe.wait_ge(sem("km4_ready"), 4 * (b + 1))
                    misc_written(pe, ("tqm", 4, b))
                    keys = lambda r, B, kt: km4[:, b % 2, r, B, kt * P:(kt + 1) * P]
                if kind == "k0":
                    for r in range(4):
                        o = dst[:, r * T:(r + 1) * T]
                        ins = mm(o, keys(r, n, 0), qT[:, n, toks(b)], start=True, stop=s == 0)
                        if s:
                            ins = mm(o[:, 0:P], identb[:, :], causal_tr[:, 0, :], start=False, stop=True)
                else:
                    for q in range(2):
                        if s:
                            mm(dst[:, q * 512:(q + 1) * 512], identb[:, :],
                               causal_tr[:, :, :].rearrange("p r t -> p (r t)"), start=True, stop=False)
                        for r in range(4):
                            o = dst[:, q * 512 + r * P:q * 512 + (r + 1) * P]
                            ins = mm(o, keys(r, 2 * n + q, 1), qT[:, 2 * n + q, b * T + P:(b + 1) * T],
                                     start=s == 0, stop=s == 0 or r == 3)
                ins.then_inc(score_full, 1)

            def cross_scores(step, s):
                _, b, J = step
                misc_written(pe, ("tqm", s, b))
                dst = take_scores(step)
                q = qT[:, :, toks(b)] if s == 1 else qcT[:, b % 2, :, :]
                for r in range(4):
                    for jj in range(2):
                        ins = mm(dst[64 * jj:64 * jj + 64, r * T:(r + 1) * T],
                                 kcm[:, r, 2 * J + jj, b * KV:(b + 1) * KV], q[:, 2 * J + jj, :],
                                 start=True, stop=True)
                ins.then_inc(score_full, 1)

            def weighted_values(step):
                s, b, c = int(step[0][2]), step[1], step[2]
                dst = outs[:, OS.slot((s, b)), :]
                pr = probs[:, PR.slot(step), :]
                if c == 0 and OS.before((s, b)):
                    pe.wait_ge(out_done[OS.slot((s, b))], OS.before((s, b)))
                if s == 0:
                    pe.wait_ge(sem("prob_masked"), count(("at0",), step))
                    pe.wait_ge(sem("v0_ready"), 4 * (b + 1))
                else:
                    score_written(pe, step)
                if s in (1, 5):
                    misc_written(pe, ("kc", 1 if s == 1 else 4, "v"))
                    for r in range(4):
                        ins = mm(dst[32 * r:32 * r + 32, c * T:(c + 1) * T], vc[:, s // 4, b, c, r, :],
                                 pr[:, r * T:(r + 1) * T], start=True, stop=True)
                else:
                    if s == 4:
                        misc_written(pe, ("v4", b))
                    kind, n = SELF_CHUNKS[c]
                    vals = lambda r, B, kt: (v0[:, 2 * b + kt, r, B % 2, :] if s == 0 else
                                             vst[:, 2 * b + kt, 4 * B + r, :])
                    if kind == "k0":
                        for r in range(4):
                            ins = mm(dst[32 * r:32 * r + 32, n // 2 * T:(n // 2 + 1) * T],
                                     vals(r, n, 0), pr[:, r * T:(r + 1) * T],
                                     start=n % 2 == 0, stop=False)
                    else:
                        for q in range(2):
                            for r in range(4):
                                ins = mm(dst[32 * r:32 * r + 32, n * T + P:(n + 1) * T],
                                         vals(r, 2 * n + q, 1),
                                         pr[:, (4 * q + r) * P:(4 * q + r + 1) * P],
                                         start=False, stop=q == 1)
                ins.then_inc(prob_done[PR.slot(step)], 1)

            waiting = []

            def attention(step):
                s = int(step[0][2])
                (self_scores if s in (0, 4) else cross_scores)(step, s)
                flush()
                waiting.append(step)

            def flush():
                while waiting:
                    weighted_values(waiting.pop())

            pe.wait_ge(sem("cst_loaded"), 16)
            for step in ORDER:
                kind, b = step[0], step[-1]
                if kind == "tr":
                    pe.wait_ge(sem("xn_ready"), count(("ln", "ln3"), ("ln", step[1], b)))
                    transposes(step, take_misc(step), [xn[:, half[step[1]], 2 * b + i, :]
                                                       for i in range(2)], ident)
                elif kind == "qkv":
                    pe.wait_ge(sem("wa_loaded"), 16)
                    misc_written(pe, ("tr", 0, b))
                    natural(step, tile_cols(xnT[:, 0, :], b), part(wa, WA, "qkv"))
                elif kind == "tq0":
                    _, b, i = step
                    pe.wait_ge(sem("stack_ready"), count(("rope", "kc", "q1", "q4", "k4", "qc4"), ("rope", b)))
                    take_misc(step)
                    transposes(step, misc16[MISC.slot(step)],
                               [qn[:, b % 2, i, 4 * B:4 * B + 4, :].rearrange("p h n -> p (h n)")
                                for B in range(4)] +
                               [kn[:, b % 2, i, 0:4, :].rearrange("p h n -> p (h n)")], ident16[:, :])
                elif kind == "kc":
                    l = step[1]
                    pe.wait_ge(sem("w64_loaded"), 16)
                    ctxT, ctx2 = W6("ctx"), W6("ctx2")
                    natural(step + ("k",), tile_cols(ctxT, 0), W6({1: "wk1", 4: "wck4"}[l]))
                    natural(step + ("v",), [ctx2[:, n * P:(n + 1) * P] for n in range(NB)],
                            W6({1: "wv1", 4: "wcv4"}[l]))
                    pe.wait_ge(sem("stack_ready"), count(("rope", "kc", "q1", "q4", "k4", "qc4"), step))
                    stacked(step + ("t",), kn[:, 0])
                elif kind in ATTENTION:
                    attention(step)
                elif kind == "out_copy":
                    flush()
                elif kind == "out_norm":
                    _, s, b = step
                    pe.wait_ge(out_done[OS.slot((s, b))], OS.done((s, b)))
                    mm(take_misc(step), perm, copied[:, norm_slot(s, b), :], start=True, stop=True)\
                        .then_inc(misc_full, 1)
                elif kind == "out_proj":
                    _, s, b = step
                    pe.wait_ge(sem("normed_ready"), NORMS.index(("out_norm", s, b)) + 1)
                    if s:
                        pe.wait_ge(sem("wb_loaded"), 16)
                    w = part(wa, WA, "wo0") if s == 0 else W({1: "wo1", 5: "wp4"}[s])
                    dst, y = take_misc(step), normed[:, norm_slot(s, b), :]
                    for i in range(2):
                        for J in range(2):
                            ins = mm(dst[:, i * P:(i + 1) * P], y[:, J * T + i * P:J * T + (i + 1) * P],
                                     w[:, J * P:(J + 1) * P], start=J == 0, stop=J == 1)
                    ins.then_inc(misc_full, 1)
                elif kind in ("q1", "q4", "k4", "qc4", "v4"):
                    s = 1 if kind == "q1" else 4
                    pe.wait_ge(sem("wb_loaded"), 16)
                    misc_written(pe, ("tr", s, b))
                    w = {"q1": "wq1", "q4": "wq4", "k4": "wk4", "qc4": "wcq4", "v4": "wv4"}[kind]
                    natural(step, tile_cols(xnT[:, half[s], :], b), W(w))
                elif kind in ("tq", "tk4", "tqm"):
                    made = {"tk4": ("k4", b)}.get(kind) or {1: ("q1", b), 4: ("q4", b), 5: ("qc4", b)}[step[1]]
                    pe.wait_ge(sem("stack_ready"), count(("rope", "kc", "q1", "q4", "k4", "qc4"), made))
                    if kind == "tqm":
                        m = ("mxs_end", b) if step[1] == 4 else ("mxc", step[1], b)
                        pe.wait_ge(sem("max_ready"), count(("mxc", "mxs_end"), m))
                    buf = kn if kind == "tk4" else qcn if step[1] == 5 else qn
                    stacked(step, buf[:, b % 2])
                elif kind == "mxc":
                    _, s, b = step
                    misc_written(pe, ("tq", s, b))
                    misc_written(pe, ("kc", 1 if s == 1 else 4, "t"))
                    for i in range(2):
                        dst = take_scores(step + (i,))
                        q = (qT[:, :, toks(b)] if s == 1 else qcT[:, b % 2, :, :])[:, :, i * P:(i + 1) * P]
                        for B in range(4):
                            ins = mm(dst[:, B * T:(B + 1) * T], q[:, B, :],
                                     kcm[:, :, B, b * KV:(b + 1) * KV], start=True, stop=True)
                        ins.then_inc(score_full, 1)
                elif kind == "mxs":
                    _, b, c = step
                    pe.wait_ge(sem("masks_ready"), 2)
                    misc_written(pe, ("tq", 4, b))
                    pe.wait_ge(sem("km4_ready"), 4 * (b + 1))
                    dst = take_scores(step)
                    for n in range(2):
                        o = dst[:, n * 512:(n + 1) * 512]
                        if c < 2:
                            B = 2 * c + n
                            mm(o, identb[:, :], causal_nat[:, :, :].rearrange("p r t -> p (r t)"),
                               start=True, stop=False)
                            ins = mm(o, qT[:, B, b * T:b * T + P], km4[:, b % 2, :, B, 0:P],
                                     start=False, stop=True)
                        else:
                            B = c - 2
                            mm(o, qT[:, B, b * T + P:(b + 1) * T], km4[:, b % 2, 2 * n:2 * n + 2, B, :],
                               start=True, stop=False)
                            ins = mm(o.rearrange("p (r k) -> p r k", r=2)[:, :, P:T], identb[:, :],
                                     causal_nat[:, 0:2, :], start=False, stop=True)
                    ins.then_inc(score_full, 1)
                elif kind == "tr2":
                    pe.wait_ge(sem("xn_ready"), count(("ln", "ln3"), ("ln", 2, b)))
                    transposes(step, take_misc(step), [xn[:, 0, 2 * b + i, :] for i in range(2)] +
                               [n2[:, 2 * b + i, :] for i in range(2)], ident)
                elif kind == "xa":
                    misc_written(pe, ("tr2", b))
                    mm(take_misc(step)[:, 0:T], W("attn_w"), n2T[:, toks(b)], start=True, stop=True)\
                        .then_inc(misc_full, 1)
                elif kind == "ffn_up":
                    flush()
                    j = step[1]
                    for n in range(NB):
                        misc_written(pe, ("xa", n))
                    pe.wait_ge(sem(f"w1a_loaded{j // 2}"), 16)
                    dst = take_scores(step)
                    for n in range(2 * HC):
                        e, c = 2 * j + n // HC, n % HC
                        ins = mm(dst[:, n * P:(n + 1) * P], w1[:, e, c * P:(c + 1) * P],
                                 experts(xaT, e), start=True, stop=True)
                    ins.then_inc(score_full, 1)
                elif kind == "ffn_down":
                    j = step[1]
                    score_written(pe, ("ffn_up", j))
                    pe.wait_ge(sem(f"w2a_loaded{j // 2}"), 16)
                    dst = take_misc(step)
                    for n in range(2):
                        for c in range(HC):
                            ins = mm(dst[:, n * P:(n + 1) * P], w2[:, 2 * j + n, c, :],
                                     hid0[:, 2 * j + n, c * P:(c + 1) * P], start=c == 0, stop=c == HC - 1)
                    ins.then_inc(misc_full, 1)
                elif kind == "nxt":
                    for n in range(NE // 2):
                        misc_written(pe, ("ffn_down", n))
                    natural(step, tile_cols(eoT, b), W("next_w"))
                elif kind == "tr3":
                    pe.wait_ge(sem("xn_ready"), count(("ln", "ln3"), ("ln3", b)))
                    transposes(step, take_misc(step), [n2[:, 2 * b + i, :] for i in range(2)], ident)
                elif kind == "prj3":
                    misc_written(pe, ("tr3", b))
                    dst = take_misc(step + ("qk",))
                    for n, w in enumerate(("wq3", "wk3")):
                        ins = mm(dst[0:DH, n * T:(n + 1) * T], W(w), xnT[:, 1, toks(b)], start=True, stop=True)
                    ins.then_inc(misc_full, 1)
                    natural(step + ("vo",), tile_cols(xnT[:, 1, :], b), W("wvo3"))
                elif kind == "rows3":
                    dst = take_misc(step)
                    for n, w in enumerate(("wi3", "wf3")):
                        ins = mm(dst[0:1, n * T:(n + 1) * T], W(w), xnT[:, 1, toks(b)], start=True, stop=True)
                    ins.then_inc(misc_full, 1)
                elif kind == "ml" and step[2] == 0:
                    b = step[1]
                    pe.wait_ge(sem("rows_ready"), b + 1)
                    pe.wait_ge(sem("presets"), 1)
                    pe.wait_ge(sem("masks_ready"), 2)
                    misc_written(pe, ("prj3", b, "qk"))
                    dst = take_scores(step)
                    for kt, (at, n) in enumerate(((0, T), (T, P))):
                        o, ts = dst[:, at:at + n], slice(T - n, T)
                        mm(o, rowa[:, b % 2, kt * P:(kt + 1) * P], one_row[:, 0:n], start=True, stop=False)
                        mm(o, one_row[:, 0:P], rowg[:, b % 2, ts], start=False, stop=False)
                        mm(o[:, 0:P], identb[:, :], causal_tr[:, 0, :], start=False, stop=True)
                        ins = mm(dst[:, 512 + at:512 + at + n], kT3[:, b % 2, kt * P:(kt + 1) * P],
                                 qT3[:, b % 2, ts], start=True, stop=True)
                    ins.then_inc(score_full, 1)
                elif kind == "ml" and step[2] == 1:
                    b = step[1]
                    score_written(pe, ("ml", b, 0))
                    misc_written(pe, ("prj3", b, "vo"))
                    pe.wait_ge(sem("v3_ones"), b + 1)
                    dst, w = take_misc(step), weight[:, b % 2, :]
                    n = DH + 1
                    mm(dst[:, 0:n], w[:, 0:P], v3[:, b % 2, 0, :], start=True, stop=True)
                    mm(dst[:, n:2 * n], w[:, P:T], v3[:, b % 2, 0, :], start=True, stop=False)
                    mm(dst[:, n:2 * n], w[:, T:T + P], v3[:, b % 2, 1, :], start=False, stop=True)\
                        .then_inc(misc_full, 1)
                elif kind == "ml" and step[2] == 2:
                    b = step[1]
                    misc_written(pe, ("ml", b, 1))
                    dst = take_misc(step)
                    for i in range(2):
                        ins = nc.tensor.transpose(dst[0:DH, i * P:(i + 1) * P], h3[:, b % 2, i, :], ident)
                    ins.then_inc(misc_full, 1)
                elif kind == "ml":
                    misc_written(pe, ("ml", step[1], 2))
                    natural(step, [h3T[:, i * P:(i + 1) * P] for i in range(2)], W6("wout3"))
                elif kind == "gate":
                    misc_written(pe, ("tr", 6, b))
                    natural(step, tile_cols(xnT[:, 1, :], b), W("gate"))
                elif kind == "gate_b":
                    pe.wait_ge(sem("comb_ready"), 2 * (b + 1))
                    pe.wait_ge(sem("b2m_loaded"), 16)
                    key = step + ("t",)
                    dst = take_misc(key)
                    for i in range(2):
                        ins = nc.tensor.transpose(dst[0:NE, i * P:(i + 1) * P], comb[:, 2 * b + i, :], ident)
                    ins.then_inc(misc_full, 1)
                    misc_written(pe, key)
                    natural(step + ("b",), [combT[:, i * P:(i + 1) * P] for i in range(2)], b2m[:, :])
                elif kind == "moe_up":
                    flush()
                    _, h, e = step
                    for b in (2 * h, 2 * h + 1):
                        misc_written(pe, ("tr", 6, b))
                    pe.wait_ge(sem(f"w1b_loaded{e // 4}"), 16)
                    for n in range(2):
                        dst = take_scores(step + (n,))
                        for cc in range(2):
                            c = 2 * n + cc
                            ins = mm(dst[:, cc * 512:(cc + 1) * 512], w1[:, e, c * P:(c + 1) * P],
                                     xnT[:, 1, h * 512:(h + 1) * 512], start=True, stop=True)
                        ins.then_inc(score_full, 1)
                elif kind == "moe_down":
                    _, h, e = step
                    k = h * NE + e
                    for n in range(2):
                        score_written(pe, ("moe_up", h, e, n))
                    pe.wait_ge(sem(f"w2b_loaded{e // 4}"), 16)
                    dst = take_misc(step)
                    for i in range(4):
                        for c in range(HC):
                            ins = mm(dst[:, i * P:(i + 1) * P], hid1[:, k % 2, c, i * P:(i + 1) * P],
                                     w2[:, e, c, :], start=c == 0, stop=c == HC - 1)
                    ins.then_inc(misc_full, 1)



def constants():
    import numpy as np

    p = np.arange(P)
    c = np.zeros((P, CST["all"][1]), np.float32)

    def put(name, value):
        a, n = CST[name]
        c[:, a:a + n] = value

    put("ident", np.eye(P))
    source = (p // 16) * 16 + 8 + p % 8
    perm = np.zeros((P, P))
    perm[source, p] = 1
    put("perm", perm)
    put("causal_nat", np.where(p[None, :] > p[:, None], -1e30, 0))
    put("causal_tr", np.where(p[:, None] > p[None, :], -1e30, 0))
    put("rowmask", p[:, None] // 32 == np.arange(4)[None, :])
    put("iota", np.broadcast_to(np.arange(NE), (P, NE)))
    half = HD // 2
    inv = (1.0 / np.float32(10000.0) ** (np.arange(half, dtype=np.float32) / half)).astype(np.float32)
    ang = np.arange(T, dtype=np.float32)[:, None] * inv[None, :]
    cos, sin = np.cos(ang), np.sin(ang)
    for name, t in (("cos", np.concatenate([cos, cos], 1)), ("sin", np.concatenate([-sin, sin], 1))):
        put(name, t.reshape(2, P, HD).transpose(1, 0, 2).reshape(P, 2 * HD))
    return c


def padded(w, head_of):
    import numpy as np

    out = np.zeros((P, 2, P), np.float32)
    for B in range(4):
        for r in range(4):
            h, at = head_of(B, r), 32 * r + 16 * (B % 2)
            out[at:at + HD, B // 2, :] = w[h * HD:(h + 1) * HD, :]
    return out.reshape(P, 2 * P)


def kernel(**inputs):
    import numpy as np
    import concourse.bacc as bacc
    from concourse.bass_utils import run_bass_kernel_spmd

    g = {k: np.asarray(v) for k, v in inputs.items()}
    wqkv = g["L0_attn_w_qkv"]
    wq = wqkv[:, 0:P].reshape(P, 4, 4, HD).transpose(0, 2, 1, 3).reshape(P, P)
    row1 = lambda n: g[n].reshape(1, -1)
    ctx = g["ctx_512"].transpose(2, 0, 1)
    w1 = lambda w: np.ascontiguousarray(w.transpose(1, 0, 2))
    w2 = lambda w: np.ascontiguousarray(w.reshape(NE, HC, P, P).transpose(2, 0, 1, 3))
    arrays = {
        "x": g["x"],
        "cst": constants(),
        "wa": np.concatenate([wq, wqkv[:, P:], padded(g["L0_attn_w_o"], lambda B, r: 4 * r + B)], 1),
        "wb": np.concatenate([
            g["L0_xattn_Wq"], padded(g["L0_xattn_Wo"], lambda B, r: 4 * B + r),
            g["L0_ffn_attn_w"].T, g["L0_ffn_next_w"].T, g["L1_attn_Wq"].T, g["L1_attn_Wk"].T,
            g["L1_attn_Wv"].T, g["L1_attn_Wo"].T, g["L1_attn_wi_w"].T, g["L1_attn_wf_w"].T,
            g["L1_xattn_Wk"], g["L1_xattn_Wq"], g["L1_xattn_Wv"], g["L1_xattn_Wcq"],
            padded(g["L1_xattn_Wp"], lambda B, r: 4 * B + r), g["L1_ffn_gate_w"].T], 1),
        "w64": np.concatenate([
            g["L0_xattn_Wk"], g["L0_xattn_Wv"], g["L1_xattn_Wck"], g["L1_xattn_Wcv"],
            g["L1_attn_Wout"].T, ctx.reshape(64, NB * KV),
            np.stack([ctx, ctx], 2).reshape(64, NB * 2 * KV)], 1),
        "col": np.concatenate([
            row1("L0_ffn_ln_scale"), row1("L0_ffn_ln_bias"), row1("L0_ffn_attn_b"), g["L0_ffn_b2"],
            g["L0_ffn_b1"].reshape(NE * HC, P), row1("L1_attn_norm_w"),
            g["L1_ffn_b1"].reshape(NE * HC, P)], 0).T,
        "row": np.concatenate([row1(n) for n in (
            "L0_xattn_bq", "L0_xattn_bk", "L0_xattn_bv", "L0_xattn_bo", "L0_ffn_next_b",
            "L1_attn_bo", "L1_xattn_bk", "L1_xattn_bq", "L1_xattn_bv", "L1_xattn_bck",
            "L1_xattn_bcq", "L1_xattn_bcv", "L1_xattn_bp")], 1),
        "gate_bias": np.concatenate([row1("L1_attn_wi_b"), row1("L1_attn_wf_b")], 1),
        "b2m": g["L1_ffn_b2"],
        "w1a": w1(g["L0_ffn_w1"]),
        "w2a": w2(g["L0_ffn_w2"]),
        "w1b": np.ascontiguousarray(g["L1_ffn_w1"].transpose(2, 0, 1)),
        "w2b": w2(g["L1_ffn_w2"].transpose(0, 2, 1)),
    }
    nc = bacc.Bacc("TRN2", target_bir_lowering=False, num_devices=1)
    maps, d = {}, {}
    for name, a in arrays.items():
        maps[f"in_{name}"] = np.ascontiguousarray(a)
        d[name] = nc.dram_tensor(f"in_{name}", a.shape, mybir.dt.from_np(a.dtype), kind="ExternalInput").ap()
    out = nc.dram_tensor("out", (NB, T, P), F32, kind="ExternalOutput").ap()
    decoder(nc, d, out)
    r = run_bass_kernel_spmd(nc, [maps], core_ids=[0])
    return r.results[0]["out"]
```

```python
from contextlib import ExitStack

import concourse.bass as bass
from concourse import mybir

F32 = mybir.dt.float32
F16 = mybir.dt.float16
BF16 = mybir.dt.bfloat16
U32 = mybir.dt.uint32
ALU = mybir.AluOpType
ACT = mybir.ActivationFunctionType
X = mybir.AxisListType.X

P = 128
NB = 4
T = 256
NT = NB * T // P
NTOK = NB * T
H = 16
HD = 8
KV = 64
DH = 64
NE = 8
HC = 4
SCALE = float(1.0 / (HD ** 0.5))
MAXDIV = 64.0



def columns(*sizes):
    at, out = 0, {}
    for name, n in sizes:
        out[name] = (at, n)
        at += n
    out["all"] = (0, at)
    return out


CST = columns(("ident", P), ("causal_nat", P), ("causal_tr", P), ("rowmask", 4),
              ("iota", NE), ("cos", 2 * HD), ("sin", 2 * HD))
WA = columns(("qkv", 192), ("wo0", P))
WB = columns(("wq1", P), ("wo1", P), ("attn_w", P), ("next_w", P), ("wqi3", DH + 1),
             ("wkf3", DH + 1), ("wvo3", 2 * DH), ("wk4", P), ("wq4", P), ("wv4", P),
             ("wcq4", P), ("wp4", P), ("gate", NE))
W64 = columns(("wk1", P), ("wv1", P), ("wck4", P), ("wcv4", P), ("wout3", P), ("ctx", NB * KV),
              ("ctx2", NB * 2 * KV))
COL = columns(("ln_scale", 1), ("ln_bias", 1), ("attn_b", 1), ("b2", NE), ("b1", NE * HC),
              ("norm_w", 1), ("b1m", NE * HC))
ROW = columns(("bq1", P), ("bk1", P), ("bv1", P), ("bo1", P), ("next_b", P), ("bo3", DH),
              ("bk4", P), ("bq4", P), ("bv4", P), ("bck4", P), ("bcq4", P), ("bcv4", P), ("bp4", P))


class Ring:

    def __init__(self, slots, uses):
        self.at, given = {}, [0] * slots
        for n, (key, gives) in enumerate(uses):
            s = n % slots
            self.at[key] = (s, n + 1, given[s], given[s] + gives)
            given[s] += gives

    def slot(self, key):
        return self.at[key][0]

    def full(self, key):
        return self.at[key][1]

    def before(self, key):
        return self.at[key][2]

    def done(self, key):
        return self.at[key][3]


class Slots:

    def __init__(self, slots, holders):
        self.at, last = {}, [None] * slots
        for n, (holder, release) in enumerate(holders):
            self.at[holder] = (n % slots, last[n % slots], n // slots)
            last[n % slots] = release

    def slot(self, holder):
        return self.at[holder][0]

    def before(self, holder):
        return self.at[holder][1]

    def turn(self, holder):
        return self.at[holder][2]


SELF_CHUNKS = [("k0", 0), ("k0", 1), ("k1", 0), ("k0", 2), ("k0", 3), ("k1", 1)]
CHUNKS = {0: 6, 1: 2, 4: 6, 5: 2}
HELD = {"stack_q": 2, "stack_k": 2, "stack_c": 2, "qcT": 2, "km4": 2, "prob": 4, "out": 2,
        "copied": 2, "y": 2, "y4": 2, "yT": 2, "rope": 2, "mlstm": 2, "hidden": 2, "kT": 1, "combT": 1,
        "zn": 2, "mx": 2, "mxc": 2, "hid0": 2}
PAIRS = [(0, 2), (1, 3)]
TABLES = {"ropea": "sqrt", "sc": "exp", "p3b": "exp", "ml0": "exp", "ga": "exp", "fup": "gelu",
          "nxa": "gelu"}


def the_steps():
    steps, take, give = {}, {}, {}

    def add(step, after, *parts):
        steps[step] = ([a for a in after if a], parts)

    def hold(pool, holder, first, last):
        take.setdefault(first, []).append((pool, holder))
        give.setdefault(last, []).append((pool, holder))

    def norm(s, b, after):
        add(("lna", s, b), after, ("D", 0.7), ("G", 2.2 if s == "3b" else 0.95))
        parts = [("D", 0.5)] + ([("G", 0.7)] if s in (1, 4) else [])
        add(("lnb", s, b), [("lna", s, b)], *parts)
        return ("lnb", s, b)

    def attention(s, b, after):
        for c in range(CHUNKS[s]):
            sc, pv = ("sc", s, b, c), ("pv", s, b, c)
            parts = {0: (("P", 0.45), ("A", 0.95), ("G", 0.85)), 4: (("P", 0.7), ("A", 0.95))}.get(
                s, (("P", 0.5), ("A", 0.95)))
            add(sc, after + [c and ("sc", s, b, c - 1)], *parts)
            add(pv, [sc, c and ("pv", s, b, c - 1)], ("P", 0.55 if s in (0, 4) else 0.3))
            hold("prob", pv, sc, pv)
        hold("out", (s, b), ("sc", s, b, 0), ("oc", s, b))
        add(("oc", s, b), [("pv", s, b, CHUNKS[s] - 1), ("oc", 4, b) if s == 5 else None], ("A", 0.5))
        hold("copied", (s, b), ("oc", s, b), ("ot", s, b))
        add(("ot", s, b), [("oc", s, b), ("ot", 4, b) if s == 5 else None], ("P", 0.45),
            ("D", 1.2 if s == 5 else 0.8))
        if s == 4:
            hold("y4", b, ("ot", 4, b), ("ot", 5, b))
        else:
            hold("y", (s, b), ("ot", s, b), ("ou", s, b))
            add(("ou", s, b), [("ot", s, b)], ("P", 0.4), ("A", 0.4))
            hold("yT", (s, b), ("ou", s, b), ("op", s, b))
            add(("op", s, b), [("ou", s, b)], ("P", 0.45), ("D", 0.5))

    def stacked_queries(kind, s, b, after, keys):
        pool = "stack_c" if s == 5 else "stack_q"
        add((kind, b), after, ("P", 0.45), ("D", 1.5))
        add(("tq", s, b), [(kind, b)], ("P", 0.5), ("A", 1.05))
        if s == 4:
            for c in range(6):
                add(("mxs", b, c), [("tq", 4, b), c and ("mxs", b, c - 1)] + keys, ("P", 0.7), ("D", 1.15))
            hold("mx", b, ("mxs", b, 0), ("mxe", s, b))
            last = ("mxs", b, 5)
        else:
            for i in range(2):
                add(("mxc", s, b, i), [("tq", s, b), i and ("mxc", s, b, 0)] + keys, ("P", 0.5), ("D", 1.15))
            hold("mxc", (s, b), ("mxc", s, b, 0), ("mxe", s, b))
            last = ("mxc", s, b, 1)
        add(("mxe", s, b), [last], ("D", 0.6))
        add(("tqm", s, b), [("mxe", s, b)], ("P", 0.5), ("A", 1.05))
        hold(pool, (s, b), (kind, b), ("tqm", s, b))
        return ("tqm", s, b)

    every = range(NB)
    for b in every:
        n = norm(0, b, [])
        add(("tr", 0, b), [n], ("P", 0.4), ("A", 0.4))
        add(("qkv", b), [("tr", 0, b)], ("P", 0.7), ("A", 0.5))
        add(("ropea", b), [("qkv", b)], ("A", 0.45), ("D", 0.4), ("A", 0.3))
        add(("ropeb", b), [("ropea", b)], ("D", 3.7), ("G", 2.2))
        hold("rope", b, ("ropea", b), ("ropeb", b))
        for i in range(2):
            add(("tq0", b, i), [("ropeb", b), i and ("tq0", b, 0)], ("P", 0.5), ("A", 0.5), ("D", 0.6))
        hold("stack_q", (0, b), ("ropeb", b), ("tq0", b, 1))
        hold("stack_k", (0, b), ("ropeb", b), ("tq0", b, 1))
    for l, after in ((1, []), (4, [("sc", 1, b, 1) for b in every])):
        add(("kck", l), after, ("P", 0.6), ("D", 1.2))
        if l == 1:
            add(("presets1", 0), [], ("G", 3.5))
        add(("kcv", l), after + [("presets1", 0)], ("P", 1.0), ("D", 1.2))
        add(("kct", l), [("kck", l)], ("P", 0.6), ("D", 3.2))
        hold("stack_k", ("context", l), ("kck", l), ("kct", l))
    for b in every:
        attention(0, b, [("tq0", b, 1)])
        add(("presets4", b), [("pv", 0, b, 5)], ("G", 1.8))
        n = norm(1, b, [("op", 0, b)])
        add(("tr", 1, b), [n], ("P", 0.4), ("A", 0.4))
        m = stacked_queries("q1", 1, b, [("tr", 1, b)], [("kct", 1)])
        attention(1, b, [m, ("kcv", 1)])
        n = norm("2b", b, [norm(2, b, [("op", 1, b)])])
        add(("tr2", b), [n], ("P", 0.8), ("A", 0.4), ("D", 0.5))
        add(("xa", b), [("tr2", b)], ("P", 0.5), ("D", 0.6))
    for j in range(NE // 2):
        pair = PAIRS[j // 2]
        add(("fup", j), [("xa", b) for b in pair] + [j % 2 and ("fup", j - 1)], ("P", 1.8), ("A", 2.2))
        add(("fdown", j), [("fup", j), j % 2 and ("fdown", j - 1)], ("P", 1.8), ("D", 0.6))
        hold("hid0", j, ("fup", j), ("fdown", j))
    for b in every:
        j = 2 * (b % 2)
        add(("nxa", b), [("fdown", j), ("fdown", j + 1)], ("P", 0.45), ("D", 0.4), ("A", 0.4))
        add(("nxb", b), [("nxa", b)], ("D", 0.4))
        hold("zn", b, ("nxa", b), ("nxb", b))
        n = norm("3b", b, [norm(3, b, [("nxb", b)])])
        add(("tr3", b), [n], ("P", 0.4), ("A", 0.4))
        add(("p3a", b), [("tr3", b)] + [("ropeb", n) for n in every], ("P", 1.0), ("A", 0.4), ("D", 1.1))
        add(("p3b", b), [("tr3", b), ("p3a", b)], ("P", 0.5), ("A", 0.3), ("D", 0.4), ("A", 0.3))
        add(("rows", b), [("p3a", b)], ("D", 2.0))
        add(("ml", b, 0), [("rows", b)], ("P", 3.2), ("A", 0.5), ("D", 0.6))
        add(("ml", b, 1), [("ml", b, 0), ("p3b", b)], ("P", 0.7), ("D", 2.2))
        add(("ml", b, 2), [("ml", b, 1)], ("P", 0.4), ("A", 0.4))
        add(("ml", b, 3), [("ml", b, 2)], ("P", 0.5), ("D", 0.5))
        hold("mlstm", b, ("p3a", b), ("ml", b, 3))
    for b in every:
        n = norm(4, b, [("ml", b, 3)])
        add(("tr", 4, b), [n], ("P", 0.4), ("A", 0.4))
        add(("k4", b), [("tr", 4, b)], ("P", 0.45), ("D", 1.5))
        add(("tk4", b), [("k4", b)] + [("sc", 0, n, 5) for n in every],
            ("P", 0.5), ("A", 1.05), ("D", 1.8))
        hold("stack_k", (4, b), ("k4", b), ("tk4", b))
        hold("km4", b, ("tk4", b), ("sc", 4, b, 5))
        add(("v4", b), [("tr", 4, b), ("presets4", b)], ("P", 0.45), ("D", 0.6))
        m = stacked_queries("q4", 4, b, [("tk4", b)], [])
        attention(4, b, [m, ("v4", b)])
        m = stacked_queries("qc4", 5, b, [("tr", 4, b)], [("kct", 4)])
        hold("qcT", b, ("tq", 5, b), ("sc", 5, b, 1))
        attention(5, b, [m, ("kcv", 4), ("sc", 4, b, 5)])
        n = norm(6, b, [("op", 5, b)])
        add(("tr", 6, b), [n], ("P", 0.4), ("A", 0.4))
        add(("ga", b), [("tr", 6, b)], ("P", 0.3), ("D", 1.3), ("A", 0.2))
        add(("gb", b), [("ga", b)], ("D", 1.8))
        add(("gc", b), [("gb", b)], ("P", 0.3), ("D", 0.4))
        add(("gd", b), [("gc", b)], ("P", 0.4), ("D", 0.5))
        hold("combT", b, ("gc", b), ("gd", b))
    for n in range(2 * NE):
        h, e = n // NE, n % NE
        prev = ((n - 1) // NE, (n - 1) % NE)
        after = [("tr", 6, b) for b in PAIRS[h]] + [("ml", b, 3) for b in every]
        for q in range(2):
            add(("mup", h, e, q), after + [("mup", h, e, 0) if q else n and ("mup",) + prev + (1,)],
                ("P", 1.72), ("A", 0.6), ("D", 0.67))
        add(("mdown", h, e), [("mup", h, e, 1), n and ("mdown",) + prev] +
            [("gd", b) for b in PAIRS[h]], ("P", 3.45), ("D", 1.15))
        hold("hidden", (h, e), ("mup", h, e, 0), ("mdown", h, e))
    return steps, take, give


STEPS, TAKE, GIVE = the_steps()
HOP = 0.25


def kind_of(step):
    if step[0] == "ml":
        return f"ml{step[2]}"
    staged = ("lna", "lnb", "tr", "sc", "pv", "oc", "ot", "ou", "op", "tq", "tqm", "mxc", "mxe")
    return f"{step[0]}{step[1]}" if step[0] in staged else step[0]


MISC_GIVES = {"tr": 1, "qkv": 1, "tq0": 2, "kck": 1, "kcv": 1, "kct": 1, "ot": 1, "ou": 1, "op": 1,
              "q1": 1, "tq": 1, "tqm": 1, "tr2": 2, "xa": 1, "fdown": 1, "nxa": 1, "tr3": 1,
              "p3a": 2, "p3b": 2, "q4": 1, "k4": 1, "tk4": 1, "qc4": 1, "v4": 1, "ga": 1, "gc": 1,
              "gd": 1, "mdown": 1}
SCORE_GIVES = {"sc": 1, "mxc": 1, "mxs": 1, "fup": 1, "mup": 2}
RINGS = {"misc": 2, "scores": 2}


def ring_of(step):
    if step[0] == "ml":
        return "misc" if step[2] else "scores"
    return "misc" if step[0] in MISC_GIVES else "scores" if step[0] in SCORE_GIVES else None


def reading_part(step):
    return 1 if step[0] in ("sc", "tk4", "nxa", "ga") else len(STEPS[step][1]) - 1


def table_of(step):
    return TABLES.get("sc" if step[0] == "sc" else kind_of(step))


def pair_of(step):
    if step[0] in ("kck", "kcv", "kct"):
        return 0
    if step[0] in ("fup", "fdown"):
        return step[1] // 2
    if step[0] in ("mup", "mdown"):
        return step[1]
    b = step[1] if step[0] in ("ml", "tq0", "mxs") or step[0] == "presets4" else step[-1]
    if step[0] in ("sc", "pv", "mxc"):
        b = step[2]
    return b % 2


def the_order():
    after = {s: [] for s in STEPS}
    for s, (deps, _) in STEPS.items():
        for dep in deps:
            after[dep].append(s)
    way = {}

    def to_end(s):
        if s not in way:
            own = sum(t + HOP for _, t in STEPS[s][1])
            way[s] = own + max((to_end(n) for n in after[s]), default=0)
        return way[s]

    for s in reversed(list(STEPS)):
        to_end(s)
    left = {s: len(deps) for s, (deps, _) in STEPS.items()}
    ends = {}
    free = dict.fromkeys("PADG", 0.0)
    held = {pool: [] for pool in HELD}
    released = {pool: {} for pool in HELD}
    ready = [s for s in STEPS if not left[s]]
    order = []
    table = None
    given = {ring: [0.0] * n for ring, n in RINGS.items()}
    while ready:
        best = None
        for s in ready:
            t = max((ends[dep] for dep in STEPS[s][0]), default=0.0)
            blocked = False
            for pool, holder in TAKE.get(s, ()):
                n = len(held[pool]) - HELD[pool]
                if n >= 0:
                    last = released[pool].get(held[pool][n])
                    if last is None:
                        blocked = True
                        break
                    t = max(t, last)
            if blocked:
                continue
            if ring_of(s):
                t = max(t, given[ring_of(s)][-RINGS[ring_of(s)]])
            t = max(t + HOP, free[STEPS[s][1][0][0]])
            switch = table_of(s) not in (None, table)
            key = t - PULL * (way[s] + AHEAD.get(kind_of(s), (0, 0))[pair_of(s)]) + SWITCH * switch
            if best is None or key < best[0]:
                best = (key, s, t)
        assert best is not None, "the steps hold each other up"
        _, s, t = best
        ready.remove(s)
        order.append(s)
        for n, (engine, dur) in enumerate(STEPS[s][1]):
            t = max(t, free[engine])
            if engine == "A" and table_of(s) not in (None, table):
                table = table_of(s)
                t += 1.3
            t = free[engine] = t + dur
            if ring_of(s) and n == reading_part(s):
                given[ring_of(s)].append(t)
            t += HOP
        ends[s] = t - HOP
        for pool, holder in TAKE.get(s, ()):
            held[pool].append(holder)
        for pool, holder in GIVE.get(s, ()):
            released[pool][holder] = ends[s]
        for n in after[s]:
            left[n] -= 1
            if not left[n]:
                ready.append(n)
    return order, max(ends.values())


PULL, SWITCH = 0.0021781337777084177, 1.6396770363479596
AHEAD = {"fdown": (120, -180), "fup": (610, 20), "ga": (-50, -250), "gb": (300, 590), "gc": (10,
         -90), "gd": (180, -250), "k4": (-660, 60), "kck": (-240, 0), "kct": (-120, 0), "kcv":
         (-380, 0), "lna0": (-170, -420), "lna1": (350, 670), "lna2": (-130, 490), "lna2b": (730,
         930), "lna3": (900, 380), "lna3b": (1080, 1210), "lna4": (190, -320), "lna6": (-280, 810),
         "lnb0": (280, 490), "lnb1": (-350, -330), "lnb2": (-50, 250), "lnb2b": (300, -160),
         "lnb3": (680, -160), "lnb3b": (810, 1010), "lnb4": (370, -180), "lnb6": (10, 940),
         "mdown": (-240, 20), "ml0": (-810, 40), "ml1": (60, 10), "ml2": (-50, 470), "ml3": (-450,
         50), "mup": (-130, 210), "mxc1": (-120, 100), "mxc5": (-600, 70), "mxe1": (730, 440),
         "mxe4": (400, 620), "mxe5": (-490, -110), "mxs": (-100, -180), "nxa": (110, -220), "nxb":
         (660, -540), "oc0": (630, -90), "oc1": (660, -1200), "oc4": (-490, -720), "oc5": (-1120,
         -630), "op0": (-10, 430), "op1": (20, 810), "op5": (660, -610), "ot0": (790, 590), "ot1":
         (-80, -120), "ot4": (1530, 140), "ot5": (340, 300), "ou0": (80, 180), "ou1": (-180, -130),
         "ou5": (-570, 80), "p3a": (130, 180), "p3b": (-350, 70), "presets1": (-220, 0),
         "presets4": (560, 950), "pv0": (-170, -60), "pv1": (-160, 80), "pv4": (110, -170), "pv5":
         (190, -160), "q1": (-150, 690), "q4": (280, -40), "qc4": (-50, -120), "qkv": (1470, 410),
         "ropea": (320, -100), "ropeb": (-260, -670), "rows": (520, 1180), "sc0": (-120, 60),
         "sc1": (280, 200), "sc4": (-10, -150), "sc5": (190, 250), "tk4": (100, -210), "tq0": (30,
         -80), "tq1": (-140, 380), "tq4": (510, -150), "tq5": (550, -560), "tqm1": (-200, -150),
         "tqm4": (840, 70), "tqm5": (-360, 310), "tr0": (760, 30), "tr1": (-180, 570), "tr2":
         (-270, -570), "tr3": (-820, 570), "tr4": (360, 770), "tr6": (-240, -240), "v4": (-540,
         620), "xa": (-240, -160)}
ORDER, ABOUT = the_order()
INDEX = {step: n for n, step in enumerate(ORDER)}


def count(kinds, step):
    return sum(1 for s in ORDER[:INDEX[step] + 1] if s[0] in kinds)


def slots(pool):
    release = {(p, holder): s for s, gives in GIVE.items() for p, holder in gives}
    return Slots(HELD[pool], [(holder, release[pool, holder]) for s in ORDER
                              for p, holder in TAKE.get(s, ()) if p == pool])


SLOTS = {pool: slots(pool) for pool in HELD}
MISC = Ring(2, [(s, 1 if s[0] == "ml" else MISC_GIVES[s[0]]) for s in ORDER
                if s[0] in MISC_GIVES or s[0] == "ml" and s[2]])
SC = Ring(2, [(s, 1 if s[0] == "ml" else SCORE_GIVES[s[0]]) for s in ORDER
              if s[0] in SCORE_GIVES or s[0] == "ml" and not s[2]])


def decoder(nc, d, out):
    with ExitStack() as ctx:
        sb = lambda name, shape, dt=F32: ctx.enter_context(nc.sbuf_tensor(name, shape, dt))
        psum = lambda name, shape, dt=F32: ctx.enter_context(nc.psum_tensor(name, shape, dt))
        sems = {}

        def sem(name):
            if name not in sems:
                sems[name] = ctx.enter_context(nc.semaphore(name))
            return sems[name]

        scores = psum("scores", [P, 2, 1024])
        outs = psum("outs", [P, 2, 512])
        misc = psum("misc", [P, 2, 512])
        misc16 = [misc[:, s, :].bitcast(F16) for s in range(2)]

        x = sb("x", [P, NT, P])
        cst = sb("cst", [P, CST["all"][1]])
        wa = sb("wa", [P, WA["all"][1]])
        wb = sb("wb", [P, WB["all"][1]])
        w64 = sb("w64", [64, W64["all"][1]])
        col = sb("col", [P, COL["all"][1]])
        row = sb("row", [P, ROW["all"][1]])
        gate_bias = sb("gate_bias", [P, 2])
        b2m = sb("b2m", [NE, P])
        w1 = sb("w1", [P, NE, HC * P])
        w2 = sb("w2", [P, NE, HC, P])
        xn = sb("xn", [P, 2, NT, P])
        xnT = sb("xnT", [P, 2, NTOK])
        stat = sb("stat", [P, 2, NT, 6])
        mv = sb("mv", [P, 2, NT, 2])
        rstd = sb("rstd", [P, 2, NT])
        neg_half = sb("neg_half", [P, 2])
        ident16 = sb("ident16", [P, P], F16)
        identb = sb("identb", [P, P], BF16)
        causal_nat = sb("causal_nat", [P, P], BF16)
        causal_tr = sb("causal_tr", [P, P], BF16)
        qn = sb("qn", [P, 2, 2, H, 32], F16)
        kn = sb("kn", [P, 2, 2, H, 32], F16)
        qcn = sb("qcn", [P, 2, 2, H, 32], F16)
        qT = sb("qT", [P, 4, NTOK], F16)
        qcT = sb("qcT", [P, 2, 4, T], F16)
        kT = sb("kT", [P, 4, T], F16)
        kcm = sb("kcm", [P, 4, 4, NB * KV], F16)
        split = sb("split", [P, 2, P])
        vst = sb("vst", [P, NT, H, 32])
        vc = sb("vc", [P, 2, NB, 2, 4, 32])
        mx = sb("mx", [P, 2, 2, H])
        mxc = sb("mxc", [P, 2, 2, H])
        copied = sb("copied", [P, 2, 512])
        y4 = sb("y4", [P, 2, 2, P])
        y = sb("y", [P, 2, 2, P])
        yT = sb("yT", [P, 2, T])
        sums = sb("sums", [P, 2 * H])
        region_k = sb("region_k", [P, 4096])
        km0 = region_k[:, 0:2048].bitcast(F16).rearrange("p (r t) -> p r t", r=4)
        km4 = region_k[:, :].bitcast(F16).rearrange("p (s r g t) -> p s r g t", s=2, r=4, g=4)
        flatT, n2T = xnT[:, 0, :], xnT[:, 1, :]
        xaT, eoT = xnT[:, 0, :], xnT[:, 1, :]
        region_p = sb("region_p", [P, HELD["prob"] * 1024])
        probs = region_p[:, :].rearrange("p (s n) -> p s n", s=HELD["prob"])
        hid0 = sb("hid0", [P, HELD["hid0"], 2 * HC * P])
        tmp = sb("tmp", [P, 4620])

        def of_tmp(rows, first, n):
            return tmp[rows, first:first + n]

        every = slice(0, P)
        raw = of_tmp(every, 0, 1280).rearrange("p (b h e) -> p b h e", b=4, e=HD)
        rawv = of_tmp(every, 1280, 256).rearrange("p (b i n) -> p b i n", b=4, i=2)
        sq = of_tmp(every, 1536, 640).rearrange("p (s h e) -> p s h e", s=2, e=HD)
        rot = of_tmp(every, 2176, 320).rearrange("p (h e) -> p h e", e=HD)
        swp = of_tmp(every, 2496, 320).rearrange("p (h e) -> p h e", e=HD)
        cosx = of_tmp(every, 2816, 320).rearrange("p (h e) -> p h e", e=HD)
        sinx = of_tmp(every, 3136, 320).rearrange("p (h e) -> p h e", e=HD)
        nrm = of_tmp(every, 3456, 160).rearrange("p (b h) -> p b h", b=4)
        qT3 = of_tmp(slice(0, DH), 0, 512).rearrange("p (s t) -> p s t", s=2)
        kT3 = of_tmp(slice(0, DH), 512, 512).rearrange("p (s t) -> p s t", s=2)
        v3 = of_tmp(every, 1024, 260).rearrange("p (s i n) -> p s i n", s=2, i=2)
        og3 = of_tmp(every, 1290, 256).rearrange("p (s i n) -> p s i n", s=2, i=2)
        decay = of_tmp(every, 1546, 768).rearrange("p (s n) -> p s n", s=2)
        weight = of_tmp(every, 2314, 768).rearrange("p (s n) -> p s n", s=2)
        h3 = of_tmp(every, 3082, 256).rearrange("p (s i n) -> p s i n", s=2, i=2)
        h3T = of_tmp(slice(0, DH), 3338, 512).rearrange("p (s t) -> p s t", s=2)
        den3 = of_tmp(every, 3850, 2)
        gate_row = slice(DH, DH + 1)
        zif = [of_tmp(gate_row, 512, 512), of_tmp(gate_row, 3338, 512)]
        cumf = of_tmp(gate_row, 3852, T)
        rowa = of_tmp(gate_row, 3852 + T, 2 * T).rearrange("p (s t) -> p s t", s=2)
        rowg = of_tmp(gate_row, 0, 2 * T).rearrange("p (s t) -> p s t", s=2)
        hid1 = of_tmp(every, 0, 4096).rearrange("p (s c n) -> p s c n", s=2, c=HC)
        one_row = sb("one_row", [P, T])[gate_row, :]
        zn = sb("zn", [P, 2, 2, P])
        gl = sb("gl", [P, NT, NE])
        top = sb("top", [P, NT, NE])
        topi = sb("topi", [P, NT, NE], U32)
        topf = sb("topf", [P, NT, 2])
        gex = sb("gex", [P, NT, 2])
        gtmp = sb("gtmp", [P, 2, NE])
        comb = sb("comb", [P, NT, NE])
        combT = sb("combT", [NE, T])

        def part(t, table, name):
            a, n = table[name]
            return t[:, a:a + n]

        ident = part(cst, CST, "ident")
        rowmask = part(cst, CST, "rowmask")
        bias = lambda name: part(row, ROW, name)
        both = lambda name: bias(name).unsqueeze(1).to_broadcast([P, 2, P])
        W = lambda name: part(wb, WB, name)
        W6 = lambda name: part(w64, W64, name)
        colv = lambda name, n=0: part(col, COL, name)[:, n:n + 1]
        tiles = lambda b: slice(2 * b, 2 * b + 2)
        toks = lambda b: slice(T * b, T * (b + 1))
        half = {0: 0, 1: 1, 2: 0, "2b": 0, 3: 1, "3b": 1, 4: 0, 6: 1}
        experts = lambda ap, e: ap.rearrange("p (m t) -> p m t", m=2)[:, :, e * 64:(e + 1) * 64]
        v0 = vst[:, :, 0:8, :].rearrange("p t (r j) n -> p t r j n", r=4)
        v4 = vst[:, :, :, :].rearrange("p t (j q r) n -> p t j q r n", j=2, q=2)

        misc_done = [sem(f"misc_done{s}") for s in range(2)]
        score_done = [sem(f"score_done{s}") for s in range(2)]
        prob_used = [sem(f"prob_used{s}") for s in range(HELD["prob"])]
        out_copied = [sem(f"out_copied{s}") for s in range(2)]
        misc_full, score_full = sem("misc_full"), sem("score_full")

        def misc_written(eng, key):
            eng.wait_ge(misc_done[MISC.slot(key)], MISC.done(key))

        def score_written(eng, key):
            eng.wait_ge(score_done[SC.slot(key)], SC.done(key))

        def after_scalar(eng, key):
            eng.wait_ge(misc_done[MISC.slot(key)], MISC.before(key) + 1)

        def read_by_tensor(eng, pool, holder):
            step = SLOTS[pool].before(holder)
            if step is not None:
                if step in MISC.at:
                    eng.wait_ge(misc_full, MISC.full(step))
                else:
                    eng.wait_ge(score_full, SC.full(step))

        def slot(pool, holder):
            return SLOTS[pool].slot(holder)

        def psum_misc(key):
            return misc[:, MISC.slot(key), :]

        def psum_scores(key):
            return scores[:, SC.slot(key), :]

        def biased(step):
            return sum(1 for s in ORDER[:INDEX[step] + 1]
                       if s[0] == "lnb" and s[1] in (1, 4) or s[:2] == ("lna", "3b"))

        two = lambda ap: ap.rearrange("p (i n) -> p i n", i=2)
        STACKS = ("ropeb", "kck", "q1", "q4", "k4", "qc4")

        block = ctx.enter_context(nc.Block())

        @block.sync
        def _(sp):
            xin = d["x"].rearrange("b (i p) n -> p (b i) n", p=P)
            sp.dma_start(x[:, tiles(0), :], xin[:, tiles(0), :]).then_inc(sem("x_loaded0"), 16)
            sp.dma_start(cst[:, :], d["cst"]).then_inc(sem("cst_loaded"), 16)
            for b in range(1, NB):
                sp.dma_start(x[:, tiles(b), :], xin[:, tiles(b), :]).then_inc(sem(f"x_loaded{b}"), 16)
            sp.dma_start(wa[:, :], d["wa"]).then_inc(sem("wa_loaded"), 16)
            sp.dma_start(w64[:, :], d["w64"]).then_inc(sem("w64_loaded"), 16)
            sp.dma_start(row[:, :], d["row"].to_broadcast([P, ROW["all"][1]])).then_inc(
                sem("row_loaded"), 16)
            sp.dma_start(wb[:, :], d["wb"]).then_inc(sem("wb_loaded"), 16)
            sp.dma_start(col[:, :], d["col"]).then_inc(sem("col_loaded"), 16)
            sp.dma_start(gate_bias[gate_row, :], d["gate_bias"]).then_inc(sem("gate_bias_loaded"), 16)
            sp.dma_start(b2m[:, :], d["b2m"]).then_inc(sem("b2m_loaded"), 16)
            for h in range(2):
                es = slice(4 * h, 4 * h + 4)
                sp.dma_start(w1[:, es, :], d["w1a"][:, es, :]).then_inc(sem(f"w1a_loaded{h}"), 16)
                sp.dma_start(w2[:, es, :, :], d["w2a"][:, es, :, :]).then_inc(sem(f"w2a_loaded{h}"), 16)
            for h in range(2):
                for j in (2 * h, 2 * h + 1):
                    sp.wait_ge(misc_full, MISC.full(("fdown", j)))
                es = slice(4 * h, 4 * h + 4)
                sp.dma_start(w1[:, es, :], d["w1b"][:, es, :]).then_inc(sem(f"w1b_loaded{h}"), 16)
                sp.dma_start(w2[:, es, :, :], d["w2b"][:, es, :, :]).then_inc(sem(f"w2b_loaded{h}"), 16)
            outv = out.rearrange("b (i p) n -> p (b i) n", p=P)
            for h in range(2):
                misc_written(sp, ("mdown", h, NE - 1))
                for b in PAIRS[h]:
                    sp.dma_start(outv[:, tiles(b), :], x[:, tiles(b), :]).then_inc(sem("stored"), 16)
            sp.wait_ge(sem("stored"), 16 * NB)

        @block.gpsimd
        def _(pool):
            g = nc.gpsimd
            counts = {}

            def then(ins, name="pool_step"):
                counts[name] = counts.get(name, 0) + 1
                ins.then_inc(sem(name), 1)
                pool.wait_ge(sem(name), counts[name])

            then(g.memset(neg_half[:, :], -0.5))
            then(g.memset(one_row, 1.0))
            then(g.memset(vst[:, :, :, :], 0.0))
            for jj in range(2):
                a = 16 * jj + 8
                then(g.memset(v0[:, :, :, jj, a:a + 8], 1.0))
            pool.wait_ge(sem("cst_loaded"), 16)
            for table, name in ((cosx, "cos"), (sinx, "sin")):
                for i in range(2):
                    src = part(cst, CST, name)[:, i * HD:(i + 1) * HD].unsqueeze(1)
                    then(g.tensor_copy(table[:, 20 * i:20 * i + 20, :], src.to_broadcast([P, 20, HD])),
                         "rope_tables")

            for step in ORDER:
                kind, b = step[0], step[-1]
                if kind == "lna":
                    s = step[1]
                    h = half[s]
                    pool.wait_ge(sem("var_ready"), count(("lna",), step))
                    m, v, r = mv[:, h, tiles(b), 0], mv[:, h, tiles(b), 1], rstd[:, h, tiles(b)]
                    if s == "3b":
                        then(g.tensor_tensor(m, m, m, ALU.mult))
                        then(g.tensor_tensor(v, v, m, ALU.add))
                    then(g.tensor_scalar(r, v, 1e-6 if s == "3b" else 1e-5, None, ALU.add))
                    then(g.tensor_tensor(r, r, neg_half[:, :], ALU.pow), "rstd_ready")
                    if s == "3b":
                        then(g.tensor_tensor(x[:, tiles(b), :], x[:, tiles(b), :],
                                             xn[:, h, tiles(b), :], ALU.add), "x_biased")
                elif kind == "lnb" and step[1] in (1, 4):
                    pool.wait_ge(sem("xn_ready"), count(("lnb",), step))
                    pool.wait_ge(sem("row_loaded"), 16)
                    then(g.tensor_tensor(x[:, tiles(b), :], x[:, tiles(b), :],
                                         both({1: "bo1", 4: "bp4"}[step[1]]), ALU.add), "x_biased")
                elif kind == "ropeb":
                    misc_written(pool, ("qkv", b))
                    for i in range(2):
                        for jj in range(2):
                            v = rawv[:, b, i, :].rearrange("p (r e) -> p r e", e=HD)
                            then(g.tensor_copy(v0[:, 2 * b + i, :, jj, 16 * jj:16 * jj + HD], v),
                                 "v0_ready")
                    pool.wait_ge(sem("rope_done"), count(("ropeb",), step))
                    read_by_tensor(pool, "stack_k", (0, b))
                    k = kn[:, slot("stack_k", (0, b)), :, 0:4, :]
                    rk = rot.rearrange("p (i h) e -> p i h e", i=2)[:, :, 16:20, :]
                    then(g.tensor_copy(k[:, :, :, 0:8], rk))
                    then(g.tensor_tensor(k[:, :, :, 16:24], rk, k[:, :, :, 0:8], ALU.subtract))
                    then(g.tensor_copy(k[:, :, :, 8:16], k[:, :, :, 0:8]))
                    then(g.tensor_copy(k[:, :, :, 24:32], k[:, :, :, 16:24]), "k0_ready")
                elif kind == "sc" and step[1] == 0:
                    score_written(pool, step)
                    key = ("pv",) + step[1:]
                    n = 8 if SELF_CHUNKS[step[3]][0] == "k1" else 4
                    v = probs[:, slot("prob", key), :].rearrange("p (h t) -> p h t", h=n)[:, :, 0:P]
                    then(g.affine_select(out=v, in_=v, compare_op=ALU.is_ge, fill=0.0, base=0,
                                         pattern=[[0, n], [1, P]], channel_multiplier=-1),
                         "prob_masked")
                elif kind == "presets1":
                    then(g.memset(vc[:, :, :, :, :, :], 0.0))
                    for rows, a in ((slice(0, 64), 8), (slice(64, 128), 24)):
                        for l in range(2):
                            then(g.memset(vc[rows, l, :, :, :, a:a + 8].rearrange(
                                "p b j r n -> p (b j r) n"), 1.0), "vc_presets")
                elif kind == "presets4":
                    for c in range(CHUNKS[0]):
                        key = ("pv", 0, b, c)
                        pool.wait_ge(prob_used[slot("prob", key)], SLOTS["prob"].turn(key) + 1)
                    then(g.memset(vst[:, tiles(b), :, :], 0.0))
                    for jj in range(2):
                        for t in (2 * b, 2 * b + 1):
                            a = 16 * jj + 8
                            then(g.memset(v4[:, t, :, jj, :, a:a + 8], 1.0), "presets4")

        @block.scalar
        def _(act):
            a = nc.scalar
            counts = {}

            def then(ins, name="act_step"):
                counts[name] = counts.get(name, 0) + 1
                ins.then_inc(sem(name), 1)
                act.wait_ge(sem(name), counts[name])

            def evac(key, out_ap, in_ap, scale=1.0):
                act.wait_ge(misc_full, MISC.full(key))
                func = ACT.Copy if isinstance(scale, float) else ACT.Identity
                a.activation(out_ap, in_ap, func, scale=scale).then_inc(misc_done[MISC.slot(key)], 1)

            def stack_evac(step, dst):
                act.wait_ge(misc_full, MISC.full(step))
                src = misc16[MISC.slot(step)].rearrange("p (i g t) -> p i g t", i=2, g=4)
                a.activation(dst[:, :, 0:P], src[:, 0], ACT.Copy).then_inc(sem("stack_half"), 1)
                a.activation(dst[:, :, P:T], src[:, 1], ACT.Copy).then_inc(
                    misc_done[MISC.slot(step)], 1)

            for step in ORDER:
                kind, b = step[0], step[-1]
                if kind == "tr":
                    evac(step, xnT[:, half[step[1]], toks(b)], psum_misc(step)[:, 0:T])
                elif kind == "qkv":
                    act.wait_ge(misc_full, MISC.full(step))
                    src = two(psum_misc(step)[:, 0:384])
                    a.activation(two(raw[:, b, :, :].rearrange("p h e -> p (h e)")), src[:, :, 0:160],
                                 ACT.Copy).then_inc(sem("raw_ready"), 1)
                    a.activation(rawv[:, b, :, :], src[:, :, 160:192], ACT.Copy).then_inc(
                        misc_done[MISC.slot(step)], 1)
                elif kind == "ropea":
                    act.wait_ge(sem("raw_ready"), count(("qkv",), ("qkv", b)))
                    last = SLOTS["rope"].before(b)
                    if last is not None:
                        act.wait_ge(sem("rope_done"), count(("ropeb",), last))
                    then(a.activation(sq[:, slot("rope", b)], raw[:, b], ACT.Square), "squares_ready")
                    act.wait_ge(sem("sums_ready"), count(("ropea",), step))
                    then(a.activation(nrm[:, b, :], nrm[:, b, :], ACT.Sqrt), "norms_ready")
                elif kind == "tq0":
                    _, b, i = step
                    evac(step, qT[:, :, (2 * b + i) * P:(2 * b + i + 1) * P],
                         misc16[MISC.slot(step)][:, 0:512].rearrange("p (g t) -> p g t", g=4))
                elif kind in ("tq", "tqm"):
                    if step[1] == 5:
                        read_by_tensor(act, "qcT", b)
                        stack_evac(step, qcT[:, slot("qcT", b)])
                    else:
                        stack_evac(step, qT[:, :, toks(b)])
                elif kind == "tk4":
                    n = count(("tk4",), step)
                    if n > 1:
                        act.wait_ge(sem("km4_ready"), 4 * (n - 1))
                    stack_evac(step, kT[:, :, :])
                elif kind == "sc":
                    key = ("pv",) + step[1:]
                    act.wait_ge(score_full, SC.full(step))
                    if SLOTS["prob"].turn(key):
                        act.wait_ge(prob_used[slot("prob", key)], SLOTS["prob"].turn(key))
                    a.activation(probs[:, slot("prob", key), :], psum_scores(step), ACT.Exp,
                                 scale=SCALE).then_inc(score_done[SC.slot(step)], 1)
                elif kind == "oc":
                    _, s, b = step
                    read_by_tensor(act, "copied", (s, b))
                    key = ("pv", s, b, CHUNKS[s] - 1)
                    act.wait_ge(prob_used[slot("prob", key)], SLOTS["prob"].turn(key) + 1)
                    a.activation(copied[:, slot("copied", (s, b)), :], outs[:, slot("out", (s, b)), :],
                                 ACT.Copy).then_inc(out_copied[slot("out", (s, b))], 1)
                elif kind == "ou":
                    _, s, b = step
                    read_by_tensor(act, "yT", (s, b))
                    evac(step, yT[:, slot("yT", (s, b)), :], psum_misc(step)[:, 0:T])
                elif kind == "tr2":
                    evac(step, flatT[:, toks(b)], psum_misc(step)[:, 0:T])
                elif kind == "fup":
                    read_by_tensor(act, "hid0", b)
                    act.wait_ge(score_full, SC.full(step))
                    act.wait_ge(sem("col_loaded"), 16)
                    for n in range(2 * HC):
                        e, c = 2 * step[1] + n // HC, n % HC
                        a.activation(hid0[:, slot("hid0", b), n * P:(n + 1) * P],
                                     psum_scores(step)[:, n * P:(n + 1) * P],
                                     ACT.Gelu, bias=colv("b1", e * HC + c)).then_inc(
                            sem("gelu_part") if n < 2 * HC - 1 else score_done[SC.slot(step)], 1)
                elif kind == "nxa":
                    misc_written(act, step)
                    z = zn[:, slot("zn", b)]
                    then(a.activation(z, z, ACT.Gelu), "gelu_ready")
                elif kind == "tr3":
                    evac(step, xnT[:, 1, toks(b)], psum_misc(step)[:, 0:T], colv("norm_w"))
                elif kind == "p3a":
                    read_by_tensor(act, "mlstm", b)
                    evac(step, qT3[:, slot("mlstm", b), :], psum_misc(step)[0:DH, 0:T], 1.0 / DH)
                elif kind == "p3b":
                    w = slot("mlstm", b)
                    evac(step, v3[:, w, :, 0:DH], two(psum_misc(step)[:, 0:T])[:, :, 0:DH])
                    misc_written(act, step)
                    then(a.activation(og3[:, w], og3[:, w], ACT.Exp, scale=-1.0), "og_exp")
                elif kind == "ml" and step[2] == 0:
                    act.wait_ge(score_full, SC.full(step))
                    then(a.activation(decay[:, slot("mlstm", step[1]), :], psum_scores(step)[:, 0:384],
                                      ACT.Exp), "decay_ready")
                elif kind == "ml" and step[2] == 2:
                    evac(step, h3T[:, slot("mlstm", step[1]), :], psum_misc(step)[0:DH, 0:T])
                elif kind == "ga":
                    act.wait_ge(sem("gate_diff"), count(("ga",), step))
                    then(a.activation(gex[:, tiles(b), 0], gex[:, tiles(b), 0], ACT.Exp), "gate_exp")
                elif kind == "mup":
                    _, h, e, n = step
                    act.wait_ge(sem("col_loaded"), 16)
                    if n == 0:
                        read_by_tensor(act, "hidden", (h, e))
                    act.wait_ge(score_full, SC.full(step))
                    a.activation(hid1[:, slot("hidden", (h, e)), 2 * n, :], psum_scores(step)[:, 0:512],
                                 ACT.Relu, bias=colv("b1m", e * HC + 2 * n)).then_inc(
                        score_done[SC.slot(step)], 1)

        @block.vector
        def _(dve):
            v = nc.vector
            counts = {}

            def then(ins, name="dve_step", wait=True):
                counts[name] = counts.get(name, 0) + 1
                ins.then_inc(sem(name), 1)
                if wait:
                    dve.wait_ge(sem(name), counts[name])

            def gives(key, ins):
                ins.then_inc(misc_done[MISC.slot(key)], 1)
                misc_written(dve, key)

            def gives_scores(key, ins):
                ins.then_inc(score_done[SC.slot(key)], 1)
                score_written(dve, key)

            def biased_operand(key, name):
                dve.wait_ge(misc_full, MISC.full(key))
                dve.wait_ge(sem("row_loaded"), 16)
                gives(key, v.tensor_tensor(split[:, :, :], two(psum_misc(key)[:, 0:T]), both(name),
                                           ALU.add))
                return split[:, :, :].rearrange("p i (h e) -> p (i h) e", e=HD)

            def query_stack(dst, key, name):
                q = dst.rearrange("p i h n -> p (i h) n")
                then(v.memset(q[:, :, 24:32], 0.0), wait=False)
                s = biased_operand(key, name)
                then(v.tensor_copy(q[:, :, 0:8], s))
                then(v.tensor_tensor(q[:, :, 8:16], s, q[:, :, 0:8], ALU.subtract), wait=False)
                then(v.tensor_copy(q[:, :, 16:24], q[:, :, 0:8]), "stack_ready")

            def key_stack(dst, key, name):
                q = dst.rearrange("p i h n -> p (i h) n")
                then(v.memset(q[:, :, 26:32], 0.0), wait=False)
                then(v.memset(q[:, :, 24:26], MAXDIV), wait=False)
                s = biased_operand(key, name)
                then(v.tensor_copy(q[:, :, 0:8], s))
                then(v.tensor_tensor(q[:, :, 16:24], s, q[:, :, 0:8], ALU.subtract), wait=False)
                then(v.tensor_copy(q[:, :, 8:16], q[:, :, 0:8]), "stack_ready")

            dve.wait_ge(sem("cst_loaded"), 16)
            then(v.tensor_copy(ident16[:, :], ident), wait=False)
            then(v.tensor_copy(identb[:, :], ident), wait=False)
            for name, dst in (("causal_nat", causal_nat), ("causal_tr", causal_tr)):
                then(v.tensor_copy(dst[:, :], part(cst, CST, name)), "masks_ready")

            source = {0: x, 1: x, 2: x, 3: x, 4: x, 6: x, "2b": xn[:, 0], "3b": xn[:, 1]}

            for step in ORDER:
                kind, b = step[0], step[-1]
                if kind == "lna":
                    s = step[1]
                    h, src = half[s], source[s]
                    if s == 0:
                        dve.wait_ge(sem(f"x_loaded{b}"), 16)
                    t0, t1 = 2 * b, 2 * b + 1
                    then(v.bn_stats(stat[:, h, t0, :], src[:, t0, :]), wait=False)
                    then(v.bn_stats(stat[:, h, t1, :], src[:, t1, :]))
                    then(v.bn_aggr(mv[:, h, t0, :], stat[:, h, t0, :]), wait=False)
                    then(v.bn_aggr(mv[:, h, t1, :], stat[:, h, t1, :]), "var_ready")
                elif kind == "lnb":
                    s = step[1]
                    h, src = half[s], source[s]
                    dst = xn[:, 1 - h if s in ("2b", "3b") else h]
                    dve.wait_ge(sem("rstd_ready"), count(("lna",), ("lna", s, b)))
                    for t in (2 * b, 2 * b + 1):
                        r = rstd[:, h, t:t + 1]
                        if s == "3b":
                            ins = v.tensor_scalar(dst[:, t, :], src[:, t, :], r, None, ALU.mult)
                        else:
                            ins = v.tensor_scalar(dst[:, t, :], src[:, t, :], mv[:, h, t, 0:1], r,
                                                  ALU.subtract, ALU.mult)
                        then(ins, "xn_ready" if t % 2 else "dve_step", wait=t % 2 == 1)
                elif kind == "ropea":
                    dve.wait_ge(sem("squares_ready"), count(("ropea",), step))
                    then(v.tensor_reduce(nrm[:, b, :], sq[:, slot("rope", b)], X, ALU.add), "sums_ready")
                elif kind == "ropeb":
                    dve.wait_ge(sem("norms_ready"), count(("ropea",), ("ropea", b)))
                    dve.wait_ge(sem("rope_tables"), 4)
                    s = sq[:, slot("rope", b)]
                    then(v.tensor_scalar(nrm[:, b, :], nrm[:, b, :], 1e-10, None, ALU.add))
                    then(v.reciprocal(nrm[:, b, :], nrm[:, b, :]))
                    then(v.tensor_tensor(s, raw[:, b], nrm[:, b, :].unsqueeze(2).to_broadcast([P, 40, HD]),
                                         ALU.mult))
                    n = count(("ropeb",), step)
                    if n > 1:
                        dve.wait_ge(sem("k0_ready"), n - 1)
                    then(v.tensor_tensor(rot, s, cosx, ALU.mult), wait=False)
                    then(v.tensor_tensor(swp[:, :, 0:4], s[:, :, 4:8], sinx[:, :, 0:4], ALU.mult), wait=False)
                    then(v.tensor_tensor(swp[:, :, 4:8], s[:, :, 0:4], sinx[:, :, 4:8], ALU.mult))
                    then(v.tensor_tensor(rot, rot, swp, ALU.add), "rope_done")
                    read_by_tensor(dve, "stack_q", (0, b))
                    q = qn[:, slot("stack_q", (0, b))]
                    rq = rot.rearrange("p (i h) e -> p i h e", i=2)[:, :, 0:16, :]
                    then(v.tensor_copy(q[:, :, :, 0:8], rq))
                    then(v.tensor_tensor(q[:, :, :, 8:16], rq, q[:, :, :, 0:8], ALU.subtract))
                    then(v.tensor_copy(q[:, :, :, 16:32], q[:, :, :, 0:16]), "stack_ready")
                elif kind == "tq0":
                    _, b, i = step
                    t = 2 * b + i
                    after_scalar(dve, step)
                    m = misc16[MISC.slot(step)][:, 512:640].unsqueeze(1).to_broadcast([P, 4, P])
                    v.tensor_tensor(km0[:, :, t * P:(t + 1) * P], m,
                                    rowmask.unsqueeze(2).to_broadcast([P, 4, P]), ALU.mult)\
                        .then_inc(misc_done[MISC.slot(step)], 1)
                elif kind == "kck":
                    l = b
                    read_by_tensor(dve, "stack_k", ("context", l))
                    key_stack(kn[:, slot("stack_k", ("context", l))], step, {1: "bk1", 4: "bck4"}[l])
                elif kind == "kcv":
                    l = b
                    dve.wait_ge(misc_full, MISC.full(step))
                    dve.wait_ge(sem("row_loaded"), 16)
                    dve.wait_ge(sem("vc_presets"), 4)
                    bv = bias({1: "bv1", 4: "bcv4"}[l])
                    for n, rows in enumerate((slice(0, 64), slice(64, 128))):
                        for m in range(NB):
                            sel = lambda ap: ap.rearrange("p (j q r e) -> p j q r e", j=2, q=2, r=4)[:, :, n]
                            ins = v.tensor_tensor(vc[rows, l // 4, m, :, :, 16 * n:16 * n + HD],
                                                  sel(psum_misc(step)[rows, m * P:(m + 1) * P]),
                                                  sel(bv[rows, :]), ALU.add)
                            if (n, m) == (1, NB - 1):
                                gives(step, ins)
                            else:
                                then(ins, wait=False)
                elif kind == "kct":
                    dve.wait_ge(misc_full, MISC.full(step))
                    m = misc16[MISC.slot(step)].rearrange("p (i g t) -> p i g t", i=2, g=4)
                    for i in range(2):
                        for r in range(4):
                            ins = v.tensor_scalar(kcm[:, r, :, i * P:(i + 1) * P], m[:, i],
                                                  rowmask[:, r:r + 1], None, ALU.mult)
                            if (i, r) == (1, 3):
                                gives(step, ins)
                            else:
                                then(ins, wait=False)
                elif kind == "ot":
                    _, s, b = step
                    dve.wait_ge(misc_full, MISC.full(step))
                    ps = psum_misc(step).rearrange("p (h n) -> p h n", n=16)
                    then(v.reciprocal(sums[:, :], ps[:, :, HD]))
                    if s == 4:
                        dst = y4[:, slot("y4", b)]
                    else:
                        read_by_tensor(dve, "y", (s, b))
                        dst = y[:, slot("y", (s, b))]
                    gives(step, v.tensor_tensor(
                        dst.rearrange("p i (h e) -> p (i h) e", e=HD), ps[:, :, 0:HD],
                        sums[:, :].unsqueeze(2).to_broadcast([P, 2 * H, HD]), ALU.mult))
                    if s == 5:
                        then(v.tensor_tensor(dst, dst, y4[:, slot("y4", b)], ALU.add), "y_added")
                elif kind == "op" or kind == "ml" and step[2] == 3:
                    b = step[2] if kind == "op" else step[1]
                    dve.wait_ge(misc_full, MISC.full(step))
                    before = {("op", 1): ("lnb", 1, b), ("op", 5): ("lnb", 4, b),
                              ("ml", b): ("lna", "3b", b)}.get(step[:2])
                    if before:
                        dve.wait_ge(sem("x_biased"), biased(before))
                    gives(step, v.tensor_tensor(x[:, tiles(b), :], x[:, tiles(b), :],
                                                two(psum_misc(step)[:, 0:T]), ALU.add))
                elif kind == "q1":
                    read_by_tensor(dve, "stack_q", (1, b))
                    query_stack(qn[:, slot("stack_q", (1, b))], step, "bq1")
                elif kind == "q4":
                    read_by_tensor(dve, "stack_q", (4, b))
                    query_stack(qn[:, slot("stack_q", (4, b))], step, "bq4")
                elif kind == "qc4":
                    read_by_tensor(dve, "stack_c", (5, b))
                    query_stack(qcn[:, slot("stack_c", (5, b))], step, "bcq4")
                elif kind == "k4":
                    read_by_tensor(dve, "stack_k", (4, b))
                    key_stack(kn[:, slot("stack_k", (4, b))], step, "bk4")
                elif kind == "tk4":
                    misc_written(dve, step)
                    read_by_tensor(dve, "km4", b)
                    for r in range(4):
                        then(v.tensor_scalar(km4[:, slot("km4", b), r, :, :], kT[:, :, :],
                                             rowmask[:, r:r + 1], None, ALU.mult), "km4_ready",
                             wait=False)
                elif kind == "v4":
                    dve.wait_ge(misc_full, MISC.full(step))
                    dve.wait_ge(sem("presets4"), 4 * count(("presets4",), ("presets4", b)))
                    for i in range(2):
                        for jj in range(2):
                            sel = lambda ap: ap.rearrange("p (j q r e) -> p j q r e", j=2, q=2, r=4)[:, :, jj]
                            ins = v.tensor_tensor(v4[:, 2 * b + i, :, jj, :, 16 * jj:16 * jj + HD],
                                                  sel(psum_misc(step)[:, i * P:(i + 1) * P]),
                                                  sel(bias("bv4")), ALU.add)
                            if i == jj == 1:
                                gives(step, ins)
                            else:
                                then(ins, wait=False)
                elif kind == "mxc":
                    _, s, b, i = step
                    dve.wait_ge(score_full, SC.full(step))
                    gives_scores(step, v.tensor_reduce(
                        mxc[:, slot("mxc", (s, b)), i, :],
                        psum_scores(step).rearrange("p (h k) -> p h k", k=KV), X, ALU.max))
                elif kind == "mxs":
                    _, b, c = step
                    dve.wait_ge(score_full, SC.full(step))
                    w = slot("mx", b)
                    if c < 2:
                        dst, k = mx[:, w, 0, 8 * c:8 * c + 8], P
                    else:
                        dst, k = mx[:, w, 1, 4 * (c - 2):4 * (c - 2) + 4], T
                    gives_scores(step, v.tensor_reduce(
                        dst, psum_scores(step).rearrange("p (h k) -> p h k", k=k), X, ALU.max))
                elif kind == "mxe":
                    _, s, b = step
                    m = mx[:, slot("mx", b)] if s == 4 else mxc[:, slot("mxc", (s, b))]
                    m = m.rearrange("p i h -> p (i h)")
                    q = qcn[:, slot("stack_c", (5, b))] if s == 5 else qn[:, slot("stack_q", (s, b))]
                    q = q.rearrange("p i h n -> p (i h) n")
                    then(v.tensor_scalar(m, m, -1.0 / MAXDIV, None, ALU.mult))
                    then(v.tensor_copy(q[:, :, 24], m))
                    then(v.tensor_tensor(q[:, :, 25], m, q[:, :, 24], ALU.subtract), "max_ready")
                elif kind == "tr2":
                    after_scalar(dve, step)
                    dve.wait_ge(sem("col_loaded"), 16)
                    gives(step, v.tensor_scalar(n2T[:, toks(b)], psum_misc(step)[:, T:2 * T],
                                                colv("ln_scale"), colv("ln_bias"), ALU.mult, ALU.add))
                elif kind == "xa":
                    dve.wait_ge(misc_full, MISC.full(step))
                    gives(step, v.scalar_tensor_tensor(xaT[:, toks(b)], psum_misc(step)[:, 0:T],
                                                       colv("attn_b"), flatT[:, toks(b)],
                                                       ALU.add, ALU.add))
                elif kind == "fdown":
                    dve.wait_ge(misc_full, MISC.full(step))
                    for n in range(2):
                        e = 2 * step[1] + n
                        ins = v.tensor_scalar(experts(eoT, e), psum_misc(step)[:, n * P:(n + 1) * P]
                                              .rearrange("p (m t) -> p m t", m=2),
                                              colv("b2", e), None, ALU.add)
                        if n == 0:
                            then(ins, wait=False)
                        else:
                            gives(step, ins)
                elif kind == "nxa":
                    dve.wait_ge(misc_full, MISC.full(step))
                    gives(step, v.tensor_tensor(zn[:, slot("zn", b)], two(psum_misc(step)[:, 0:T]),
                                                both("next_b"), ALU.add))
                elif kind == "nxb":
                    dve.wait_ge(sem("gelu_ready"), count(("nxa",), ("nxa", b)))
                    then(v.tensor_tensor(x[:, tiles(b), :], x[:, tiles(b), :], zn[:, slot("zn", b)],
                                         ALU.add))
                elif kind == "p3a":
                    read_by_tensor(dve, "mlstm", b)
                    after_scalar(dve, step)
                    dve.wait_ge(sem("gate_bias_loaded"), 16)
                    w, ps = slot("mlstm", b), psum_misc(step)
                    for n in range(2):
                        then(v.tensor_scalar(zif[w][:, n * T:(n + 1) * T], ps[gate_row, n * T:(n + 1) * T],
                                             gate_bias[gate_row, n:n + 1], None, ALU.add), wait=False)
                    gives(step, v.tensor_copy(kT3[:, w, :], ps[0:DH, T:2 * T]))
                elif kind == "p3b":
                    w = slot("mlstm", b)
                    then(v.memset(v3[:, w, :, DH:DH + 1], 1.0), "v3_ones", wait=False)
                    after_scalar(dve, step)
                    gives(step, v.tensor_tensor(og3[:, w], two(psum_misc(step)[:, 0:T])[:, :, DH:2 * DH],
                                                bias("bo3").unsqueeze(1).to_broadcast([P, 2, DH]),
                                                ALU.add))
                elif kind == "rows":
                    dve.wait_ge(sem("rope_tables"), 4)
                    w = slot("mlstm", b)
                    zi, zf = zif[w][:, 0:T], zif[w][:, T:2 * T]
                    then(v.tensor_tensor_scan(cumf, one_row, zf, 0.0, ALU.mult, ALU.add))
                    then(v.tensor_tensor(rowa[:, w, :], zi, cumf, ALU.subtract))
                    then(v.tensor_tensor_scan(cumf, rowa[:, w, :], rowa[:, w, :], -3.0e38,
                                              ALU.max, ALU.max))
                    then(v.tensor_scalar(rowg[:, w, :], cumf, -1.0, None, ALU.mult), "rows_ready")
                elif kind == "ml" and step[2] == 0:
                    b = step[1]
                    w = slot("mlstm", b)
                    dve.wait_ge(sem("decay_ready"), sum(
                        1 for s in ORDER[:INDEX[step] + 1] if s[0] == "ml" and s[2] == 0))
                    gives_scores(step, v.tensor_tensor(weight[:, w, :], decay[:, w, :],
                                                       psum_scores(step)[:, 512:896], ALU.mult))
                elif kind == "ml" and step[2] == 1:
                    b = step[1]
                    w = slot("mlstm", b)
                    dve.wait_ge(sem("og_exp"), count(("p3b",), ("p3b", b)))
                    o = og3[:, w]
                    then(v.tensor_scalar(o, o, 1.0, None, ALU.add))
                    then(v.reciprocal(o, o), wait=False)
                    dve.wait_ge(misc_full, MISC.full(step))
                    ps = psum_misc(step)[:, 0:2 * (DH + 1)].rearrange("p (i n) -> p i n", i=2)
                    then(v.tensor_scalar(den3, ps[:, :, DH], -1.0, None, ALU.mult))
                    then(v.tensor_tensor(den3, den3, ps[:, :, DH], ALU.max))
                    then(v.tensor_scalar(den3, den3, 1.0, None, ALU.max))
                    then(v.reciprocal(den3, den3))
                    for i in range(2):
                        ins = v.scalar_tensor_tensor(h3[:, w, i, :], ps[:, i, 0:DH], den3[:, i:i + 1],
                                                     og3[:, w, i, :], ALU.mult, ALU.mult)
                        if i == 0:
                            then(ins, wait=False)
                        else:
                            gives(step, ins)
                elif kind == "ga":
                    dve.wait_ge(misc_full, MISC.full(step))
                    gives(step, v.tensor_copy(gl[:, tiles(b), :], two(psum_misc(step)[:, 0:2 * NE])))
                    t0, t1 = 2 * b, 2 * b + 1
                    then(v.max(top[:, t0, :], gl[:, t0, :]), wait=False)
                    then(v.max(top[:, t1, :], gl[:, t1, :]))
                    then(v.tensor_tensor(gex[:, tiles(b), 0], top[:, tiles(b), 1], top[:, tiles(b), 0],
                                         ALU.subtract), "gate_diff", wait=False)
                    then(v.max_index(topi[:, t0, :], top[:, t0, :], gl[:, t0, :]), wait=False)
                    then(v.max_index(topi[:, t1, :], top[:, t1, :], gl[:, t1, :]))
                    then(v.tensor_copy(topf[:, tiles(b), :], topi[:, tiles(b), 0:2]))
                elif kind == "gb":
                    dve.wait_ge(sem("gate_exp"), count(("ga",), ("ga", b)))
                    e, w = gex[:, tiles(b), 0], gex[:, tiles(b), 1]
                    then(v.tensor_scalar(w, e, 1.0, None, ALU.add))
                    then(v.reciprocal(w, w))
                    then(v.tensor_tensor(e, e, w, ALU.mult))
                    iota = part(cst, CST, "iota")
                    for i in range(2):
                        t = 2 * b + i
                        then(v.tensor_scalar(comb[:, t, :], iota, topf[:, t, 0:1], gex[:, t, 1:2],
                                             ALU.is_equal, ALU.mult), wait=False)
                        then(v.tensor_scalar(gtmp[:, i, :], iota, topf[:, t, 1:2], gex[:, t, 0:1],
                                             ALU.is_equal, ALU.mult), wait=i == 1)
                    then(v.tensor_tensor(comb[:, tiles(b), :], comb[:, tiles(b), :], gtmp[:, :, :],
                                         ALU.add), "comb_ready")
                elif kind == "gc":
                    dve.wait_ge(misc_full, MISC.full(step))
                    read_by_tensor(dve, "combT", b)
                    gives(step, v.tensor_copy(combT[:, :], psum_misc(step)[0:NE, 0:T]))
                elif kind == "gd":
                    dve.wait_ge(misc_full, MISC.full(step))
                    gives(step, v.tensor_tensor(x[:, tiles(b), :], x[:, tiles(b), :],
                                                two(psum_misc(step)[:, 0:T]), ALU.add))
                elif kind == "mup":
                    _, h, e, n = step
                    dve.wait_ge(sem("col_loaded"), 16)
                    if n == 0:
                        read_by_tensor(dve, "hidden", (h, e))
                    dve.wait_ge(score_full, SC.full(step))
                    c = 2 * n + 1
                    v.tensor_scalar(hid1[:, slot("hidden", (h, e)), c, :], psum_scores(step)[:, 512:1024],
                                    colv("b1m", e * HC + c), 0.0, ALU.add, ALU.max).then_inc(
                        score_done[SC.slot(step)], 1)
                elif kind == "mdown":
                    _, h, e = step
                    dve.wait_ge(misc_full, MISC.full(step))
                    for i in range(4):
                        t = 2 * PAIRS[h][i // 2] + i % 2
                        ins = v.scalar_tensor_tensor(x[:, t, :], psum_misc(step)[:, i * P:(i + 1) * P],
                                                     comb[:, t, e:e + 1], x[:, t, :], ALU.mult, ALU.add)
                        if i < 3:
                            then(ins, wait=False)
                        else:
                            gives(step, ins)

        @block.tensor
        def _(pe):
            mm = nc.tensor.matmul

            def take_misc(key):
                if MISC.before(key):
                    pe.wait_ge(misc_done[MISC.slot(key)], MISC.before(key))
                return psum_misc(key)

            def take_scores(key):
                if SC.before(key):
                    pe.wait_ge(score_done[SC.slot(key)], SC.before(key))
                return psum_scores(key)

            def transposes(dst, blocks, identity):
                for n, blk in enumerate(blocks):
                    ins = nc.tensor.transpose(dst[:, n * P:(n + 1) * P], blk, identity)
                ins.then_inc(misc_full, 1)

            def natural(key, lhsTs, rhs):
                dst = take_misc(key)
                n = rhs.shape[-1]
                for i, l in enumerate(lhsTs):
                    ins = mm(dst[:, i * n:(i + 1) * n], l, rhs, start=True, stop=True)
                ins.then_inc(misc_full, 1)

            tile_cols = lambda ap, b: [ap[:, (2 * b + i) * P:(2 * b + i + 1) * P] for i in range(2)]

            def stacked(step, buf, made):
                pe.wait_ge(sem("stack_ready"), count(STACKS, made))
                take_misc(step)
                transposes(misc16[MISC.slot(step)],
                           [buf[:, i, 4 * B:4 * B + 4, :].rearrange("p h n -> p (h n)")
                            for i in range(2) for B in range(4)], ident16[:, :])

            masks = lambda m, n: m[:, :].unsqueeze(1).to_broadcast([P, n, P])

            def self_scores(step):
                _, s, b, c = step
                kind, n = SELF_CHUNKS[c]
                if s == 0:
                    for i in range(2):
                        misc_written(pe, ("tq0", b, i))
                    keys = lambda r, B, kt: km0[:, r, (2 * b + kt) * P:(2 * b + kt + 1) * P]
                else:
                    pe.wait_ge(sem("masks_ready"), 2)
                    misc_written(pe, ("tqm", 4, b))
                    w = slot("km4", b)
                    keys = lambda r, B, kt: km4[:, w, r, B, kt * P:(kt + 1) * P]
                dst = take_scores(step)
                if kind == "k0":
                    for r in range(4):
                        o = dst[:, r * T:(r + 1) * T]
                        ins = mm(o, keys(r, n, 0), qT[:, n, toks(b)], start=True, stop=s == 0)
                        if s:
                            ins = mm(o[:, 0:P], identb[:, :], causal_tr[:, :], start=False, stop=True)
                else:
                    for q in range(2):
                        if s:
                            mm(dst[:, q * 512:(q + 1) * 512].rearrange("p (r t) -> p r t", r=4),
                               identb[:, :], masks(causal_tr, 4), start=True, stop=False)
                        for r in range(4):
                            o = dst[:, q * 512 + r * P:q * 512 + (r + 1) * P]
                            ins = mm(o, keys(r, 2 * n + q, 1), qT[:, 2 * n + q, b * T + P:(b + 1) * T],
                                     start=s == 0, stop=s == 0 or r == 3)
                ins.then_inc(score_full, 1)

            def cross_scores(step):
                _, s, b, J = step
                misc_written(pe, ("tqm", s, b))
                dst = take_scores(step)
                q = qT[:, :, toks(b)] if s == 1 else qcT[:, slot("qcT", b)]
                for r in range(4):
                    for jj in range(2):
                        ins = mm(dst[64 * jj:64 * jj + 64, r * T:(r + 1) * T],
                                 kcm[:, r, 2 * J + jj, b * KV:(b + 1) * KV], q[:, 2 * J + jj, :],
                                 start=True, stop=True)
                ins.then_inc(score_full, 1)

            def weighted_values(step):
                _, s, b, c = step
                dst = outs[:, slot("out", (s, b)), :]
                pr = probs[:, slot("prob", step), :]
                if c == 0 and SLOTS["out"].turn((s, b)):
                    pe.wait_ge(out_copied[slot("out", (s, b))], SLOTS["out"].turn((s, b)))
                if s == 0:
                    n = sum(1 for t in ORDER[:INDEX["sc", s, b, c] + 1] if t[:2] == ("sc", 0))
                    pe.wait_ge(sem("prob_masked"), n)
                    pe.wait_ge(sem("v0_ready"), 4 * count(("ropeb",), ("ropeb", b)))
                else:
                    score_written(pe, ("sc", s, b, c))
                if s in (1, 5):
                    misc_written(pe, ("kcv", 1 if s == 1 else 4))
                    for r in range(4):
                        ins = mm(dst[32 * r:32 * r + 32, c * T:(c + 1) * T], vc[:, s // 4, b, c, r, :],
                                 pr[:, r * T:(r + 1) * T], start=True, stop=True)
                else:
                    if s == 4:
                        misc_written(pe, ("v4", b))
                    kind, n = SELF_CHUNKS[c]
                    vals = lambda r, B, kt: (v0[:, 2 * b + kt, r, B % 2, :] if s == 0 else
                                             vst[:, 2 * b + kt, 4 * B + r, :])
                    if kind == "k0":
                        for r in range(4):
                            ins = mm(dst[32 * r:32 * r + 32, n // 2 * T:(n // 2 + 1) * T],
                                     vals(r, n, 0), pr[:, r * T:(r + 1) * T],
                                     start=n % 2 == 0, stop=False)
                    else:
                        for q in range(2):
                            for r in range(4):
                                ins = mm(dst[32 * r:32 * r + 32, n * T + P:(n + 1) * T],
                                         vals(r, 2 * n + q, 1),
                                         pr[:, (4 * q + r) * P:(4 * q + r + 1) * P],
                                         start=False, stop=q == 1)
                ins.then_inc(prob_used[slot("prob", step)], 1)

            pe.wait_ge(sem("cst_loaded"), 16)
            for step in ORDER:
                kind, b = step[0], step[-1]
                if kind == "tr":
                    pe.wait_ge(sem("xn_ready"), count(("lnb",), ("lnb", step[1], b)))
                    transposes(take_misc(step), [xn[:, half[step[1]], 2 * b + i, :]
                                                 for i in range(2)], ident)
                elif kind == "qkv":
                    pe.wait_ge(sem("wa_loaded"), 16)
                    misc_written(pe, ("tr", 0, b))
                    natural(step, tile_cols(xnT[:, 0, :], b), part(wa, WA, "qkv"))
                elif kind == "tq0":
                    _, b, i = step
                    pe.wait_ge(sem("stack_ready"), count(STACKS, ("ropeb", b)))
                    pe.wait_ge(sem("k0_ready"), count(("ropeb",), ("ropeb", b)))
                    q, k = qn[:, slot("stack_q", (0, b)), i], kn[:, slot("stack_k", (0, b)), i]
                    take_misc(step)
                    transposes(misc16[MISC.slot(step)],
                               [q[:, 4 * B:4 * B + 4, :].rearrange("p h n -> p (h n)") for B in range(4)] +
                               [k[:, 0:4, :].rearrange("p h n -> p (h n)")], ident16[:, :])
                elif kind == "kck":
                    pe.wait_ge(sem("w64_loaded"), 16)
                    natural(step, tile_cols(W6("ctx"), 0), W6({1: "wk1", 4: "wck4"}[b]))
                elif kind == "kcv":
                    pe.wait_ge(sem("w64_loaded"), 16)
                    natural(step, [W6("ctx2")[:, n * P:(n + 1) * P] for n in range(NB)],
                            W6({1: "wv1", 4: "wcv4"}[b]))
                elif kind == "kct":
                    stacked(step, kn[:, slot("stack_k", ("context", b))], ("kck", b))
                elif kind == "sc":
                    if step[1] in (0, 4):
                        self_scores(step)
                    else:
                        cross_scores(step)
                elif kind == "pv":
                    weighted_values(step)
                elif kind == "ot":
                    _, s, b = step
                    pe.wait_ge(out_copied[slot("out", (s, b))], SLOTS["out"].turn((s, b)) + 1)
                    c = copied[:, slot("copied", (s, b)), :]
                    transposes(take_misc(step), [c[:, J * T + i * P:J * T + (i + 1) * P]
                                                 for i in range(2) for J in range(2)], ident)
                elif kind == "ou":
                    _, s, b = step
                    misc_written(pe, ("ot", s, b))
                    if s == 5:
                        pe.wait_ge(sem("y_added"), sum(1 for t in ORDER[:INDEX["ot", s, b] + 1]
                                                       if t[:2] == ("ot", 5)))
                    transposes(take_misc(step), [y[:, slot("y", (s, b)), i, :] for i in range(2)], ident)
                elif kind == "op":
                    _, s, b = step
                    misc_written(pe, ("ou", s, b))
                    if s:
                        pe.wait_ge(sem("wb_loaded"), 16)
                    w = yT[:, slot("yT", (s, b)), :]
                    natural(step, [w[:, i * P:(i + 1) * P] for i in range(2)],
                            part(wa, WA, "wo0") if s == 0 else W({1: "wo1", 5: "wp4"}[s]))
                elif kind in ("q1", "q4", "k4", "qc4", "v4"):
                    s = 1 if kind == "q1" else 4
                    pe.wait_ge(sem("wb_loaded"), 16)
                    misc_written(pe, ("tr", s, b))
                    w = {"q1": "wq1", "q4": "wq4", "k4": "wk4", "qc4": "wcq4", "v4": "wv4"}[kind]
                    natural(step, tile_cols(xnT[:, half[s], :], b), W(w))
                elif kind in ("tq", "tqm"):
                    _, s, b = step
                    if kind == "tqm":
                        pe.wait_ge(sem("max_ready"), count(("mxe",), ("mxe", s, b)))
                    buf = qcn[:, slot("stack_c", (5, b))] if s == 5 else qn[:, slot("stack_q", (s, b))]
                    stacked(step, buf, ({1: "q1", 4: "q4", 5: "qc4"}[s], b))
                elif kind == "tk4":
                    stacked(step, kn[:, slot("stack_k", (4, b))], ("k4", b))
                elif kind == "mxc":
                    _, s, b, i = step
                    misc_written(pe, ("tq", s, b))
                    misc_written(pe, ("kct", 1 if s == 1 else 4))
                    dst = take_scores(step)
                    q = (qT[:, :, toks(b)] if s == 1 else qcT[:, slot("qcT", b)])[:, :, i * P:(i + 1) * P]
                    for B in range(4):
                        ins = mm(dst[:, B * T:(B + 1) * T], q[:, B, :],
                                 kcm[:, :, B, b * KV:(b + 1) * KV], start=True, stop=True)
                    ins.then_inc(score_full, 1)
                elif kind == "mxs":
                    _, b, c = step
                    pe.wait_ge(sem("masks_ready"), 2)
                    misc_written(pe, ("tq", 4, b))
                    pe.wait_ge(sem("km4_ready"), 4 * count(("tk4",), ("tk4", b)))
                    dst, w = take_scores(step), slot("km4", b)
                    for n in range(2):
                        o = dst[:, n * 512:(n + 1) * 512]
                        if c < 2:
                            B = 2 * c + n
                            mm(o.rearrange("p (r k) -> p r k", r=4), identb[:, :],
                               masks(causal_nat, 4), start=True, stop=False)
                            ins = mm(o, qT[:, B, b * T:b * T + P], km4[:, w, :, B, 0:P],
                                     start=False, stop=True)
                        else:
                            B = c - 2
                            mm(o, qT[:, B, b * T + P:(b + 1) * T], km4[:, w, 2 * n:2 * n + 2, B, :],
                               start=True, stop=False)
                            ins = mm(o.rearrange("p (r k) -> p r k", r=2)[:, :, P:T], identb[:, :],
                                     masks(causal_nat, 2), start=False, stop=True)
                    ins.then_inc(score_full, 1)
                elif kind == "tr2":
                    pe.wait_ge(sem("xn_ready"), count(("lnb",), ("lnb", "2b", b)))
                    transposes(take_misc(step), [xn[:, n, 2 * b + i, :] for n in range(2)
                                                 for i in range(2)], ident)
                elif kind == "xa":
                    misc_written(pe, ("tr2", b))
                    mm(take_misc(step)[:, 0:T], W("attn_w"), n2T[:, toks(b)], start=True, stop=True)\
                        .then_inc(misc_full, 1)
                elif kind == "fup":
                    j = step[1]
                    for n in PAIRS[j // 2]:
                        misc_written(pe, ("xa", n))
                    pe.wait_ge(sem(f"w1a_loaded{j // 2}"), 16)
                    dst = take_scores(step)
                    for n in range(2 * HC):
                        e, c = 2 * j + n // HC, n % HC
                        ins = mm(dst[:, n * P:(n + 1) * P], w1[:, e, c * P:(c + 1) * P],
                                 experts(xaT, e), start=True, stop=True)
                    ins.then_inc(score_full, 1)
                elif kind == "fdown":
                    j = step[1]
                    score_written(pe, ("fup", j))
                    pe.wait_ge(sem(f"w2a_loaded{j // 2}"), 16)
                    dst = take_misc(step)
                    for n in range(2):
                        for c in range(HC):
                            ins = mm(dst[:, n * P:(n + 1) * P], w2[:, 2 * j + n, c, :],
                                     hid0[:, slot("hid0", j), (n * HC + c) * P:(n * HC + c + 1) * P], start=c == 0, stop=c == HC - 1)
                    ins.then_inc(misc_full, 1)
                elif kind == "nxa":
                    for n in range(2):
                        misc_written(pe, ("fdown", 2 * (b % 2) + n))
                    natural(step, tile_cols(eoT, b), W("next_w"))
                elif kind == "tr3":
                    pe.wait_ge(sem("xn_ready"), count(("lnb",), ("lnb", "3b", b)))
                    transposes(take_misc(step), [xn[:, 0, 2 * b + i, :] for i in range(2)], ident)
                elif kind == "p3a":
                    misc_written(pe, ("tr3", b))
                    dst = take_misc(step)
                    for n, w in enumerate(("wqi3", "wkf3")):
                        ins = mm(dst[0:DH + 1, n * T:(n + 1) * T], W(w), xnT[:, 1, toks(b)],
                                 start=True, stop=True)
                    ins.then_inc(misc_full, 1)
                elif kind == "p3b":
                    misc_written(pe, ("tr3", b))
                    natural(step, tile_cols(xnT[:, 1, :], b), W("wvo3"))
                elif kind == "ml" and step[2] == 0:
                    b = step[1]
                    w = slot("mlstm", b)
                    pe.wait_ge(sem("rows_ready"), count(("rows",), ("rows", b)))
                    pe.wait_ge(sem("masks_ready"), 2)
                    misc_written(pe, ("p3a", b))
                    dst = take_scores(step)
                    for kt, (at, n) in enumerate(((0, T), (T, P))):
                        o, ts = dst[:, at:at + n], slice(T - n, T)
                        mm(o, rowa[:, w, kt * P:(kt + 1) * P], one_row[:, 0:n], start=True, stop=False)
                        mm(o, one_row[:, 0:P], rowg[:, w, ts], start=False, stop=False)
                        mm(o[:, 0:P], identb[:, :], causal_tr[:, :], start=False, stop=True)
                        ins = mm(dst[:, 512 + at:512 + at + n], kT3[:, w, kt * P:(kt + 1) * P],
                                 qT3[:, w, ts], start=True, stop=True)
                    ins.then_inc(score_full, 1)
                elif kind == "ml" and step[2] == 1:
                    b = step[1]
                    s3 = slot("mlstm", b)
                    score_written(pe, ("ml", b, 0))
                    misc_written(pe, ("p3b", b))
                    pe.wait_ge(sem("v3_ones"), count(("p3b",), ("p3b", b)))
                    dst, w, n = take_misc(step), weight[:, s3, :], DH + 1
                    mm(dst[:, 0:n], w[:, 0:P], v3[:, s3, 0, :], start=True, stop=True)
                    mm(dst[:, n:2 * n], w[:, P:T], v3[:, s3, 0, :], start=True, stop=False)
                    mm(dst[:, n:2 * n], w[:, T:T + P], v3[:, s3, 1, :], start=False, stop=True)\
                        .then_inc(misc_full, 1)
                elif kind == "ml" and step[2] == 2:
                    b = step[1]
                    misc_written(pe, ("ml", b, 1))
                    dst = take_misc(step)
                    for i in range(2):
                        ins = nc.tensor.transpose(dst[0:DH, i * P:(i + 1) * P],
                                                  h3[:, slot("mlstm", b), i, :], ident)
                    ins.then_inc(misc_full, 1)
                elif kind == "ml":
                    b = step[1]
                    misc_written(pe, ("ml", b, 2))
                    natural(step, [h3T[:, slot("mlstm", b), i * P:(i + 1) * P] for i in range(2)],
                            W6("wout3"))
                elif kind == "ga":
                    misc_written(pe, ("tr", 6, b))
                    natural(step, tile_cols(xnT[:, 1, :], b), W("gate"))
                elif kind == "gc":
                    pe.wait_ge(sem("comb_ready"), count(("gb",), ("gb", b)))
                    dst = take_misc(step)
                    for i in range(2):
                        ins = nc.tensor.transpose(dst[0:NE, i * P:(i + 1) * P], comb[:, 2 * b + i, :], ident)
                    ins.then_inc(misc_full, 1)
                elif kind == "gd":
                    pe.wait_ge(sem("b2m_loaded"), 16)
                    misc_written(pe, ("gc", b))
                    natural(step, [combT[:, i * P:(i + 1) * P] for i in range(2)], b2m[:, :])
                elif kind == "mup":
                    _, h, e, n = step
                    for b in PAIRS[h]:
                        misc_written(pe, ("tr", 6, b))
                    pe.wait_ge(sem(f"w1b_loaded{e // 4}"), 16)
                    dst = take_scores(step)
                    for cc in range(2):
                        c = 2 * n + cc
                        ins = mm(two(dst[:, cc * 512:(cc + 1) * 512]), w1[:, e, c * P:(c + 1) * P],
                                 xnT[:, 1, :].rearrange("p (m q t) -> p q m t", m=2, q=2)[:, h],
                                 start=True, stop=True)
                    ins.then_inc(score_full, 1)
                elif kind == "mdown":
                    _, h, e = step
                    for n in range(2):
                        score_written(pe, ("mup", h, e, n))
                    pe.wait_ge(sem(f"w2b_loaded{e // 4}"), 16)
                    dst, w = take_misc(step), slot("hidden", (h, e))
                    for i in range(4):
                        for c in range(HC):
                            ins = mm(dst[:, i * P:(i + 1) * P], hid1[:, w, c, i * P:(i + 1) * P],
                                     w2[:, e, c, :], start=c == 0, stop=c == HC - 1)
                    ins.then_inc(misc_full, 1)



def constants():
    import numpy as np

    p = np.arange(P)
    c = np.zeros((P, CST["all"][1]), np.float32)

    def put(name, value):
        a, n = CST[name]
        c[:, a:a + n] = value

    put("ident", np.eye(P))
    put("causal_nat", np.where(p[None, :] > p[:, None], -1e30, 0))
    put("causal_tr", np.where(p[:, None] > p[None, :], -1e30, 0))
    put("rowmask", p[:, None] // 32 == np.arange(4)[None, :])
    put("iota", np.broadcast_to(np.arange(NE), (P, NE)))
    half = HD // 2
    inv = (1.0 / np.float32(10000.0) ** (np.arange(half, dtype=np.float32) / half)).astype(np.float32)
    ang = np.arange(T, dtype=np.float32)[:, None] * inv[None, :]
    cos, sin = np.cos(ang), np.sin(ang)
    for name, t in (("cos", np.concatenate([cos, cos], 1)), ("sin", np.concatenate([-sin, sin], 1))):
        put(name, t.reshape(2, P, HD).transpose(1, 0, 2).reshape(P, 2 * HD))
    return c


def ordered(w, head_of):
    import numpy as np

    w = w.reshape(H, HD, P)
    return np.concatenate([w[head_of(2 * J + jj, r)] for J in range(2) for r in range(4)
                           for jj in range(2)], 0)


def kernel(**inputs):
    import numpy as np
    import concourse.bacc as bacc
    from concourse.bass_utils import run_bass_kernel_spmd

    g = {k: np.asarray(v) for k, v in inputs.items()}
    wqkv = g["L0_attn_w_qkv"]
    wq = wqkv[:, 0:P].reshape(P, 4, 4, HD).transpose(0, 2, 1, 3).reshape(P, P)
    row1 = lambda n: g[n].reshape(1, -1)
    ctx = g["ctx_512"].transpose(2, 0, 1)
    w1 = lambda w: np.ascontiguousarray(w.transpose(1, 0, 2))
    w2 = lambda w: np.ascontiguousarray(w.reshape(NE, HC, P, P).transpose(2, 0, 1, 3))
    arrays = {
        "x": g["x"],
        "cst": constants(),
        "wa": np.concatenate([wq, wqkv[:, P:], ordered(g["L0_attn_w_o"], lambda B, r: 4 * r + B)], 1),
        "wb": np.concatenate([
            g["L0_xattn_Wq"], ordered(g["L0_xattn_Wo"], lambda B, r: 4 * B + r),
            g["L0_ffn_attn_w"].T, g["L0_ffn_next_w"].T, g["L1_attn_Wq"].T, g["L1_attn_wi_w"].T,
            g["L1_attn_Wk"].T, g["L1_attn_wf_w"].T, g["L1_attn_Wv"].T, g["L1_attn_Wo"].T,
            g["L1_xattn_Wk"], g["L1_xattn_Wq"], g["L1_xattn_Wv"], g["L1_xattn_Wcq"],
            ordered(g["L1_xattn_Wp"], lambda B, r: 4 * B + r), g["L1_ffn_gate_w"].T], 1),
        "w64": np.concatenate([
            g["L0_xattn_Wk"], g["L0_xattn_Wv"], g["L1_xattn_Wck"], g["L1_xattn_Wcv"],
            g["L1_attn_Wout"].T, ctx.reshape(64, NB * KV),
            np.stack([ctx, ctx], 2).reshape(64, NB * 2 * KV)], 1),
        "col": np.concatenate([
            row1("L0_ffn_ln_scale"), row1("L0_ffn_ln_bias"), row1("L0_ffn_attn_b"), g["L0_ffn_b2"],
            g["L0_ffn_b1"].reshape(NE * HC, P), row1("L1_attn_norm_w"),
            g["L1_ffn_b1"].reshape(NE * HC, P)], 0).T,
        "row": np.concatenate([row1(n) for n in (
            "L0_xattn_bq", "L0_xattn_bk", "L0_xattn_bv", "L0_xattn_bo", "L0_ffn_next_b",
            "L1_attn_bo", "L1_xattn_bk", "L1_xattn_bq", "L1_xattn_bv", "L1_xattn_bck",
            "L1_xattn_bcq", "L1_xattn_bcv", "L1_xattn_bp")], 1),
        "gate_bias": np.concatenate([row1("L1_attn_wi_b"), row1("L1_attn_wf_b")], 1),
        "b2m": g["L1_ffn_b2"],
        "w1a": w1(g["L0_ffn_w1"]),
        "w2a": w2(g["L0_ffn_w2"]),
        "w1b": np.ascontiguousarray(g["L1_ffn_w1"].transpose(2, 0, 1)),
        "w2b": w2(g["L1_ffn_w2"].transpose(0, 2, 1)),
    }
    nc = bacc.Bacc("TRN2", target_bir_lowering=False, num_devices=1)
    maps, d = {}, {}
    for name, a in arrays.items():
        maps[f"in_{name}"] = np.ascontiguousarray(a)
        d[name] = nc.dram_tensor(f"in_{name}", a.shape, mybir.dt.from_np(a.dtype), kind="ExternalInput").ap()
    out = nc.dram_tensor("out", (NB, T, P), F32, kind="ExternalOutput").ap()
    decoder(nc, d, out)
    r = run_bass_kernel_spmd(nc, [maps], core_ids=[0])
    return r.results[0]["out"]
```

```python
from contextlib import ExitStack

import concourse.bass as bass
from concourse import mybir

F32 = mybir.dt.float32
F16 = mybir.dt.float16
BF16 = mybir.dt.bfloat16
U32 = mybir.dt.uint32
ALU = mybir.AluOpType
ACT = mybir.ActivationFunctionType
X = mybir.AxisListType.X

P = 128
NB = 4
T = 256
NT = NB * T // P
NTOK = NB * T
H = 16
HD = 8
KV = 64
DH = 64
NE = 8
HC = 4
EPS = 1e-5
AGAIN = {2: 1e-5, 3: 1e-6}
SCALE = float(1.0 / (HD ** 0.5))
MAXDIV = 64.0
WSCALE = 64.0



def columns(*sizes):
    at, out = 0, {}
    for name, n in sizes:
        out[name] = (at, n)
        at += n
    out["all"] = (0, at)
    return out


CST = columns(("ident", P), ("causal_nat", P), ("causal_tr", P), ("rowmask", 4),
              ("iota", NE), ("cos", 2 * HD), ("sin", 2 * HD))
WA = columns(("qkv", 192), ("wo0", P))
WB = columns(("wq1", P), ("wo1", P), ("attn_w", P), ("next_w", P), ("wqi3", DH + 1),
             ("wkf3", DH + 1), ("wvo3", 2 * DH), ("wk4", P), ("wq4", P), ("wv4", P),
             ("wcq4", P), ("wp4", P), ("gate", NE))
W64 = columns(("wk1", P), ("wv1", P), ("wck4", P), ("wcv4", P), ("wout3", P), ("ctx", NB * KV),
              ("ctx2", NB * 2 * KV))
COL = columns(("ln_scale", 1), ("ln_bias", 1), ("attn_b", 1), ("b2", NE), ("b1", NE * HC),
              ("norm_w", 1), ("b1m", NE * HC))
ROW = columns(("bq1", P), ("bk1", P), ("bv1", P), ("bo1", P), ("next_b", P), ("bo3", DH),
              ("bk4", P), ("bq4", P), ("bv4", P), ("bck4", P), ("bcq4", P), ("bcv4", P), ("bp4", P))


class Uses:

    def __init__(self, uses):
        self.at, given = {}, {}
        for n, (step, slot, gives) in enumerate(uses):
            before = given.get(slot, 0)
            given[slot] = before + gives
            self.at[step] = (slot, n + 1, before, before + gives)

    def slot(self, step):
        return self.at[step][0]

    def full(self, step):
        return self.at[step][1]

    def before(self, step):
        return self.at[step][2]

    def done(self, step):
        return self.at[step][3]


class Slots:

    def __init__(self, slots, holders):
        self.at, last, turns = {}, [None] * slots, [0] * slots
        for holder, slot, release in holders:
            self.at[holder] = (slot, last[slot], turns[slot])
            last[slot] = release
            turns[slot] += 1

    def slot(self, holder):
        return self.at[holder][0]

    def before(self, holder):
        return self.at[holder][1]

    def turn(self, holder):
        return self.at[holder][2]


SELF_CHUNKS = [("k0", 0), ("k0", 1), ("k1", 0), ("k0", 2), ("k0", 3), ("k1", 1)]
CHUNKS = {0: 6, 1: 2, 4: 6, 5: 2}
HELD = {"stack_q": 2, "stack_k": 2, "stack_c": 2, "qcT": 2, "km4": 2, "prob": 4, "out": 2,
        "copied": 2, "y": 2, "y4": 2, "yT": 2, "rope": 2, "mlstm": 2, "hidden": 2, "kT": 1, "combT": 1,
        "zn": 2, "mx": 2, "mxc": 2, "hid0": 2}
PAIRS = [(0, 2), (1, 3)]
TABLES = {"ropea": "sqrt", "sc": "exp", "p3b": "exp", "ml0": "exp", "ga": "exp", "fup": "gelu",
          "nxa": "gelu"}


def the_steps():
    steps, take, give = {}, {}, {}

    def add(step, after, *parts, behind=()):
        steps[step] = ([a for a in after if a], parts, [a for a in behind if a])

    def hold(pool, holder, first, last):
        take.setdefault(first, []).append((pool, holder))
        give.setdefault(last, []).append((pool, holder))

    def norm(s, b, after):
        twice = s in (2, 3)
        add(("lna", s, b), after, ("D", 0.7), ("G", 1.35 if twice else 1.0))
        parts = [("D", 0.9 if twice else 0.5)] + ([("G", 0.7)] if s in (1, 3, 4) else [])
        add(("lnb", s, b), [("lna", s, b)], *parts)
        return ("lnb", s, b)

    def attention(s, b, after):
        for c in range(CHUNKS[s]):
            sc, pv = ("sc", s, b, c), ("pv", s, b, c)
            parts = {0: (("P", 0.45), ("A", 0.95), ("G", 0.85)), 4: (("P", 0.7), ("A", 0.95))}.get(
                s, (("P", 0.5), ("A", 0.95)))
            add(sc, after, *parts, behind=[c and ("sc", s, b, c - 1), s == 5 and ("sc", 4, b, 5)])
            add(pv, [sc], ("P", 0.55), behind=[c and ("pv", s, b, c - 1)])
            hold("prob", pv, sc, pv)
        hold("out", (s, b), ("sc", s, b, 0), ("oc", s, b))
        add(("oc", s, b), [("pv", s, b, CHUNKS[s] - 1)], ("A", 0.5), behind=[s == 5 and ("oc", 4, b)])
        hold("copied", (s, b), ("oc", s, b), ("ot", s, b))
        add(("ot", s, b), [("oc", s, b), ("ot", 4, b) if s == 5 else None], ("P", 0.45),
            ("D", 1.2 if s == 5 else 0.8))
        if s == 4:
            hold("y4", b, ("ot", 4, b), ("ot", 5, b))
        else:
            hold("y", (s, b), ("ot", s, b), ("ou", s, b))
            add(("ou", s, b), [("ot", s, b)], ("P", 0.4), ("A", 0.4))
            hold("yT", (s, b), ("ou", s, b), ("op", s, b))
            add(("op", s, b), [("ou", s, b)], ("P", 0.45), ("D", 0.5))

    def stacked_queries(kind, s, b, after, keys):
        pool = "stack_c" if s == 5 else "stack_q"
        add((kind, b), after, ("P", 0.45), ("D", 1.5))
        add(("tq", s, b), [(kind, b)], ("P", 0.5), ("A", 1.05))
        if s == 4:
            for c in range(6):
                add(("mxs", b, c), [("tq", 4, b)] + keys, ("P", 0.75), ("D", 1.25),
                    behind=[c and ("mxs", b, c - 1)])
            hold("mx", b, ("mxs", b, 0), ("mxe", s, b))
            last = ("mxs", b, 5)
        else:
            for i in range(2):
                add(("mxc", s, b, i), [("tq", s, b)] + keys, ("P", 0.5), ("D", 1.15),
                    behind=[i and ("mxc", s, b, 0)])
            hold("mxc", (s, b), ("mxc", s, b, 0), ("mxe", s, b))
            last = ("mxc", s, b, 1)
        add(("mxe", s, b), [last], ("D", 0.6))
        add(("tqm", s, b), [("mxe", s, b)], ("P", 0.5), ("A", 1.05))
        hold(pool, (s, b), (kind, b), ("tqm", s, b))
        return ("tqm", s, b)

    every = range(NB)
    add(("casts", 0), [], ("D", 0.9))
    add(("presets0", 0), [], ("G", 4.0))
    for b in every:
        n = norm(0, b, [])
        add(("tr", 0, b), [n], ("P", 0.4), ("A", 0.3))
        add(("qkv", b), [("tr", 0, b)], ("P", 1.3), ("A", 0.5))
        add(("ropea", b), [("qkv", b)], ("A", 0.45), ("D", 0.4), ("A", 0.5))
        add(("ropeb", b), [("ropea", b), ("presets0", 0)], ("D", 3.7), ("G", 2.2))
        hold("rope", b, ("ropea", b), ("ropeb", b))
        for i in range(2):
            add(("tq0", b, i), [("ropeb", b), ("casts", 0)], ("P", 0.5), ("A", 0.5), ("D", 0.6),
                behind=[i and ("tq0", b, 0)])
        hold("stack_q", (0, b), ("ropeb", b), ("tq0", b, 1))
        hold("stack_k", (0, b), ("ropeb", b), ("tq0", b, 1))
    for l, after in ((1, []), (4, [("sc", 1, b, 1) for b in every])):
        add(("kck", l), after, ("P", 0.8), ("D", 1.45))
        if l == 1:
            add(("presets1", 0), [], ("G", 3.5))
        add(("kcv", l), after + [("presets1", 0)], ("P", 1.4), ("D", 1.2))
        add(("kct", l), [("kck", l), ("casts", 0)], ("P", 0.6), ("D", 3.2))
        hold("stack_k", ("context", l), ("kck", l), ("kct", l))
    for b in every:
        attention(0, b, [("tq0", b, 1)])
        add(("presets4", b), [("pv", 0, b, 5)], ("G", 1.8))
        n = norm(1, b, [("op", 0, b)])
        add(("tr", 1, b), [n], ("P", 0.4), ("A", 0.4))
        m = stacked_queries("q1", 1, b, [("tr", 1, b)], [("kct", 1)])
        attention(1, b, [m, ("kcv", 1)])
        n = norm(2, b, [("op", 1, b)])
        add(("tr2", b), [n], ("P", 0.8), ("A", 0.4), ("D", 0.5))
        add(("xa", b), [("tr2", b)], ("P", 0.5), ("D", 0.6))
    for j in range(NE // 2):
        pair = PAIRS[j // 2]
        add(("fup", j), [("xa", b) for b in pair], ("P", 2.0), ("A", 2.2),
            behind=[j % 2 and ("fup", j - 1)])
        add(("fdown", j), [("fup", j)], ("P", 2.0), ("D", 0.6), behind=[j % 2 and ("fdown", j - 1)])
        hold("hid0", j, ("fup", j), ("fdown", j))
    for b in every:
        j = 2 * (b % 2)
        add(("nxa", b), [("fdown", j), ("fdown", j + 1)], ("P", 0.45), ("D", 0.4), ("A", 0.4))
        add(("nxb", b), [("nxa", b)], ("D", 0.4))
        hold("zn", b, ("nxa", b), ("nxb", b))
        n = norm(3, b, [("nxb", b)])
        add(("tr3", b), [n], ("P", 0.4), ("A", 0.4))
        add(("p3a", b), [("tr3", b)] + [("ropeb", n) for n in every], ("P", 1.4), ("A", 0.4), ("D", 1.1))
        add(("p3b", b), [("tr3", b)], ("P", 0.5), ("A", 0.3), ("D", 0.4), ("A", 0.3),
            behind=[("p3a", b)])
        add(("rows", b), [("p3a", b)], ("D", 2.0))
        add(("ml", b, 0), [("rows", b)], ("P", 2.3), ("A", 0.5), ("D", 0.6))
        add(("ml", b, 1), [("ml", b, 0), ("p3b", b)], ("P", 0.7), ("D", 2.2))
        add(("ml", b, 2), [("ml", b, 1)], ("P", 0.4), ("A", 0.4))
        add(("ml", b, 3), [("ml", b, 2)], ("P", 0.75), ("D", 0.5))
        hold("mlstm", b, ("p3a", b), ("ml", b, 3))
    for b in every:
        n = norm(4, b, [("ml", b, 3)])
        add(("tr", 4, b), [n], ("P", 0.4), ("A", 0.4))
        add(("k4", b), [("tr", 4, b)], ("P", 0.45), ("D", 1.5))
        add(("tk4", b), [("k4", b)] + [("sc", 0, n, 5) for n in every],
            ("P", 0.5), ("A", 1.05), ("D", 1.8))
        hold("stack_k", (4, b), ("k4", b), ("tk4", b))
        hold("km4", b, ("tk4", b), ("sc", 4, b, 5))
        add(("v4", b), [("tr", 4, b), ("presets4", b)], ("P", 0.45), ("D", 0.6))
        m = stacked_queries("q4", 4, b, [("tk4", b)], [])
        attention(4, b, [m, ("v4", b)])
        m = stacked_queries("qc4", 5, b, [("tr", 4, b)], [("kct", 4)])
        hold("qcT", b, ("tq", 5, b), ("sc", 5, b, 1))
        attention(5, b, [m, ("kcv", 4)])
        n = norm(6, b, [("op", 5, b)])
        add(("tr", 6, b), [n], ("P", 0.4), ("A", 0.4))
        add(("xs", b), [("tr", 6, b)], ("G", 1.5))
        add(("ga", b), [("tr", 6, b)], ("P", 0.3), ("D", 1.3), ("A", 0.2))
        add(("gb", b), [("ga", b)], ("D", 1.8))
        add(("gc", b), [("gb", b)], ("P", 0.3), ("D", 0.4))
        add(("gd", b), [("gc", b)], ("P", 0.4), ("D", 0.5))
        hold("combT", b, ("gc", b), ("gd", b))
    for e in range(NE):
        add(("ws", e), [("ml", PAIRS[e // 4][1], 0), e and ("ws", e - 1)] +
            [("lnb", 1, b) for b in every] + [("q1", b) for b in every], ("A", 0.65), ("D", 0.65))
    for e in range(NE):
        add(("w2s", e), [("ws", NE - 1), e and ("w2s", e - 1)], ("A", 0.65), ("D", 0.65))
    for n in range(2 * NE):
        h, e = n // NE, n % NE
        prev = ((n - 1) // NE, (n - 1) % NE)
        after = [("ws", e)] + [("xs", b) for b in PAIRS[h]] + [("ml", b, 3) for b in every]
        for q in range(2):
            add(("mup", h, e, q), after, ("P", 1.33), ("A", 1.2),
                behind=[("mup", h, e, 0) if q else n and ("mup",) + prev + (1,)])
            add(("hs", h, e, q), [("mup", h, e, q)], ("A", 1.0), ("D", 1.1),
                behind=[q and ("hs", h, e, 0)])
            hold("hid0", (h, e, q), ("mup", h, e, q), ("hs", h, e, q))
        add(("mdown", h, e), [("hs", h, e, 1), ("w2s", e)] + [("gd", b) for b in PAIRS[h]],
            ("P", 2.65), ("D", 1.2), behind=[n and ("mdown",) + prev])
        hold("hidden", (h, e), ("hs", h, e, 0), ("mdown", h, e))
    return steps, take, give


STEPS, TAKE, GIVE = the_steps()
LOADED = {"lna0": 4.2, "kck": 7.5, "kcv": 7.5, "casts": 3.7, "presets0": 3.7}
HOP = 0.25


PSUM_GIVES = {"tr": 1, "qkv": 1, "tq0": 2, "kck": 1, "kcv": 1, "kct": 1, "ot": 1, "ou": 1, "op": 1,
              "q1": 1, "tq": 1, "tqm": 1, "tr2": 2, "xa": 1, "fdown": 1, "nxa": 1, "tr3": 1,
              "p3a": 2, "p3b": 2, "q4": 1, "k4": 1, "tk4": 1, "qc4": 1, "v4": 1, "ga": 1, "gc": 1,
              "gd": 1, "mdown": 1, "sc": 1, "mxc": 1, "mxs": 1, "fup": 1, "mup": 2}


def fills(step):
    if step[0] == "ml":
        return 1
    return PSUM_GIVES.get(step[0])


def wide(step):
    return step[0] in ("sc", "mxc", "mxs", "fup", "mup") or step[0] == "ml" and step[2] == 0


def reading_part(step):
    return 1 if step[0] in ("sc", "tk4", "nxa", "ga") else len(STEPS[step][1]) - 1


def kind_of(step):
    if step[0] == "ml":
        return f"ml{step[2]}"
    staged = ("lna", "lnb", "tr", "sc", "pv", "oc", "ot", "ou", "op", "tq", "tqm", "mxc", "mxe")
    return f"{step[0]}{step[1]}" if step[0] in staged else step[0]


def table_of(step):
    return TABLES.get("sc" if step[0] == "sc" else kind_of(step))


def pair_of(step):
    if step[0] in ("kck", "kcv", "kct", "ws", "w2s", "casts", "presets0"):
        return 0
    if step[0] in ("fup", "fdown"):
        return step[1] // 2
    if step[0] in ("mup", "hs", "mdown"):
        return step[1]
    b = step[1] if step[0] in ("ml", "tq0", "mxs") or step[0] == "presets4" else step[-1]
    if step[0] in ("sc", "pv", "mxc"):
        b = step[2]
    return b % 2


def the_order():
    after = {s: [] for s in STEPS}
    for s, (deps, _, behind) in STEPS.items():
        for dep in deps + behind:
            after[dep].append(s)
    way = {}

    def to_end(s):
        if s not in way:
            own = sum(t + HOP for _, t in STEPS[s][1])
            way[s] = max((to_end(n) + (own if s in STEPS[n][0] else 0) for n in after[s]), default=own)
        return way[s]

    for s in reversed(list(STEPS)):
        to_end(s)
    left = {s: len(deps) + len(behind) for s, (deps, _, behind) in STEPS.items()}
    ends = {}
    free = dict.fromkeys("PADG", 0.0)
    released = {pool: [0.0] * n for pool, n in HELD.items()}
    banks = [0.0] * BANKS
    at = {}
    rank = {s: PULL * way[s] + AHEAD.get(kind_of(s), (0, 0))[pair_of(s)] for s in STEPS}
    ready = [s for s in STEPS if not left[s]]
    order = []
    table = None

    def choice(times, allowed, t, narrow=0):
        best = None
        for n in allowed:
            if times[n] is not None:
                when = max(times[n], t)
                if best is None or when < best[1] - PREFER * (best[0] < narrow <= n):
                    best = n, when
        return best

    while ready:
        best = None
        for s in ready:
            t = max((ends[dep] for dep in STEPS[s][0]), default=LOADED.get(kind_of(s), 0.0))
            slots = []
            for pool, holder in TAKE.get(s, ()):
                found = choice(released[pool], range(HELD[pool]), t)
                if found is None:
                    break
                slots.append(found[0])
                t = found[1]
            else:
                if fills(s):
                    found = choice(banks, range(NARROW, BANKS) if wide(s) else range(BANKS), t, NARROW)
                    if found is None:
                        continue
                    bank, t = found
                    slots.append(bank)
                t = max(t + HOP, free[STEPS[s][1][0][0]])
                key = t - rank[s]
                if table_of(s) not in (None, table):
                    key += SWITCH
                if best is None or key < best[0]:
                    best = (key, s, t, slots)
        assert best is not None, "the steps hold each other up"
        _, s, t, slots = best
        ready.remove(s)
        order.append(s)
        for (pool, holder), n in zip(TAKE.get(s, ()), slots):
            at[pool, holder] = n
            released[pool][n] = None
        if fills(s):
            at["psum", s] = slots[-1]
        for n, (engine, dur) in enumerate(STEPS[s][1]):
            t = max(t, free[engine])
            if engine == "A" and table_of(s) not in (None, table):
                table = table_of(s)
                t += 1.3
            t = free[engine] = t + dur
            if fills(s) and n == reading_part(s):
                banks[slots[-1]] = t
            t += HOP
        ends[s] = t - HOP
        for pool, holder in GIVE.get(s, ()):
            released[pool][at[pool, holder]] = ends[s]
        for n in after[s]:
            left[n] -= 1
            if not left[n]:
                ready.append(n)
    return order, at, max(ends.values())


NARROW, BANKS, PREFER = 2, 4, 0.12
PULL, SWITCH = 0.00095, 0
AHEAD = {"casts": (3.8, 0), "fdown": (-5.1, -3.8), "fup": (0, -1.9), "ga": (0.2, -1.2),
         "gb": (-0.2, 3), "gc": (0.1, -0.7), "gd": (-0.9, 0), "hs": (0.4, 35.2), "k4": (0.9, 0),
         "kct": (-0.4, 0), "kcv": (-3.8, 0), "lna0": (31.1, 0), "lna1": (5.2, -0.2),
         "lna2": (12.5, 2.8), "lna3": (-1.3, -0.8), "lna4": (12.1, 22.6), "lna6": (14.5, 3.2),
         "lnb0": (0.2, 2), "lnb1": (0.7, -0.1), "lnb2": (2.4, -0.2), "lnb3": (-3.2, 5.2),
         "lnb4": (3.4, 1.1), "lnb6": (-0.2, 0), "mdown": (-1.2, -1.7), "ml0": (-1.2, 0.1),
         "ml1": (-2.5, -0.3), "ml2": (0.5, 0.4), "ml3": (1.3, 0.4), "mup": (-1.1, -0.1),
         "mxc1": (0, 0.4), "mxc5": (1.2, 0), "mxe1": (0, 19.6), "mxe4": (0, 10),
         "mxe5": (-1, -0.4), "mxs": (-2.5, 0.7), "nxa": (-5.4, -0.7), "nxb": (-4.9, -1.6),
         "oc0": (27, 9.3), "oc1": (0, 2.7), "oc4": (2.4, -1), "oc5": (0, 17.6), "op0": (0.3, 2.3),
         "op1": (0, -2.8), "op5": (-0.8, 1.5), "ot0": (0, 0.3), "ot1": (0, -0.2),
         "ot4": (-0.4, -0.4), "ot5": (-1, 0), "ou0": (-0.2, 0.7), "ou1": (0, -0.5),
         "ou5": (-2, -0.2), "p3a": (-1.4, 0), "p3b": (0.1, 0), "presets0": (0.9, 0),
         "presets4": (0, -2.7), "pv0": (-0.4, -0.3), "pv1": (-0.5, -0.1), "pv4": (-0.1, -0.2),
         "pv5": (-1.1, -1.1), "q1": (0.4, 0.1), "q4": (-1.3, 0.4), "qc4": (-1.2, -0.1),
         "qkv": (-1.7, 0), "ropea": (5.8, 0.1), "ropeb": (1.7, 0), "rows": (60.3, -0.9),
         "sc0": (0.5, -0.2), "sc1": (-0.2, -0.2), "sc4": (-0.1, 0), "sc5": (0, -1.3),
         "tk4": (-0.2, 0.1), "tq0": (-1.2, 0), "tq4": (-3.8, -0.3), "tq5": (-2.7, -1.2),
         "tqm1": (0.6, 0.1), "tqm4": (-2.1, -1.2), "tqm5": (-2.7, 0), "tr0": (0.5, -0.2),
         "tr1": (0.1, 0), "tr2": (0, -5.2), "tr3": (0.4, 0.6), "tr4": (-1, -0.5),
         "tr6": (14.9, -0.7), "v4": (-0.1, 0), "w2s": (-1.6, 0), "xa": (-0.1, -5.1), "xs": (0, 0.1)}
ORDER, AT, ABOUT = the_order()
INDEX = {step: n for n, step in enumerate(ORDER)}


def count(kinds, step):
    return sum(1 for s in ORDER[:INDEX[step] + 1] if s[0] in kinds)


def slots(pool):
    release = {(p, holder): s for s, gives in GIVE.items() for p, holder in gives}
    return Slots(HELD[pool], [(holder, AT[pool, holder], release[pool, holder]) for s in ORDER
                              for p, holder in TAKE.get(s, ()) if p == pool])


SLOTS = {pool: slots(pool) for pool in HELD}
PSUM = Uses([(s, AT["psum", s], fills(s)) for s in ORDER if fills(s)])


def decoder(nc, d, out):
    with ExitStack() as ctx:
        sb = lambda name, shape, dt=F32: ctx.enter_context(nc.sbuf_tensor(name, shape, dt))
        in_psum = lambda name, shape, dt=F32: ctx.enter_context(nc.psum_tensor(name, shape, dt))
        sems = {}

        def sem(name):
            if name not in sems:
                sems[name] = ctx.enter_context(nc.semaphore(name))
            return sems[name]

        double = in_psum("double", [P, BANKS - NARROW, 1024])
        single = in_psum("single", [P, NARROW, 512])
        outs = in_psum("outs", [P, HELD["out"], 512])

        x = sb("x", [P, NT, P])
        cst = sb("cst", [P, CST["all"][1]])
        wa = sb("wa", [P, WA["all"][1]])
        wb = sb("wb", [P, WB["all"][1]])
        w64 = sb("w64", [64, W64["all"][1]])
        col = sb("col", [P, COL["all"][1]])
        row = sb("row", [P, ROW["all"][1]])
        gate_bias = sb("gate_bias", [P, 2])
        b2m = sb("b2m", [NE, P])
        b1s = sb("b1s", [P, NE * HC])
        w1 = sb("w1", [P, NE, HC * P])
        w2 = sb("w2", [P, NE, HC, P])
        xn = sb("xn", [P, 2, NT, P])
        xnT = sb("xnT", [P, 2, NTOK])
        stat = sb("stat", [P, 2, NT, 6])
        mv = sb("mv", [P, 2, NT, 2])
        rstd = sb("rstd", [P, 2, 2, NT])
        neg_half = sb("neg_half", [P, 2, 2])
        ident16 = sb("ident16", [P, P], F16)
        identb = sb("identb", [P, P], BF16)
        causal_nat = sb("causal_nat", [P, P], BF16)
        causal_tr = sb("causal_tr", [P, P], BF16)
        qn = sb("qn", [P, 2, 2, H, 32], F16)
        kn = sb("kn", [P, 2, 2, H, 32], F16)
        qcn = sb("qcn", [P, 2, 2, H, 32], F16)
        qT = sb("qT", [P, 4, NTOK], F16)
        qcT = sb("qcT", [P, 2, 4, T], F16)
        kT = sb("kT", [P, 4, T], F16)
        kcm = sb("kcm", [P, 4, 4, NB * KV], F16)
        split = sb("split", [P, 2, P])
        vst = sb("vst", [P, NT, H, 32])
        vc = sb("vc", [P, 2, NB, 2, 4, 32])
        mx = sb("mx", [P, 2, 2, H])
        mxc = sb("mxc", [P, 2, 2, H])
        copied = sb("copied", [P, 2, 512])
        y4 = sb("y4", [P, 2, 2, P])
        y = sb("y", [P, 2, 2, P])
        yT = sb("yT", [P, 2, T])
        sums = sb("sums", [P, 2 * H])
        region_k = sb("region_k", [P, 4096])
        km0 = region_k[:, 0:2048].bitcast(F16).rearrange("p (r t) -> p r t", r=4)
        km4 = region_k[:, :].bitcast(F16).rearrange("p (s r g t) -> p s r g t", s=2, r=4, g=4)
        flatT, n2T = xnT[:, 0, :], xnT[:, 1, :]
        xaT, eoT = xnT[:, 0, :], xnT[:, 1, :]
        region_p = sb("region_p", [P, HELD["prob"] * 1024])
        probs = region_p[:, :].rearrange("p (s n) -> p s n", s=HELD["prob"])
        hid0 = sb("hid0", [P, HELD["hid0"], 2 * HC * P])
        tmp = sb("tmp", [P, 4620])

        def of_tmp(rows, first, n):
            return tmp[rows, first:first + n]

        every = slice(0, P)
        raw = of_tmp(every, 0, 1280).rearrange("p (b h e) -> p b h e", b=4, e=HD)
        rawv = of_tmp(every, 1280, 256).rearrange("p (b i n) -> p b i n", b=4, i=2)
        sq = of_tmp(every, 1536, 640).rearrange("p (s h e) -> p s h e", s=2, e=HD)
        rot = of_tmp(every, 2176, 320).rearrange("p (h e) -> p h e", e=HD)
        swp = of_tmp(every, 2496, 320).rearrange("p (h e) -> p h e", e=HD)
        cosx = of_tmp(every, 2816, 320).rearrange("p (h e) -> p h e", e=HD)
        sinx = of_tmp(every, 3136, 320).rearrange("p (h e) -> p h e", e=HD)
        nrm = of_tmp(every, 3456, 160).rearrange("p (b h) -> p b h", b=4)
        qT3 = of_tmp(slice(0, DH), 0, 512).rearrange("p (s t) -> p s t", s=2)
        kT3 = of_tmp(slice(0, DH), 512, 512).rearrange("p (s t) -> p s t", s=2)
        v3 = of_tmp(every, 1024, 260).rearrange("p (s i n) -> p s i n", s=2, i=2)
        og3 = of_tmp(every, 1290, 256).rearrange("p (s i n) -> p s i n", s=2, i=2)
        decay = of_tmp(every, 1546, 768).rearrange("p (s n) -> p s n", s=2)
        weight = of_tmp(every, 2314, 768).rearrange("p (s n) -> p s n", s=2)
        h3 = of_tmp(every, 3082, 256).rearrange("p (s i n) -> p s i n", s=2, i=2)
        h3T = of_tmp(slice(0, DH), 3338, 512).rearrange("p (s t) -> p s t", s=2)
        den3 = of_tmp(every, 3850, 2)
        gate_row = slice(DH, DH + 1)
        zif = [of_tmp(gate_row, 512, 512), of_tmp(gate_row, 3338, 512)]
        cumf = of_tmp(gate_row, 3852, T)
        rowa = of_tmp(gate_row, 3852 + T, 2 * T).rearrange("p (s t) -> p s t", s=2)
        rowg = of_tmp(gate_row, 0, 2 * T).rearrange("p (s t) -> p s t", s=2)
        hid1 = of_tmp(every, 0, 4096).bitcast(F16).rearrange("p (s v c n) -> p s v c n", s=2, v=2, c=HC)
        one_row = sb("one_row", [P, T])[gate_row, :]
        zn = sb("zn", [P, 2, 2, P])
        gl = sb("gl", [P, NT, NE])
        top = sb("top", [P, NT, NE])
        topi = sb("topi", [P, NT, NE], U32)
        topf = sb("topf", [P, NT, 2])
        gex = sb("gex", [P, NT, 2])
        gtmp = sb("gtmp", [P, 2, NE])
        comb = sb("comb", [P, NT, NE])
        combT = sb("combT", [NE, T])

        w1s = [(row[:, 0:512] if e == 0 else w1[:, e - 1, :]).bitcast(F16).rearrange(
            "p (s n) -> p s n", s=2) for e in range(NE)]
        w2s = [(w1[:, NE - 1, :] if e == 0 else w2[:, e - 1, :, :].rearrange("p c n -> p (c n)"))
               .bitcast(F16).rearrange("p (s c n) -> p s c n", s=2, c=HC) for e in range(NE)]
        xs = xnT[:, 0, :].bitcast(F16).rearrange("p (m q s t) -> p q s m t", m=2, q=2, s=2)

        def part(t, table, name):
            a, n = table[name]
            return t[:, a:a + n]

        ident = part(cst, CST, "ident")
        rowmask = part(cst, CST, "rowmask")
        bias = lambda name: part(row, ROW, name)
        both = lambda name: bias(name).unsqueeze(1).to_broadcast([P, 2, P])
        W = lambda name: part(wb, WB, name)
        W6 = lambda name: part(w64, W64, name)
        colv = lambda name, n=0: part(col, COL, name)[:, n:n + 1]
        tiles = lambda b: slice(2 * b, 2 * b + 2)
        tiles_of = lambda b: (2 * b, 2 * b + 1)
        toks = lambda b: slice(T * b, T * (b + 1))
        half = {0: 0, 1: 1, 2: 0, 3: 1, 4: 0, 6: 1}
        experts = lambda ap, e: ap.rearrange("p (m t) -> p m t", m=2)[:, :, e * 64:(e + 1) * 64]
        v0 = vst[:, :, 0:8, :].rearrange("p t (r j) n -> p t r j n", r=4)
        v4 = vst[:, :, :, :].rearrange("p t (j q r) n -> p t j q r n", j=2, q=2)

        psum_done = [sem(f"psum_done{s}") for s in range(BANKS)]
        psum_full = sem("psum_full")
        prob_used = [sem(f"prob_used{s}") for s in range(HELD["prob"])]
        out_copied = [sem(f"out_copied{s}") for s in range(HELD["out"])]

        def written(eng, step):
            eng.wait_ge(psum_done[PSUM.slot(step)], PSUM.done(step))

        def after_scalar(eng, step):
            eng.wait_ge(psum_done[PSUM.slot(step)], PSUM.before(step) + 1)

        def read_by_tensor(eng, pool, holder):
            step = SLOTS[pool].before(holder)
            if step is not None:
                eng.wait_ge(psum_full, PSUM.full(step))

        def hidden_free(eng, step):
            last = SLOTS["hid0"].before(step[1:])
            if last[0] == "fdown":
                eng.wait_ge(psum_full, PSUM.full(last))
            else:
                eng.wait_ge(sem("hidden_high"), count(("hs",), last))
                eng.wait_ge(sem("hidden_low"), count(("hs",), last))

        def slot(pool, holder):
            return SLOTS[pool].slot(holder)

        def psum(step):
            n = PSUM.slot(step)
            if n < NARROW:
                return single[:, n, :]
            return double[:, n - NARROW, :] if wide(step) else double[:, n - NARROW, 0:512]

        def psum16(step):
            return psum(step).bitcast(F16)

        def biased(step):
            return sum(1 for s in ORDER[:INDEX[step] + 1]
                       if s[0] == "lnb" and s[1] in (1, 3, 4))

        two = lambda ap: ap.rearrange("p (i n) -> p i n", i=2)
        STACKS = ("ropeb", "kck", "q1", "q4", "k4", "qc4")

        block = ctx.enter_context(nc.Block())

        @block.sync
        def _(sp):
            xin = d["x"].rearrange("b (i p) n -> p (b i) n", p=P)
            load_x = lambda b: sp.dma_start(x[:, tiles(b), :], xin[:, tiles(b), :]).then_inc(
                sem(f"x_loaded{b}"), 16)
            load_x(0)
            sp.dma_start(cst[:, :], d["cst"]).then_inc(sem("cst_loaded"), 16)
            for b in (2, 1, 3):
                load_x(b)
            sp.dma_start(wa[:, :], d["wa"]).then_inc(sem("wa_loaded"), 16)
            sp.dma_start(w64[:, :], d["w64"]).then_inc(sem("w64_loaded"), 16)
            sp.dma_start(row[:, :], d["row"].to_broadcast([P, ROW["all"][1]])).then_inc(
                sem("row_loaded"), 16)
            sp.dma_start(wb[:, :], d["wb"]).then_inc(sem("wb_loaded"), 16)
            sp.dma_start(col[:, :], d["col"]).then_inc(sem("col_loaded"), 16)
            sp.dma_start(gate_bias[gate_row, :], d["gate_bias"]).then_inc(sem("gate_bias_loaded"), 16)
            sp.dma_start(b2m[:, :], d["b2m"]).then_inc(sem("b2m_loaded"), 16)
            for h in range(2):
                es = slice(4 * h, 4 * h + 4)
                sp.dma_start(w1[:, es, :], d["w1a"][:, es, :]).then_inc(sem(f"w1a_loaded{h}"), 16)
                sp.dma_start(w2[:, es, :, :], d["w2a"][:, es, :, :]).then_inc(sem(f"w2a_loaded{h}"), 16)
            for h in range(2):
                for j in (2 * h, 2 * h + 1):
                    sp.wait_ge(psum_full, PSUM.full(("fdown", j)))
                es = slice(4 * h, 4 * h + 4)
                sp.dma_start(w1[:, es, :], d["w1b"][:, es, :]).then_inc(sem(f"w1b_loaded{h}"), 16)
                sp.dma_start(w2[:, es, :, :], d["w2b"][:, es, :, :]).then_inc(sem(f"w2b_loaded{h}"), 16)
            outv = out.rearrange("b (i p) n -> p (b i) n", p=P)
            for h in range(2):
                written(sp, ("mdown", h, NE - 1))
                for b in PAIRS[h]:
                    sp.dma_start(outv[:, tiles(b), :], x[:, tiles(b), :]).then_inc(sem("stored"), 16)
            sp.wait_ge(sem("stored"), 16 * NB)

        @block.gpsimd
        def _(pool):
            g = nc.gpsimd
            counts = {}

            def then(ins, name="pool_step"):
                counts[name] = counts.get(name, 0) + 1
                ins.then_inc(sem(name), 1)
                pool.wait_ge(sem(name), counts[name])

            then(g.memset(neg_half[:, :, :], -0.5))
            for step in ORDER:
                kind, b = step[0], step[-1]
                if kind == "lna":
                    s = step[1]
                    h = half[s]
                    pool.wait_ge(sem("var_ready"), count(("lna",), step))
                    var, r = mv[:, h, tiles(b), 1], rstd[:, h, :, tiles(b)]
                    then(g.tensor_scalar(r[:, 0], var, EPS, None, ALU.add))
                    if s in AGAIN:
                        eps2 = AGAIN[s]
                        then(g.tensor_scalar(r[:, 1], var, 1.0 + eps2, EPS * eps2, ALU.mult, ALU.add))
                        then(g.tensor_tensor(r, r, neg_half[:, :, :], ALU.pow), "rstd_ready")
                    else:
                        then(g.tensor_tensor(r[:, 0], r[:, 0], neg_half[:, 0, :], ALU.pow), "rstd_ready")
                elif kind == "lnb" and step[1] in (1, 3, 4):
                    pool.wait_ge(sem("xn_ready"), count(("lnb",), step))
                    pool.wait_ge(sem("row_loaded"), 16)
                    s = step[1]
                    added = xn[:, half[s], tiles(b), :] if s == 3 else both({1: "bo1", 4: "bp4"}[s])
                    then(g.tensor_tensor(x[:, tiles(b), :], x[:, tiles(b), :], added, ALU.add),
                         "x_biased")
                elif kind == "ropeb":
                    written(pool, ("qkv", b))
                    for i in range(2):
                        for jj in range(2):
                            v = rawv[:, b, i, :].rearrange("p (r e) -> p r e", e=HD)
                            then(g.tensor_copy(v0[:, 2 * b + i, :, jj, 16 * jj:16 * jj + HD], v),
                                 "v0_ready")
                    pool.wait_ge(sem("rope_done"), count(("ropeb",), step))
                    read_by_tensor(pool, "stack_k", (0, b))
                    k = kn[:, slot("stack_k", (0, b)), :, 0:4, :]
                    rk = rot.rearrange("p (i h) e -> p i h e", i=2)[:, :, 16:20, :]
                    then(g.tensor_copy(k[:, :, :, 0:8], rk))
                    then(g.tensor_tensor(k[:, :, :, 16:24], rk, k[:, :, :, 0:8], ALU.subtract))
                    then(g.tensor_copy(k[:, :, :, 8:16], k[:, :, :, 0:8]))
                    then(g.tensor_copy(k[:, :, :, 24:32], k[:, :, :, 16:24]), "k0_ready")
                elif kind == "sc" and step[1] == 0:
                    written(pool, step)
                    key = ("pv",) + step[1:]
                    n = 8 if SELF_CHUNKS[step[3]][0] == "k1" else 4
                    v = probs[:, slot("prob", key), :].rearrange("p (h t) -> p h t", h=n)[:, :, 0:P]
                    then(g.affine_select(out=v, in_=v, compare_op=ALU.is_ge, fill=0.0, base=0,
                                         pattern=[[0, n], [1, P]], channel_multiplier=-1),
                         "prob_masked")
                elif kind == "presets0":
                    then(g.memset(one_row, 1.0))
                    then(g.memset(vst[:, :, :, :], 0.0))
                    for jj in range(2):
                        a = 16 * jj + 8
                        then(g.memset(v0[:, :, :, jj, a:a + 8], 1.0))
                    pool.wait_ge(sem("cst_loaded"), 16)
                    for table, name in ((cosx, "cos"), (sinx, "sin")):
                        for i in range(2):
                            src = part(cst, CST, name)[:, i * HD:(i + 1) * HD].unsqueeze(1)
                            then(g.tensor_copy(table[:, 20 * i:20 * i + 20, :],
                                               src.to_broadcast([P, 20, HD])), "rope_tables")
                elif kind == "xs":
                    written(pool, ("tr", 6, b))
                    hi, lo = (xs[:, b % 2, n, b // 2, :] for n in range(2))
                    src = xnT[:, 1, toks(b)]
                    then(g.tensor_copy(hi, src))
                    then(g.tensor_tensor(lo, src, hi, ALU.subtract), "x_split")
                elif kind == "presets1":
                    then(g.memset(vc[:, :, :, :, :, :], 0.0))
                    for rows, a in ((slice(0, 64), 8), (slice(64, 128), 24)):
                        for l in range(2):
                            then(g.memset(vc[rows, l, :, :, :, a:a + 8].rearrange(
                                "p b j r n -> p (b j r) n"), 1.0), "vc_presets")
                elif kind == "presets4":
                    for c in range(CHUNKS[0]):
                        key = ("pv", 0, b, c)
                        pool.wait_ge(prob_used[slot("prob", key)], SLOTS["prob"].turn(key) + 1)
                    then(g.memset(vst[:, tiles(b), :, :], 0.0))
                    for jj in range(2):
                        for t in (2 * b, 2 * b + 1):
                            a = 16 * jj + 8
                            then(g.memset(v4[:, t, :, jj, :, a:a + 8], 1.0), "presets4")

        @block.scalar
        def _(act):
            a = nc.scalar
            counts = {}

            def then(ins, name="act_step"):
                counts[name] = counts.get(name, 0) + 1
                ins.then_inc(sem(name), 1)
                act.wait_ge(sem(name), counts[name])

            def evac(key, out_ap, in_ap, scale=1.0):
                act.wait_ge(psum_full, PSUM.full(key))
                func = ACT.Copy if isinstance(scale, float) else ACT.Identity
                a.activation(out_ap, in_ap, func, scale=scale).then_inc(psum_done[PSUM.slot(key)], 1)

            def stack_evac(step, dst):
                act.wait_ge(psum_full, PSUM.full(step))
                src = psum16(step).rearrange("p (i g t) -> p i g t", i=2, g=4)
                a.activation(dst[:, :, 0:P], src[:, 0], ACT.Copy).then_inc(sem("stack_half"), 1)
                a.activation(dst[:, :, P:T], src[:, 1], ACT.Copy).then_inc(
                    psum_done[PSUM.slot(step)], 1)

            for step in ORDER:
                kind, b = step[0], step[-1]
                if kind == "tr":
                    evac(step, xnT[:, half[step[1]], toks(b)], psum(step)[:, 0:T])
                elif kind == "qkv":
                    act.wait_ge(psum_full, PSUM.full(step))
                    src = two(psum(step)[:, 0:384])
                    a.activation(two(raw[:, b, :, :].rearrange("p h e -> p (h e)")), src[:, :, 0:160],
                                 ACT.Copy).then_inc(sem("raw_ready"), 1)
                    a.activation(rawv[:, b, :, :], src[:, :, 160:192], ACT.Copy).then_inc(
                        psum_done[PSUM.slot(step)], 1)
                elif kind == "ropea":
                    act.wait_ge(sem("raw_ready"), count(("qkv",), ("qkv", b)))
                    last = SLOTS["rope"].before(b)
                    if last is not None:
                        act.wait_ge(sem("rope_done"), count(("ropeb",), last))
                    then(a.activation(sq[:, slot("rope", b)], raw[:, b], ACT.Square), "squares_ready")
                    act.wait_ge(sem("sums_ready"), count(("ropea",), step))
                    then(a.activation(nrm[:, b, :], nrm[:, b, :], ACT.Sqrt), "norms_ready")
                elif kind == "tq0":
                    _, b, i = step
                    evac(step, qT[:, :, (2 * b + i) * P:(2 * b + i + 1) * P],
                         psum16(step)[:, 0:512].rearrange("p (g t) -> p g t", g=4))
                elif kind in ("tq", "tqm"):
                    if step[1] == 5:
                        read_by_tensor(act, "qcT", b)
                        stack_evac(step, qcT[:, slot("qcT", b)])
                    else:
                        stack_evac(step, qT[:, :, toks(b)])
                elif kind == "tk4":
                    n = count(("tk4",), step)
                    if n > 1:
                        act.wait_ge(sem("km4_ready"), 4 * (n - 1))
                    stack_evac(step, kT[:, :, :])
                elif kind == "sc":
                    key = ("pv",) + step[1:]
                    act.wait_ge(psum_full, PSUM.full(step))
                    if SLOTS["prob"].turn(key):
                        act.wait_ge(prob_used[slot("prob", key)], SLOTS["prob"].turn(key))
                    a.activation(probs[:, slot("prob", key), :], psum(step), ACT.Exp,
                                 scale=SCALE).then_inc(psum_done[PSUM.slot(step)], 1)
                elif kind == "oc":
                    _, s, b = step
                    read_by_tensor(act, "copied", (s, b))
                    key = ("pv", s, b, CHUNKS[s] - 1)
                    act.wait_ge(prob_used[slot("prob", key)], SLOTS["prob"].turn(key) + 1)
                    a.activation(copied[:, slot("copied", (s, b)), :], outs[:, slot("out", (s, b)), :],
                                 ACT.Copy).then_inc(out_copied[slot("out", (s, b))], 1)
                elif kind == "ou":
                    _, s, b = step
                    read_by_tensor(act, "yT", (s, b))
                    evac(step, yT[:, slot("yT", (s, b)), :], psum(step)[:, 0:T])
                elif kind == "tr2":
                    evac(step, flatT[:, toks(b)], psum(step)[:, 0:T])
                elif kind == "fup":
                    read_by_tensor(act, "hid0", b)
                    act.wait_ge(psum_full, PSUM.full(step))
                    act.wait_ge(sem("col_loaded"), 16)
                    for n in range(2 * HC):
                        e, c = 2 * step[1] + n // HC, n % HC
                        a.activation(hid0[:, slot("hid0", b), n * P:(n + 1) * P],
                                     psum(step)[:, n * P:(n + 1) * P],
                                     ACT.Gelu, bias=colv("b1", e * HC + c)).then_inc(
                            sem("gelu_part") if n < 2 * HC - 1 else psum_done[PSUM.slot(step)], 1)
                elif kind == "nxa":
                    written(act, step)
                    z = zn[:, slot("zn", b)]
                    then(a.activation(z, z, ACT.Gelu), "gelu_ready")
                elif kind == "tr3":
                    evac(step, xnT[:, 1, toks(b)], psum(step)[:, 0:T], colv("norm_w"))
                elif kind == "p3a":
                    read_by_tensor(act, "mlstm", b)
                    evac(step, qT3[:, slot("mlstm", b), :], psum(step)[0:DH, 0:T], 1.0 / DH)
                elif kind == "p3b":
                    w = slot("mlstm", b)
                    evac(step, v3[:, w, :, 0:DH], two(psum(step)[:, 0:T])[:, :, 0:DH])
                    written(act, step)
                    then(a.activation(og3[:, w], og3[:, w], ACT.Exp, scale=-1.0), "og_exp")
                elif kind == "ml" and step[2] == 0:
                    act.wait_ge(psum_full, PSUM.full(step))
                    then(a.activation(decay[:, slot("mlstm", step[1]), :], psum(step)[:, 0:384],
                                      ACT.Exp), "decay_ready")
                elif kind == "ml" and step[2] == 2:
                    evac(step, h3T[:, slot("mlstm", step[1]), :], psum(step)[0:DH, 0:T])
                elif kind == "ga":
                    act.wait_ge(sem("gate_diff"), count(("ga",), step))
                    then(a.activation(gex[:, tiles(b), 0], gex[:, tiles(b), 0], ACT.Exp), "gate_exp")
                elif kind == "ws":
                    e = step[1]
                    act.wait_ge(sem(f"w1b_loaded{e // 4}"), 16)
                    if e == 0:
                        act.wait_ge(sem("stack_ready"), max(count(STACKS, ("q1", n)) for n in range(NB)))
                        act.wait_ge(sem("x_biased"), max(biased(("lnb", 1, n)) for n in range(NB)))
                        act.wait_ge(sem("col_loaded"), 16)
                        then(a.activation(b1s[:, :], part(col, COL, "b1m"), ACT.Copy, scale=WSCALE),
                             "biases_scaled")
                    else:
                        act.wait_ge(sem("w_split"), e)
                    then(a.activation(w1s[e][:, 0, :], w1[:, e, :], ACT.Copy, scale=WSCALE), "w_high")
                elif kind == "w2s":
                    e = step[1]
                    act.wait_ge(sem(f"w2b_loaded{e // 4}"), 16)
                    act.wait_ge(sem("w_split"), NE if e == 0 else count(("ws", "w2s"), ("w2s", e - 1)))
                    then(a.activation(w2s[e][:, 0].rearrange("p c n -> p (c n)"),
                                      w2[:, e].rearrange("p c n -> p (c n)"), ACT.Copy, scale=WSCALE),
                         "w_high")
                elif kind == "mup":
                    _, h, e, n = step
                    act.wait_ge(sem("biases_scaled"), 1)
                    hidden_free(act, step)
                    act.wait_ge(psum_full, PSUM.full(step))
                    for cc in range(2):
                        c, cols = e * HC + 2 * n + cc, slice(512 * cc, 512 * cc + 512)
                        a.activation(hid0[:, slot("hid0", (h, e, n)), cols], psum(step)[:, cols],
                                     ACT.Relu, bias=b1s[:, c:c + 1]).then_inc(
                            psum_done[PSUM.slot(step)], 1)
                elif kind == "hs":
                    _, h, e, n = step
                    if n == 0:
                        read_by_tensor(act, "hidden", (h, e))
                    written(act, ("mup", h, e, n))
                    dst = hid1[:, slot("hidden", (h, e)), 0, 2 * n:2 * n + 2, :]
                    a.activation(dst.rearrange("p c n -> p (c n)"), hid0[:, slot("hid0", (h, e, n)), :],
                                 ACT.Copy).then_inc(sem("hidden_high"), 1)

        @block.vector
        def _(dve):
            v = nc.vector
            counts = {}

            def then(ins, name="dve_step", wait=True):
                counts[name] = counts.get(name, 0) + 1
                ins.then_inc(sem(name), 1)
                if wait:
                    dve.wait_ge(sem(name), counts[name])

            def gives(key, ins):
                ins.then_inc(psum_done[PSUM.slot(key)], 1)
                written(dve, key)

            def biased_operand(key, name):
                dve.wait_ge(psum_full, PSUM.full(key))
                dve.wait_ge(sem("row_loaded"), 16)
                gives(key, v.tensor_tensor(split[:, :, :], two(psum(key)[:, 0:T]), both(name),
                                           ALU.add))
                return split[:, :, :].rearrange("p i (h e) -> p (i h) e", e=HD)

            def query_stack(dst, key, name):
                q = dst.rearrange("p i h n -> p (i h) n")
                then(v.memset(q[:, :, 24:32], 0.0), wait=False)
                s = biased_operand(key, name)
                then(v.tensor_copy(q[:, :, 0:8], s))
                then(v.tensor_tensor(q[:, :, 8:16], s, q[:, :, 0:8], ALU.subtract), wait=False)
                then(v.tensor_copy(q[:, :, 16:24], q[:, :, 0:8]), "stack_ready")

            def key_stack(dst, key, name):
                q = dst.rearrange("p i h n -> p (i h) n")
                then(v.memset(q[:, :, 26:32], 0.0), wait=False)
                then(v.memset(q[:, :, 24:26], MAXDIV), wait=False)
                s = biased_operand(key, name)
                then(v.tensor_copy(q[:, :, 0:8], s))
                then(v.tensor_tensor(q[:, :, 16:24], s, q[:, :, 0:8], ALU.subtract), wait=False)
                then(v.tensor_copy(q[:, :, 8:16], q[:, :, 0:8]), "stack_ready")

            for step in ORDER:
                kind, b = step[0], step[-1]
                if kind == "lna":
                    s = step[1]
                    h = half[s]
                    if s == 0:
                        dve.wait_ge(sem(f"x_loaded{b}"), 16)
                    t0, t1 = 2 * b, 2 * b + 1
                    then(v.bn_stats(stat[:, h, t0, :], x[:, t0, :]), wait=False)
                    then(v.bn_stats(stat[:, h, t1, :], x[:, t1, :]))
                    then(v.bn_aggr(mv[:, h, t0, :], stat[:, h, t0, :]), wait=False)
                    then(v.bn_aggr(mv[:, h, t1, :], stat[:, h, t1, :]), "var_ready")
                elif kind == "lnb":
                    s = step[1]
                    h = half[s]
                    dve.wait_ge(sem("rstd_ready"), count(("lna",), ("lna", s, b)))
                    for n, dst in enumerate((h, 1 - h) if s in AGAIN else (h,)):
                        for t in tiles_of(b):
                            ins = v.tensor_scalar(xn[:, dst, t, :], x[:, t, :], mv[:, h, t, 0:1],
                                                  rstd[:, h, n, t:t + 1], ALU.subtract, ALU.mult)
                            last = t % 2 and n == (s in AGAIN)
                            then(ins, "xn_ready" if last else "dve_step", wait=bool(last))
                elif kind == "ropea":
                    dve.wait_ge(sem("squares_ready"), count(("ropea",), step))
                    then(v.tensor_reduce(nrm[:, b, :], sq[:, slot("rope", b)], X, ALU.add), "sums_ready")
                elif kind == "ropeb":
                    dve.wait_ge(sem("norms_ready"), count(("ropea",), ("ropea", b)))
                    dve.wait_ge(sem("rope_tables"), 4)
                    s = sq[:, slot("rope", b)]
                    then(v.tensor_scalar(nrm[:, b, :], nrm[:, b, :], 1e-10, None, ALU.add))
                    then(v.reciprocal(nrm[:, b, :], nrm[:, b, :]))
                    then(v.tensor_tensor(s, raw[:, b], nrm[:, b, :].unsqueeze(2).to_broadcast([P, 40, HD]),
                                         ALU.mult))
                    n = count(("ropeb",), step)
                    if n > 1:
                        dve.wait_ge(sem("k0_ready"), n - 1)
                    then(v.tensor_tensor(rot, s, cosx, ALU.mult), wait=False)
                    then(v.tensor_tensor(swp[:, :, 0:4], s[:, :, 4:8], sinx[:, :, 0:4], ALU.mult), wait=False)
                    then(v.tensor_tensor(swp[:, :, 4:8], s[:, :, 0:4], sinx[:, :, 4:8], ALU.mult))
                    then(v.tensor_tensor(rot, rot, swp, ALU.add), "rope_done")
                    read_by_tensor(dve, "stack_q", (0, b))
                    q = qn[:, slot("stack_q", (0, b))]
                    rq = rot.rearrange("p (i h) e -> p i h e", i=2)[:, :, 0:16, :]
                    then(v.tensor_copy(q[:, :, :, 0:8], rq))
                    then(v.tensor_tensor(q[:, :, :, 8:16], rq, q[:, :, :, 0:8], ALU.subtract))
                    then(v.tensor_copy(q[:, :, :, 16:32], q[:, :, :, 0:16]), "stack_ready")
                elif kind == "tq0":
                    _, b, i = step
                    t = 2 * b + i
                    after_scalar(dve, step)
                    m = psum16(step)[:, 512:640].unsqueeze(1).to_broadcast([P, 4, P])
                    v.tensor_tensor(km0[:, :, t * P:(t + 1) * P], m,
                                    rowmask.unsqueeze(2).to_broadcast([P, 4, P]), ALU.mult)\
                        .then_inc(psum_done[PSUM.slot(step)], 1)
                elif kind == "kck":
                    l = b
                    read_by_tensor(dve, "stack_k", ("context", l))
                    key_stack(kn[:, slot("stack_k", ("context", l))], step, {1: "bk1", 4: "bck4"}[l])
                elif kind == "kcv":
                    l = b
                    dve.wait_ge(psum_full, PSUM.full(step))
                    dve.wait_ge(sem("row_loaded"), 16)
                    dve.wait_ge(sem("vc_presets"), 4)
                    bv = bias({1: "bv1", 4: "bcv4"}[l])
                    for n, rows in enumerate((slice(0, 64), slice(64, 128))):
                        for m in range(NB):
                            sel = lambda ap: ap.rearrange("p (j q r e) -> p j q r e", j=2, q=2, r=4)[:, :, n]
                            ins = v.tensor_tensor(vc[rows, l // 4, m, :, :, 16 * n:16 * n + HD],
                                                  sel(psum(step)[rows, m * P:(m + 1) * P]),
                                                  sel(bv[rows, :]), ALU.add)
                            if (n, m) == (1, NB - 1):
                                gives(step, ins)
                            else:
                                then(ins, wait=False)
                elif kind == "kct":
                    dve.wait_ge(psum_full, PSUM.full(step))
                    m = psum16(step).rearrange("p (i g t) -> p i g t", i=2, g=4)
                    for i in range(2):
                        for r in range(4):
                            ins = v.tensor_scalar(kcm[:, r, :, i * P:(i + 1) * P], m[:, i],
                                                  rowmask[:, r:r + 1], None, ALU.mult)
                            if (i, r) == (1, 3):
                                gives(step, ins)
                            else:
                                then(ins, wait=False)
                elif kind == "ot":
                    _, s, b = step
                    dve.wait_ge(psum_full, PSUM.full(step))
                    ps = psum(step).rearrange("p (h n) -> p h n", n=16)
                    then(v.reciprocal(sums[:, :], ps[:, :, HD]))
                    if s == 4:
                        dst = y4[:, slot("y4", b)]
                    else:
                        read_by_tensor(dve, "y", (s, b))
                        dst = y[:, slot("y", (s, b))]
                    gives(step, v.tensor_tensor(
                        dst.rearrange("p i (h e) -> p (i h) e", e=HD), ps[:, :, 0:HD],
                        sums[:, :].unsqueeze(2).to_broadcast([P, 2 * H, HD]), ALU.mult))
                    if s == 5:
                        then(v.tensor_tensor(dst, dst, y4[:, slot("y4", b)], ALU.add), "y_added")
                elif kind == "op" or kind == "ml" and step[2] == 3:
                    b = step[2] if kind == "op" else step[1]
                    dve.wait_ge(psum_full, PSUM.full(step))
                    before = {("op", 1): ("lnb", 1, b), ("op", 5): ("lnb", 4, b),
                              ("ml", b): ("lnb", 3, b)}.get(step[:2])
                    if before:
                        dve.wait_ge(sem("x_biased"), biased(before))
                    gives(step, v.tensor_tensor(x[:, tiles(b), :], x[:, tiles(b), :],
                                                two(psum(step)[:, 0:T]), ALU.add))
                elif kind == "q1":
                    read_by_tensor(dve, "stack_q", (1, b))
                    query_stack(qn[:, slot("stack_q", (1, b))], step, "bq1")
                elif kind == "q4":
                    read_by_tensor(dve, "stack_q", (4, b))
                    query_stack(qn[:, slot("stack_q", (4, b))], step, "bq4")
                elif kind == "qc4":
                    read_by_tensor(dve, "stack_c", (5, b))
                    query_stack(qcn[:, slot("stack_c", (5, b))], step, "bcq4")
                elif kind == "k4":
                    read_by_tensor(dve, "stack_k", (4, b))
                    key_stack(kn[:, slot("stack_k", (4, b))], step, "bk4")
                elif kind == "tk4":
                    written(dve, step)
                    read_by_tensor(dve, "km4", b)
                    for r in range(4):
                        then(v.tensor_scalar(km4[:, slot("km4", b), r, :, :], kT[:, :, :],
                                             rowmask[:, r:r + 1], None, ALU.mult), "km4_ready",
                             wait=False)
                elif kind == "v4":
                    dve.wait_ge(psum_full, PSUM.full(step))
                    dve.wait_ge(sem("presets4"), 4 * count(("presets4",), ("presets4", b)))
                    for i in range(2):
                        for jj in range(2):
                            sel = lambda ap: ap.rearrange("p (j q r e) -> p j q r e", j=2, q=2, r=4)[:, :, jj]
                            ins = v.tensor_tensor(v4[:, 2 * b + i, :, jj, :, 16 * jj:16 * jj + HD],
                                                  sel(psum(step)[:, i * P:(i + 1) * P]),
                                                  sel(bias("bv4")), ALU.add)
                            if i == jj == 1:
                                gives(step, ins)
                            else:
                                then(ins, wait=False)
                elif kind == "mxc":
                    _, s, b, i = step
                    dve.wait_ge(psum_full, PSUM.full(step))
                    gives(step, v.tensor_reduce(
                        mxc[:, slot("mxc", (s, b)), i, :],
                        psum(step).rearrange("p (h k) -> p h k", k=KV), X, ALU.max))
                elif kind == "mxs":
                    _, b, c = step
                    dve.wait_ge(psum_full, PSUM.full(step))
                    w = slot("mx", b)
                    if c < 2:
                        dst, k = mx[:, w, 0, 8 * c:8 * c + 8], P
                    else:
                        dst, k = mx[:, w, 1, 4 * (c - 2):4 * (c - 2) + 4], T
                    gives(step, v.tensor_reduce(
                        dst, psum(step).rearrange("p (h k) -> p h k", k=k), X, ALU.max))
                elif kind == "mxe":
                    _, s, b = step
                    m = mx[:, slot("mx", b)] if s == 4 else mxc[:, slot("mxc", (s, b))]
                    m = m.rearrange("p i h -> p (i h)")
                    q = qcn[:, slot("stack_c", (5, b))] if s == 5 else qn[:, slot("stack_q", (s, b))]
                    q = q.rearrange("p i h n -> p (i h) n")
                    then(v.tensor_scalar(m, m, -1.0 / MAXDIV, None, ALU.mult))
                    then(v.tensor_copy(q[:, :, 24], m))
                    then(v.tensor_tensor(q[:, :, 25], m, q[:, :, 24], ALU.subtract), "max_ready")
                elif kind == "tr2":
                    after_scalar(dve, step)
                    dve.wait_ge(sem("col_loaded"), 16)
                    gives(step, v.tensor_scalar(n2T[:, toks(b)], psum(step)[:, T:2 * T],
                                                colv("ln_scale"), colv("ln_bias"), ALU.mult, ALU.add))
                elif kind == "xa":
                    dve.wait_ge(psum_full, PSUM.full(step))
                    gives(step, v.scalar_tensor_tensor(xaT[:, toks(b)], psum(step)[:, 0:T],
                                                       colv("attn_b"), flatT[:, toks(b)],
                                                       ALU.add, ALU.add))
                elif kind == "fdown":
                    dve.wait_ge(psum_full, PSUM.full(step))
                    for n in range(2):
                        e = 2 * step[1] + n
                        ins = v.tensor_scalar(experts(eoT, e), psum(step)[:, n * P:(n + 1) * P]
                                              .rearrange("p (m t) -> p m t", m=2),
                                              colv("b2", e), None, ALU.add)
                        if n == 0:
                            then(ins, wait=False)
                        else:
                            gives(step, ins)
                elif kind == "nxa":
                    dve.wait_ge(psum_full, PSUM.full(step))
                    gives(step, v.tensor_tensor(zn[:, slot("zn", b)], two(psum(step)[:, 0:T]),
                                                both("next_b"), ALU.add))
                elif kind == "nxb":
                    dve.wait_ge(sem("gelu_ready"), count(("nxa",), ("nxa", b)))
                    then(v.tensor_tensor(x[:, tiles(b), :], x[:, tiles(b), :], zn[:, slot("zn", b)],
                                         ALU.add))
                elif kind == "p3a":
                    read_by_tensor(dve, "mlstm", b)
                    after_scalar(dve, step)
                    dve.wait_ge(sem("gate_bias_loaded"), 16)
                    w, ps = slot("mlstm", b), psum(step)
                    for n in range(2):
                        then(v.tensor_scalar(zif[w][:, n * T:(n + 1) * T], ps[gate_row, n * T:(n + 1) * T],
                                             gate_bias[gate_row, n:n + 1], None, ALU.add), wait=False)
                    gives(step, v.tensor_copy(kT3[:, w, :], ps[0:DH, T:2 * T]))
                elif kind == "p3b":
                    w = slot("mlstm", b)
                    then(v.memset(v3[:, w, :, DH:DH + 1], 1.0), "v3_ones", wait=False)
                    after_scalar(dve, step)
                    gives(step, v.tensor_tensor(og3[:, w], two(psum(step)[:, 0:T])[:, :, DH:2 * DH],
                                                bias("bo3").unsqueeze(1).to_broadcast([P, 2, DH]),
                                                ALU.add))
                elif kind == "rows":
                    dve.wait_ge(sem("rope_tables"), 4)
                    w = slot("mlstm", b)
                    zi, zf = zif[w][:, 0:T], zif[w][:, T:2 * T]
                    then(v.tensor_tensor_scan(cumf, one_row, zf, 0.0, ALU.mult, ALU.add))
                    then(v.tensor_tensor(rowa[:, w, :], zi, cumf, ALU.subtract))
                    then(v.tensor_tensor_scan(cumf, rowa[:, w, :], rowa[:, w, :], -3.0e38,
                                              ALU.max, ALU.max))
                    then(v.tensor_scalar(rowg[:, w, :], cumf, -1.0, None, ALU.mult), "rows_ready")
                elif kind == "ml" and step[2] == 0:
                    b = step[1]
                    w = slot("mlstm", b)
                    dve.wait_ge(sem("decay_ready"), sum(
                        1 for s in ORDER[:INDEX[step] + 1] if s[0] == "ml" and s[2] == 0))
                    gives(step, v.tensor_tensor(weight[:, w, :], decay[:, w, :],
                                                       psum(step)[:, 512:896], ALU.mult))
                elif kind == "ml" and step[2] == 1:
                    b = step[1]
                    w = slot("mlstm", b)
                    dve.wait_ge(sem("og_exp"), count(("p3b",), ("p3b", b)))
                    o = og3[:, w]
                    then(v.tensor_scalar(o, o, 1.0, None, ALU.add))
                    then(v.reciprocal(o, o), wait=False)
                    dve.wait_ge(psum_full, PSUM.full(step))
                    ps = psum(step)[:, 0:2 * (DH + 1)].rearrange("p (i n) -> p i n", i=2)
                    then(v.tensor_scalar(den3, ps[:, :, DH], -1.0, None, ALU.mult))
                    then(v.tensor_tensor(den3, den3, ps[:, :, DH], ALU.max))
                    then(v.tensor_scalar(den3, den3, 1.0, None, ALU.max))
                    then(v.reciprocal(den3, den3))
                    for i in range(2):
                        ins = v.scalar_tensor_tensor(h3[:, w, i, :], ps[:, i, 0:DH], den3[:, i:i + 1],
                                                     og3[:, w, i, :], ALU.mult, ALU.mult)
                        if i == 0:
                            then(ins, wait=False)
                        else:
                            gives(step, ins)
                elif kind == "ga":
                    dve.wait_ge(psum_full, PSUM.full(step))
                    gives(step, v.tensor_copy(gl[:, tiles(b), :], two(psum(step)[:, 0:2 * NE])))
                    t0, t1 = 2 * b, 2 * b + 1
                    then(v.max(top[:, t0, :], gl[:, t0, :]), wait=False)
                    then(v.max(top[:, t1, :], gl[:, t1, :]))
                    then(v.tensor_tensor(gex[:, tiles(b), 0], top[:, tiles(b), 1], top[:, tiles(b), 0],
                                         ALU.subtract), "gate_diff", wait=False)
                    then(v.max_index(topi[:, t0, :], top[:, t0, :], gl[:, t0, :]), wait=False)
                    then(v.max_index(topi[:, t1, :], top[:, t1, :], gl[:, t1, :]))
                    then(v.tensor_copy(topf[:, tiles(b), :], topi[:, tiles(b), 0:2]))
                elif kind == "gb":
                    dve.wait_ge(sem("gate_exp"), count(("ga",), ("ga", b)))
                    e, w = gex[:, tiles(b), 0], gex[:, tiles(b), 1]
                    then(v.tensor_scalar(w, e, WSCALE ** 2, WSCALE ** 2, ALU.mult, ALU.add))
                    then(v.reciprocal(w, w))
                    then(v.tensor_tensor(e, e, w, ALU.mult))
                    iota = part(cst, CST, "iota")
                    for i in range(2):
                        t = 2 * b + i
                        then(v.tensor_scalar(comb[:, t, :], iota, topf[:, t, 0:1], gex[:, t, 1:2],
                                             ALU.is_equal, ALU.mult), wait=False)
                        then(v.tensor_scalar(gtmp[:, i, :], iota, topf[:, t, 1:2], gex[:, t, 0:1],
                                             ALU.is_equal, ALU.mult), wait=i == 1)
                    then(v.tensor_tensor(comb[:, tiles(b), :], comb[:, tiles(b), :], gtmp[:, :, :],
                                         ALU.add), "comb_ready")
                elif kind == "gc":
                    dve.wait_ge(psum_full, PSUM.full(step))
                    read_by_tensor(dve, "combT", b)
                    gives(step, v.tensor_scalar(combT[:, :], psum(step)[0:NE, 0:T], WSCALE ** 2, None,
                                                ALU.mult))
                elif kind == "gd":
                    dve.wait_ge(psum_full, PSUM.full(step))
                    gives(step, v.tensor_tensor(x[:, tiles(b), :], x[:, tiles(b), :],
                                                two(psum(step)[:, 0:T]), ALU.add))
                elif kind == "ws":
                    e = step[1]
                    dve.wait_ge(sem("w_high"), e + 1)
                    then(v.scalar_tensor_tensor(w1s[e][:, 1, :], w1[:, e, :], WSCALE, w1s[e][:, 0, :],
                                                ALU.mult, ALU.subtract), "w_split", wait=False)
                elif kind == "casts":
                    dve.wait_ge(sem("cst_loaded"), 16)
                    then(v.tensor_copy(ident16[:, :], ident), "ident16_ready", wait=False)
                    then(v.tensor_copy(identb[:, :], ident), wait=False)
                    for name, dst in (("causal_nat", causal_nat), ("causal_tr", causal_tr)):
                        then(v.tensor_copy(dst[:, :], part(cst, CST, name)), "masks_ready")
                elif kind == "w2s":
                    e = step[1]
                    dve.wait_ge(sem("w_high"), count(("ws", "w2s"), step))
                    flat = lambda ap: ap.rearrange("p c n -> p (c n)")
                    then(v.scalar_tensor_tensor(flat(w2s[e][:, 1]), flat(w2[:, e]), WSCALE,
                                                flat(w2s[e][:, 0]), ALU.mult, ALU.subtract),
                         "w_split", wait=False)
                elif kind == "hs":
                    _, h, e, n = step
                    dve.wait_ge(sem("hidden_high"), count(("hs",), step))
                    hid = hid1[:, slot("hidden", (h, e)), :, 2 * n:2 * n + 2, :]
                    then(v.tensor_tensor(hid[:, 1].rearrange("p c n -> p (c n)"),
                                         hid0[:, slot("hid0", (h, e, n)), :],
                                         hid[:, 0].rearrange("p c n -> p (c n)"), ALU.subtract),
                         "hidden_low", wait=False)
                elif kind == "mdown":
                    _, h, e = step
                    dve.wait_ge(psum_full, PSUM.full(step))
                    for i in range(4):
                        t = 2 * PAIRS[h][i // 2] + i % 2
                        ins = v.scalar_tensor_tensor(x[:, t, :], psum(step)[:, i * P:(i + 1) * P],
                                                     comb[:, t, e:e + 1], x[:, t, :], ALU.mult, ALU.add)
                        if i < 3:
                            then(ins, wait=False)
                        else:
                            gives(step, ins)

        @block.tensor
        def _(pe):
            mm = nc.tensor.matmul

            def take(key):
                if PSUM.before(key):
                    pe.wait_ge(psum_done[PSUM.slot(key)], PSUM.before(key))
                return psum(key)

            def transposes(dst, blocks, identity):
                for n, blk in enumerate(blocks):
                    ins = nc.tensor.transpose(dst[:, n * P:(n + 1) * P], blk, identity)
                ins.then_inc(psum_full, 1)

            def natural(key, lhsTs, rhs):
                dst = take(key)
                n = rhs.shape[-1]
                for i, l in enumerate(lhsTs):
                    ins = mm(dst[:, i * n:(i + 1) * n], l, rhs, start=True, stop=True)
                ins.then_inc(psum_full, 1)

            tile_cols = lambda ap, b: [ap[:, (2 * b + i) * P:(2 * b + i + 1) * P] for i in range(2)]

            def stacked(step, buf, made):
                pe.wait_ge(sem("ident16_ready"), 1)
                pe.wait_ge(sem("stack_ready"), count(STACKS, made))
                take(step)
                transposes(psum16(step),
                           [buf[:, i, 4 * B:4 * B + 4, :].rearrange("p h n -> p (h n)")
                            for i in range(2) for B in range(4)], ident16[:, :])

            masks = lambda m, n: m[:, :].unsqueeze(1).to_broadcast([P, n, P])

            def self_scores(step):
                _, s, b, c = step
                kind, n = SELF_CHUNKS[c]
                if s == 0:
                    for i in range(2):
                        written(pe, ("tq0", b, i))
                    keys = lambda r, B, kt: km0[:, r, (2 * b + kt) * P:(2 * b + kt + 1) * P]
                else:
                    pe.wait_ge(sem("masks_ready"), 2)
                    written(pe, ("tqm", 4, b))
                    w = slot("km4", b)
                    keys = lambda r, B, kt: km4[:, w, r, B, kt * P:(kt + 1) * P]
                dst = take(step)
                if kind == "k0":
                    for r in range(4):
                        o = dst[:, r * T:(r + 1) * T]
                        ins = mm(o, keys(r, n, 0), qT[:, n, toks(b)], start=True, stop=s == 0)
                        if s:
                            ins = mm(o[:, 0:P], identb[:, :], causal_tr[:, :], start=False, stop=True)
                else:
                    for q in range(2):
                        if s:
                            mm(dst[:, q * 512:(q + 1) * 512].rearrange("p (r t) -> p r t", r=4),
                               identb[:, :], masks(causal_tr, 4), start=True, stop=False)
                        for r in range(4):
                            o = dst[:, q * 512 + r * P:q * 512 + (r + 1) * P]
                            ins = mm(o, keys(r, 2 * n + q, 1), qT[:, 2 * n + q, b * T + P:(b + 1) * T],
                                     start=s == 0, stop=s == 0 or r == 3)
                ins.then_inc(psum_full, 1)

            def cross_scores(step):
                _, s, b, J = step
                written(pe, ("tqm", s, b))
                dst = take(step)
                q = qT[:, :, toks(b)] if s == 1 else qcT[:, slot("qcT", b)]
                for r in range(4):
                    for jj in range(2):
                        ins = mm(dst[64 * jj:64 * jj + 64, r * T:(r + 1) * T],
                                 kcm[:, r, 2 * J + jj, b * KV:(b + 1) * KV], q[:, 2 * J + jj, :],
                                 start=True, stop=True)
                ins.then_inc(psum_full, 1)

            def weighted_values(step):
                _, s, b, c = step
                dst = outs[:, slot("out", (s, b)), :]
                pr = probs[:, slot("prob", step), :]
                if c == 0 and SLOTS["out"].turn((s, b)):
                    pe.wait_ge(out_copied[slot("out", (s, b))], SLOTS["out"].turn((s, b)))
                if s == 0:
                    n = sum(1 for t in ORDER[:INDEX["sc", s, b, c] + 1] if t[:2] == ("sc", 0))
                    pe.wait_ge(sem("prob_masked"), n)
                    pe.wait_ge(sem("v0_ready"), 4 * count(("ropeb",), ("ropeb", b)))
                else:
                    written(pe, ("sc", s, b, c))
                if s in (1, 5):
                    written(pe, ("kcv", 1 if s == 1 else 4))
                    for r in range(4):
                        ins = mm(dst[32 * r:32 * r + 32, c * T:(c + 1) * T], vc[:, s // 4, b, c, r, :],
                                 pr[:, r * T:(r + 1) * T], start=True, stop=True)
                else:
                    if s == 4:
                        written(pe, ("v4", b))
                    kind, n = SELF_CHUNKS[c]
                    vals = lambda r, B, kt: (v0[:, 2 * b + kt, r, B % 2, :] if s == 0 else
                                             vst[:, 2 * b + kt, 4 * B + r, :])
                    if kind == "k0":
                        for r in range(4):
                            ins = mm(dst[32 * r:32 * r + 32, n // 2 * T:(n // 2 + 1) * T],
                                     vals(r, n, 0), pr[:, r * T:(r + 1) * T],
                                     start=n % 2 == 0, stop=False)
                    else:
                        for q in range(2):
                            for r in range(4):
                                ins = mm(dst[32 * r:32 * r + 32, n * T + P:(n + 1) * T],
                                         vals(r, 2 * n + q, 1),
                                         pr[:, (4 * q + r) * P:(4 * q + r + 1) * P],
                                         start=False, stop=q == 1)
                ins.then_inc(prob_used[slot("prob", step)], 1)

            pe.wait_ge(sem("cst_loaded"), 16)
            for step in ORDER:
                kind, b = step[0], step[-1]
                if kind == "tr":
                    pe.wait_ge(sem("xn_ready"), count(("lnb",), ("lnb", step[1], b)))
                    transposes(take(step), [xn[:, half[step[1]], 2 * b + i, :]
                                                 for i in range(2)], ident)
                elif kind == "qkv":
                    pe.wait_ge(sem("wa_loaded"), 16)
                    written(pe, ("tr", 0, b))
                    natural(step, tile_cols(xnT[:, 0, :], b), part(wa, WA, "qkv"))
                elif kind == "tq0":
                    _, b, i = step
                    pe.wait_ge(sem("ident16_ready"), 1)
                    pe.wait_ge(sem("stack_ready"), count(STACKS, ("ropeb", b)))
                    pe.wait_ge(sem("k0_ready"), count(("ropeb",), ("ropeb", b)))
                    q, k = qn[:, slot("stack_q", (0, b)), i], kn[:, slot("stack_k", (0, b)), i]
                    take(step)
                    transposes(psum16(step),
                               [q[:, 4 * B:4 * B + 4, :].rearrange("p h n -> p (h n)") for B in range(4)] +
                               [k[:, 0:4, :].rearrange("p h n -> p (h n)")], ident16[:, :])
                elif kind == "kck":
                    pe.wait_ge(sem("w64_loaded"), 16)
                    natural(step, tile_cols(W6("ctx"), 0), W6({1: "wk1", 4: "wck4"}[b]))
                elif kind == "kcv":
                    pe.wait_ge(sem("w64_loaded"), 16)
                    natural(step, [W6("ctx2")[:, n * P:(n + 1) * P] for n in range(NB)],
                            W6({1: "wv1", 4: "wcv4"}[b]))
                elif kind == "kct":
                    stacked(step, kn[:, slot("stack_k", ("context", b))], ("kck", b))
                elif kind == "sc":
                    if step[1] in (0, 4):
                        self_scores(step)
                    else:
                        cross_scores(step)
                elif kind == "pv":
                    weighted_values(step)
                elif kind == "ot":
                    _, s, b = step
                    pe.wait_ge(out_copied[slot("out", (s, b))], SLOTS["out"].turn((s, b)) + 1)
                    c = copied[:, slot("copied", (s, b)), :]
                    transposes(take(step), [c[:, J * T + i * P:J * T + (i + 1) * P]
                                                 for i in range(2) for J in range(2)], ident)
                elif kind == "ou":
                    _, s, b = step
                    written(pe, ("ot", s, b))
                    if s == 5:
                        pe.wait_ge(sem("y_added"), sum(1 for t in ORDER[:INDEX["ot", s, b] + 1]
                                                       if t[:2] == ("ot", 5)))
                    transposes(take(step), [y[:, slot("y", (s, b)), i, :] for i in range(2)], ident)
                elif kind == "op":
                    _, s, b = step
                    written(pe, ("ou", s, b))
                    if s:
                        pe.wait_ge(sem("wb_loaded"), 16)
                    w = yT[:, slot("yT", (s, b)), :]
                    natural(step, [w[:, i * P:(i + 1) * P] for i in range(2)],
                            part(wa, WA, "wo0") if s == 0 else W({1: "wo1", 5: "wp4"}[s]))
                elif kind in ("q1", "q4", "k4", "qc4", "v4"):
                    s = 1 if kind == "q1" else 4
                    pe.wait_ge(sem("wb_loaded"), 16)
                    written(pe, ("tr", s, b))
                    w = {"q1": "wq1", "q4": "wq4", "k4": "wk4", "qc4": "wcq4", "v4": "wv4"}[kind]
                    natural(step, tile_cols(xnT[:, half[s], :], b), W(w))
                elif kind in ("tq", "tqm"):
                    _, s, b = step
                    if kind == "tqm":
                        pe.wait_ge(sem("max_ready"), count(("mxe",), ("mxe", s, b)))
                    buf = qcn[:, slot("stack_c", (5, b))] if s == 5 else qn[:, slot("stack_q", (s, b))]
                    stacked(step, buf, ({1: "q1", 4: "q4", 5: "qc4"}[s], b))
                elif kind == "tk4":
                    stacked(step, kn[:, slot("stack_k", (4, b))], ("k4", b))
                elif kind == "mxc":
                    _, s, b, i = step
                    written(pe, ("tq", s, b))
                    written(pe, ("kct", 1 if s == 1 else 4))
                    dst = take(step)
                    q = (qT[:, :, toks(b)] if s == 1 else qcT[:, slot("qcT", b)])[:, :, i * P:(i + 1) * P]
                    for B in range(4):
                        ins = mm(dst[:, B * T:(B + 1) * T], q[:, B, :],
                                 kcm[:, :, B, b * KV:(b + 1) * KV], start=True, stop=True)
                    ins.then_inc(psum_full, 1)
                elif kind == "mxs":
                    _, b, c = step
                    pe.wait_ge(sem("masks_ready"), 2)
                    written(pe, ("tq", 4, b))
                    pe.wait_ge(sem("km4_ready"), 4 * count(("tk4",), ("tk4", b)))
                    dst, w = take(step), slot("km4", b)
                    for n in range(2):
                        o = dst[:, n * 512:(n + 1) * 512]
                        if c < 2:
                            B = 2 * c + n
                            mm(o.rearrange("p (r k) -> p r k", r=4), identb[:, :],
                               masks(causal_nat, 4), start=True, stop=False)
                            ins = mm(o, qT[:, B, b * T:b * T + P], km4[:, w, :, B, 0:P],
                                     start=False, stop=True)
                        else:
                            B = c - 2
                            mm(o, qT[:, B, b * T + P:(b + 1) * T], km4[:, w, 2 * n:2 * n + 2, B, :],
                               start=True, stop=False)
                            ins = mm(o.rearrange("p (r k) -> p r k", r=2)[:, :, P:T], identb[:, :],
                                     masks(causal_nat, 2), start=False, stop=True)
                    ins.then_inc(psum_full, 1)
                elif kind == "tr2":
                    pe.wait_ge(sem("xn_ready"), count(("lnb",), ("lnb", 2, b)))
                    transposes(take(step), [xn[:, n, 2 * b + i, :] for n in range(2)
                                                 for i in range(2)], ident)
                elif kind == "xa":
                    written(pe, ("tr2", b))
                    mm(take(step)[:, 0:T], W("attn_w"), n2T[:, toks(b)], start=True, stop=True)\
                        .then_inc(psum_full, 1)
                elif kind == "fup":
                    j = step[1]
                    for n in PAIRS[j // 2]:
                        written(pe, ("xa", n))
                    pe.wait_ge(sem(f"w1a_loaded{j // 2}"), 16)
                    dst = take(step)
                    for n in range(2 * HC):
                        e, c = 2 * j + n // HC, n % HC
                        ins = mm(dst[:, n * P:(n + 1) * P], w1[:, e, c * P:(c + 1) * P],
                                 experts(xaT, e), start=True, stop=True)
                    ins.then_inc(psum_full, 1)
                elif kind == "fdown":
                    j = step[1]
                    written(pe, ("fup", j))
                    pe.wait_ge(sem(f"w2a_loaded{j // 2}"), 16)
                    dst = take(step)
                    for n in range(2):
                        for c in range(HC):
                            ins = mm(dst[:, n * P:(n + 1) * P], w2[:, 2 * j + n, c, :],
                                     hid0[:, slot("hid0", j), (n * HC + c) * P:(n * HC + c + 1) * P], start=c == 0, stop=c == HC - 1)
                    ins.then_inc(psum_full, 1)
                elif kind == "nxa":
                    for n in range(2):
                        written(pe, ("fdown", 2 * (b % 2) + n))
                    natural(step, tile_cols(eoT, b), W("next_w"))
                elif kind == "tr3":
                    pe.wait_ge(sem("xn_ready"), count(("lnb",), ("lnb", 3, b)))
                    transposes(take(step), [xn[:, 0, 2 * b + i, :] for i in range(2)], ident)
                elif kind == "p3a":
                    written(pe, ("tr3", b))
                    dst = take(step)
                    for n, w in enumerate(("wqi3", "wkf3")):
                        ins = mm(dst[0:DH + 1, n * T:(n + 1) * T], W(w), xnT[:, 1, toks(b)],
                                 start=True, stop=True)
                    ins.then_inc(psum_full, 1)
                elif kind == "p3b":
                    written(pe, ("tr3", b))
                    natural(step, tile_cols(xnT[:, 1, :], b), W("wvo3"))
                elif kind == "ml" and step[2] == 0:
                    b = step[1]
                    w = slot("mlstm", b)
                    pe.wait_ge(sem("rows_ready"), count(("rows",), ("rows", b)))
                    pe.wait_ge(sem("masks_ready"), 2)
                    written(pe, ("p3a", b))
                    dst = take(step)
                    for kt, (at, n) in enumerate(((0, T), (T, P))):
                        o, ts = dst[:, at:at + n], slice(T - n, T)
                        mm(o, rowa[:, w, kt * P:(kt + 1) * P], one_row[:, 0:n], start=True, stop=False)
                        mm(o, one_row[:, 0:P], rowg[:, w, ts], start=False, stop=False)
                        mm(o[:, 0:P], identb[:, :], causal_tr[:, :], start=False, stop=True)
                        ins = mm(dst[:, 512 + at:512 + at + n], kT3[:, w, kt * P:(kt + 1) * P],
                                 qT3[:, w, ts], start=True, stop=True)
                    ins.then_inc(psum_full, 1)
                elif kind == "ml" and step[2] == 1:
                    b = step[1]
                    s3 = slot("mlstm", b)
                    written(pe, ("ml", b, 0))
                    written(pe, ("p3b", b))
                    pe.wait_ge(sem("v3_ones"), count(("p3b",), ("p3b", b)))
                    dst, w, n = take(step), weight[:, s3, :], DH + 1
                    mm(dst[:, 0:n], w[:, 0:P], v3[:, s3, 0, :], start=True, stop=True)
                    mm(dst[:, n:2 * n], w[:, P:T], v3[:, s3, 0, :], start=True, stop=False)
                    mm(dst[:, n:2 * n], w[:, T:T + P], v3[:, s3, 1, :], start=False, stop=True)\
                        .then_inc(psum_full, 1)
                elif kind == "ml" and step[2] == 2:
                    b = step[1]
                    written(pe, ("ml", b, 1))
                    dst = take(step)
                    for i in range(2):
                        ins = nc.tensor.transpose(dst[0:DH, i * P:(i + 1) * P],
                                                  h3[:, slot("mlstm", b), i, :], ident)
                    ins.then_inc(psum_full, 1)
                elif kind == "ml":
                    b = step[1]
                    written(pe, ("ml", b, 2))
                    natural(step, [h3T[:, slot("mlstm", b), i * P:(i + 1) * P] for i in range(2)],
                            W6("wout3"))
                elif kind == "ga":
                    written(pe, ("tr", 6, b))
                    natural(step, tile_cols(xnT[:, 1, :], b), W("gate"))
                elif kind == "gc":
                    pe.wait_ge(sem("comb_ready"), count(("gb",), ("gb", b)))
                    dst = take(step)
                    for i in range(2):
                        ins = nc.tensor.transpose(dst[0:NE, i * P:(i + 1) * P], comb[:, 2 * b + i, :], ident)
                    ins.then_inc(psum_full, 1)
                elif kind == "gd":
                    pe.wait_ge(sem("b2m_loaded"), 16)
                    written(pe, ("gc", b))
                    natural(step, [combT[:, i * P:(i + 1) * P] for i in range(2)], b2m[:, :])
                elif kind == "mup":
                    _, h, e, n = step
                    for b in PAIRS[h]:
                        pe.wait_ge(sem("x_split"), count(("xs",), ("xs", b)))
                    pe.wait_ge(sem("w_split"), e + 1)
                    dst = take(step)
                    for cc in range(2):
                        c = 2 * n + cc
                        for k, (ws, x_part) in enumerate(((0, 0), (0, 1), (1, 0))):
                            ins = mm(two(dst[:, cc * 512:(cc + 1) * 512]),
                                     w1s[e][:, ws, c * P:(c + 1) * P], xs[:, h, x_part],
                                     start=k == 0, stop=k == 2)
                    ins.then_inc(psum_full, 1)
                elif kind == "mdown":
                    _, h, e = step
                    pe.wait_ge(sem("hidden_high"), count(("hs",), ("hs", h, e, 1)))
                    pe.wait_ge(sem("hidden_low"), count(("hs",), ("hs", h, e, 1)))
                    pe.wait_ge(sem("w_split"), count(("ws", "w2s"), ("w2s", e)))
                    dst, w = take(step), slot("hidden", (h, e))
                    for i in range(4):
                        for c in range(HC):
                            for k, (part_h, part_w) in enumerate(((0, 0), (0, 1), (1, 0))):
                                ins = mm(dst[:, i * P:(i + 1) * P],
                                         hid1[:, w, part_h, c, i * P:(i + 1) * P],
                                         w2s[e][:, part_w, c, :], start=c == k == 0,
                                         stop=c == HC - 1 and k == 2)
                    ins.then_inc(psum_full, 1)



def constants():
    import numpy as np

    p = np.arange(P)
    c = np.zeros((P, CST["all"][1]), np.float32)

    def put(name, value):
        a, n = CST[name]
        c[:, a:a + n] = value

    put("ident", np.eye(P))
    put("causal_nat", np.where(p[None, :] > p[:, None], -1e30, 0))
    put("causal_tr", np.where(p[:, None] > p[None, :], -1e30, 0))
    put("rowmask", p[:, None] // 32 == np.arange(4)[None, :])
    put("iota", np.broadcast_to(np.arange(NE), (P, NE)))
    half = HD // 2
    inv = (1.0 / np.float32(10000.0) ** (np.arange(half, dtype=np.float32) / half)).astype(np.float32)
    ang = np.arange(T, dtype=np.float32)[:, None] * inv[None, :]
    cos, sin = np.cos(ang), np.sin(ang)
    for name, t in (("cos", np.concatenate([cos, cos], 1)), ("sin", np.concatenate([-sin, sin], 1))):
        put(name, t.reshape(2, P, HD).transpose(1, 0, 2).reshape(P, 2 * HD))
    return c


def ordered(w, head_of):
    import numpy as np

    w = w.reshape(H, HD, P)
    return np.concatenate([w[head_of(2 * J + jj, r)] for J in range(2) for r in range(4)
                           for jj in range(2)], 0)


def kernel(**inputs):
    import numpy as np
    import concourse.bacc as bacc
    from concourse.bass_utils import run_bass_kernel_spmd

    g = {k: np.asarray(v) for k, v in inputs.items()}
    wqkv = g["L0_attn_w_qkv"]
    wq = wqkv[:, 0:P].reshape(P, 4, 4, HD).transpose(0, 2, 1, 3).reshape(P, P)
    row1 = lambda n: g[n].reshape(1, -1)
    ctx = g["ctx_512"].transpose(2, 0, 1)
    w1 = lambda w: np.ascontiguousarray(w.transpose(1, 0, 2))
    w2 = lambda w: np.ascontiguousarray(w.reshape(NE, HC, P, P).transpose(2, 0, 1, 3))
    arrays = {
        "x": g["x"],
        "cst": constants(),
        "wa": np.concatenate([wq, wqkv[:, P:], ordered(g["L0_attn_w_o"], lambda B, r: 4 * r + B)], 1),
        "wb": np.concatenate([
            g["L0_xattn_Wq"], ordered(g["L0_xattn_Wo"], lambda B, r: 4 * B + r),
            g["L0_ffn_attn_w"].T, g["L0_ffn_next_w"].T, g["L1_attn_Wq"].T, g["L1_attn_wi_w"].T,
            g["L1_attn_Wk"].T, g["L1_attn_wf_w"].T, g["L1_attn_Wv"].T, g["L1_attn_Wo"].T,
            g["L1_xattn_Wk"], g["L1_xattn_Wq"], g["L1_xattn_Wv"], g["L1_xattn_Wcq"],
            ordered(g["L1_xattn_Wp"], lambda B, r: 4 * B + r), g["L1_ffn_gate_w"].T], 1),
        "w64": np.concatenate([
            g["L0_xattn_Wk"], g["L0_xattn_Wv"], g["L1_xattn_Wck"], g["L1_xattn_Wcv"],
            g["L1_attn_Wout"].T, ctx.reshape(64, NB * KV),
            np.stack([ctx, ctx], 2).reshape(64, NB * 2 * KV)], 1),
        "col": np.concatenate([
            row1("L0_ffn_ln_scale"), row1("L0_ffn_ln_bias"), row1("L0_ffn_attn_b"), g["L0_ffn_b2"],
            g["L0_ffn_b1"].reshape(NE * HC, P), row1("L1_attn_norm_w"),
            g["L1_ffn_b1"].reshape(NE * HC, P)], 0).T,
        "row": np.concatenate([row1(n) for n in (
            "L0_xattn_bq", "L0_xattn_bk", "L0_xattn_bv", "L0_xattn_bo", "L0_ffn_next_b",
            "L1_attn_bo", "L1_xattn_bk", "L1_xattn_bq", "L1_xattn_bv", "L1_xattn_bck",
            "L1_xattn_bcq", "L1_xattn_bcv", "L1_xattn_bp")], 1),
        "gate_bias": np.concatenate([row1("L1_attn_wi_b"), row1("L1_attn_wf_b")], 1),
        "b2m": g["L1_ffn_b2"],
        "w1a": w1(g["L0_ffn_w1"]),
        "w2a": w2(g["L0_ffn_w2"]),
        "w1b": np.ascontiguousarray(g["L1_ffn_w1"].transpose(2, 0, 1)),
        "w2b": w2(g["L1_ffn_w2"].transpose(0, 2, 1)),
    }
    nc = bacc.Bacc("TRN2", target_bir_lowering=False, num_devices=1)
    maps, d = {}, {}
    for name, a in arrays.items():
        maps[f"in_{name}"] = np.ascontiguousarray(a)
        d[name] = nc.dram_tensor(f"in_{name}", a.shape, mybir.dt.from_np(a.dtype), kind="ExternalInput").ap()
    out = nc.dram_tensor("out", (NB, T, P), F32, kind="ExternalOutput").ap()
    decoder(nc, d, out)
    r = run_bass_kernel_spmd(nc, [maps], core_ids=[0])
    return r.results[0]["out"]
```
